# Optimizing a Trainium2 kernel written in Bass

```python
import numpy as np
import jax
import jax.numpy as jnp

def _softmax(x, axis=-1):
    return jax.nn.softmax(x, axis=axis)

def _gelu(x):
    return jax.nn.gelu(x, approximate=True)

def _silu(x):
    return jax.nn.silu(x)

def _sigmoid(x):
    return jax.nn.sigmoid(x)

def _layernorm(x, axis=-1, eps=1e-05):
    m = jnp.mean(x, axis=axis, keepdims=True)
    v = jnp.var(x, axis=axis, keepdims=True)
    return (x - m) / jnp.sqrt(v + eps)

def _scatter_add(tgt, idx, src, axis=0):
    return tgt.at[idx].add(src)

def _segment_sum(src, seg, n):
    return jax.ops.segment_sum(src, seg, n)
kernel_name = 'mk_prb_d2_jaxref_r8_2aea45'

def setup_inputs(seed: int=0):
    np.random.seed(seed)
    _w = jnp.asarray

    def _L0_attn_setup():
        import jax, jax.numpy as jnp
        import numpy as np
        D_MODEL = 256
        NUM_HEADS = 16
        D_HEAD = D_MODEL // NUM_HEADS
        SCALE = 1.0 / np.sqrt(D_HEAD)
        key = jax.random.key(seed)
        ks = jax.random.split(key, 5)
        B, S = (4, 256)
        qkv = jax.random.normal(ks[0], (B, S, D_MODEL), dtype=jnp.float32)
        in_proj = jax.random.normal(ks[1], (3 * D_MODEL, D_MODEL), dtype=jnp.float32) * (1.0 / np.sqrt(D_MODEL))
        in_proj_bias = jnp.zeros((3 * D_MODEL,), dtype=jnp.float32)
        out_w = jax.random.normal(ks[2], (D_MODEL, D_MODEL), dtype=jnp.float32) * (1.0 / np.sqrt(D_MODEL))
        out_b = jnp.zeros((D_MODEL,), dtype=jnp.float32)
        alibi_slopes = (2.0 ** (-jnp.linspace(1.0, 8.0, NUM_HEADS))).astype(jnp.float32)
        return {'qkv': qkv, 'in_proj': in_proj, 'in_proj_bias': in_proj_bias, 'out_w': out_w, 'out_b': out_b, 'alibi_slopes': alibi_slopes}
    _L0_attn_in = _L0_attn_setup()

    def _L0_ffn_setup():
        import jax, jax.numpy as jnp
        import numpy as np
        GOLDEN_CENTER = 1.0 / np.e
        GOLDEN_LOWER = 0.5 - np.log(4.0 / 3.0)
        GOLDEN_UPPER = 0.5

        def _golden_weights(x, Wr, temperature):
            inh = jax.nn.sigmoid(x @ Wr / temperature)
            in_zone = (inh >= GOLDEN_LOWER) & (inh <= GOLDEN_UPPER)
            distance = jnp.abs(inh - GOLDEN_CENTER)
            weights = jnp.exp(-distance / 0.1) * in_zone.astype(x.dtype)
            wsum = jnp.sum(weights, axis=-1, keepdims=True)
            no_expert = wsum < 1e-08
            fb = jnp.exp(-distance / 0.3)
            _, top2 = jax.lax.top_k(fb, 2)
            fb_mask = jnp.sum(jax.nn.one_hot(top2, weights.shape[-1], dtype=x.dtype), axis=-2)
            fb_w = fb * fb_mask
            fb_w = fb_w / jnp.maximum(jnp.sum(fb_w, axis=-1, keepdims=True), 1e-08)
            weights = jnp.where(no_expert, fb_w, weights)
            weights = weights / jnp.maximum(jnp.sum(weights, axis=-1, keepdims=True), 1e-08)
            return weights
        key = jax.random.key(seed)
        ks = jax.random.split(key, 5)
        B, T, D, E, F = (2, 256, 256, 8, 256)
        s_in = 1.0 / np.sqrt(D)
        s_f = 1.0 / np.sqrt(F)
        return {'x': jax.random.normal(ks[0], (B, T, D), dtype=jnp.float32), 'Wg': jax.random.normal(ks[1], (E, D, F), dtype=jnp.float32) * s_in, 'Wu': jax.random.normal(ks[2], (E, D, F), dtype=jnp.float32) * s_in, 'Wd': jax.random.normal(ks[3], (E, F, D), dtype=jnp.float32) * s_f, 'Wr': jax.random.normal(ks[4], (D, E), dtype=jnp.float32) * s_in, 'temperature': jnp.ones((1,), dtype=jnp.float32)}
    _L0_ffn_in = _L0_ffn_setup()

    def _L1_attn_setup():
        import jax, jax.numpy as jnp
        import numpy as np
        D_MODEL = 256
        N_HEADS = 16
        HEAD_DIM = D_MODEL // N_HEADS
        B, T = (2, 256)
        key = jax.random.key(seed)
        ks = jax.random.split(key, 9)
        s = 0.02
        x = jax.random.normal(ks[0], (B, T, D_MODEL), dtype=jnp.float32)
        Wq = jax.random.normal(ks[1], (N_HEADS, D_MODEL, HEAD_DIM), dtype=jnp.float32) * s
        bq = jax.random.normal(ks[2], (N_HEADS, HEAD_DIM), dtype=jnp.float32) * s
        Wk = jax.random.normal(ks[3], (N_HEADS, D_MODEL, HEAD_DIM), dtype=jnp.float32) * s
        bk = jax.random.normal(ks[4], (N_HEADS, HEAD_DIM), dtype=jnp.float32) * s
        Wv = jax.random.normal(ks[5], (N_HEADS, D_MODEL, HEAD_DIM), dtype=jnp.float32) * s
        bv = jax.random.normal(ks[6], (N_HEADS, HEAD_DIM), dtype=jnp.float32) * s
        Wo = jax.random.normal(ks[7], (D_MODEL, D_MODEL), dtype=jnp.float32) * s
        bo = jax.random.normal(ks[8], (D_MODEL,), dtype=jnp.float32) * s
        return {'x': x, 'Wq': Wq, 'bq': bq, 'Wk': Wk, 'bk': bk, 'Wv': Wv, 'bv': bv, 'Wo': Wo, 'bo': bo}
    _L1_attn_in = _L1_attn_setup()

    def _L1_ffn_setup():
        import jax, jax.numpy as jnp
        import numpy as np
        THRESHOLD = 0.05
        ACT_BITS = 4
        QMAX = 2 ** (ACT_BITS - 1) - 1
        EPS = 1e-08

        def ternarize(W, threshold):
            absW = jnp.abs(W)
            delta = threshold * jnp.max(absW)
            mask = absW > delta
            n = jnp.maximum(jnp.sum(mask), 1)
            alpha = jnp.sum(jnp.where(mask, absW, 0.0)) / n
            Wt = alpha * jnp.sign(W) * mask
            return W + jax.lax.stop_gradient(Wt - W)

        def ternary_linear(x, W, b, threshold=THRESHOLD):
            Wq = ternarize(W, threshold)
            return jnp.einsum('bsd,hd->bsh', x, Wq) + b

        def fp4_activation(x):
            scale = jnp.max(jnp.abs(x)) / QMAX + EPS
            q = jnp.clip(jnp.round(x / scale), -QMAX, QMAX) * scale
            return x + jax.lax.stop_gradient(q - x)
        key = jax.random.key(seed)
        k1, k2, k3, k4, k5 = jax.random.split(key, 5)
        B, S, D, H = (2, 512, 256, 1024)
        x = jax.random.normal(k1, (B, S, D), dtype=jnp.float32)
        W1 = jax.random.normal(k2, (H, D), dtype=jnp.float32) * (1.0 / np.sqrt(D))
        b1 = jax.random.normal(k3, (H,), dtype=jnp.float32) * 0.02
        W2 = jax.random.normal(k4, (D, H), dtype=jnp.float32) * (1.0 / np.sqrt(H))
        b2 = jax.random.normal(k5, (D,), dtype=jnp.float32) * 0.02
        return {'x': x, 'W1': W1, 'b1': b1, 'W2': W2, 'b2': b2}
    _L1_ffn_in = _L1_ffn_setup()
    _d = {'L0_attn_qkv': _L0_attn_in['qkv'], 'L0_attn_in_proj': _L0_attn_in['in_proj'], 'L0_attn_in_proj_bias': _L0_attn_in['in_proj_bias'], 'L0_attn_out_w': _L0_attn_in['out_w'], 'L0_attn_out_b': _L0_attn_in['out_b'], 'L0_attn_alibi_slopes': _L0_attn_in['alibi_slopes'], 'L0_ffn_Wg': _L0_ffn_in['Wg'], 'L0_ffn_Wu': _L0_ffn_in['Wu'], 'L0_ffn_Wd': _L0_ffn_in['Wd'], 'L0_ffn_Wr': _L0_ffn_in['Wr'], 'L0_ffn_temperature': _L0_ffn_in['temperature'], 'L1_attn_Wq': _L1_attn_in['Wq'], 'L1_attn_bq': _L1_attn_in['bq'], 'L1_attn_Wk': _L1_attn_in['Wk'], 'L1_attn_bk': _L1_attn_in['bk'], 'L1_attn_Wv': _L1_attn_in['Wv'], 'L1_attn_bv': _L1_attn_in['bv'], 'L1_attn_Wo': _L1_attn_in['Wo'], 'L1_attn_bo': _L1_attn_in['bo'], 'L1_ffn_W1': _L1_ffn_in['W1'], 'L1_ffn_b1': _L1_ffn_in['b1'], 'L1_ffn_W2': _L1_ffn_in['W2'], 'L1_ffn_b2': _L1_ffn_in['b2']}
    _x0 = _d['L0_attn_qkv']
    _d['L0_attn_qkv'] = jax.random.normal(jax.random.fold_in(jax.random.key(seed), 1), (8, 256, 256), dtype=_x0.dtype)
    del _x0
    return _d

def reference(L0_attn_qkv, L0_attn_in_proj, L0_attn_in_proj_bias, L0_attn_out_w, L0_attn_out_b, L0_attn_alibi_slopes, L0_ffn_Wg, L0_ffn_Wu, L0_ffn_Wd, L0_ffn_Wr, L0_ffn_temperature, L1_attn_Wq, L1_attn_bq, L1_attn_Wk, L1_attn_bk, L1_attn_Wv, L1_attn_bv, L1_attn_Wo, L1_attn_bo, L1_ffn_W1, L1_ffn_b1, L1_ffn_W2, L1_ffn_b2):

    def _L0_attn_ref(qkv, in_proj, in_proj_bias, out_w, out_b, alibi_slopes):
        import jax, jax.numpy as jnp
        import numpy as np
        D_MODEL = 256
        NUM_HEADS = 16
        D_HEAD = D_MODEL // NUM_HEADS
        SCALE = 1.0 / np.sqrt(D_HEAD)
        B, S, D = qkv.shape
        H, Dh = (NUM_HEADS, D_HEAD)
        proj = qkv @ in_proj.T + in_proj_bias
        q, k, v = jnp.split(proj, 3, axis=-1)
        q = q.reshape(B, S, H, Dh).transpose(0, 2, 1, 3)
        k = k.reshape(B, S, H, Dh).transpose(0, 2, 1, 3)
        v = v.reshape(B, S, H, Dh).transpose(0, 2, 1, 3)
        scores = jnp.einsum('bhqd,bhkd->bhqk', q, k) * SCALE
        pos = jnp.arange(S)
        rel = (pos[None, :] - pos[:, None]).astype(scores.dtype)
        scores = scores + rel[None, None] * alibi_slopes[None, :, None, None]
        causal_mask = pos[None, :] > pos[:, None]
        scores = jnp.where(causal_mask[None, None], -jnp.inf, scores)
        attn = jnp.maximum(jax.nn.softmax(scores, axis=-1), 1e-10)
        attended = jnp.einsum('bhqk,bhkd->bhqd', attn, v)
        attended = attended.transpose(0, 2, 1, 3).reshape(B, S, D)
        return attended @ out_w.T + out_b

    def _L0_ffn_ref(x, Wg, Wu, Wd, Wr, temperature):
        import jax, jax.numpy as jnp
        import numpy as np
        GOLDEN_CENTER = 1.0 / np.e
        GOLDEN_LOWER = 0.5 - np.log(4.0 / 3.0)
        GOLDEN_UPPER = 0.5

        def _golden_weights(x, Wr, temperature):
            inh = jax.nn.sigmoid(x @ Wr / temperature)
            in_zone = (inh >= GOLDEN_LOWER) & (inh <= GOLDEN_UPPER)
            distance = jnp.abs(inh - GOLDEN_CENTER)
            weights = jnp.exp(-distance / 0.1) * in_zone.astype(x.dtype)
            wsum = jnp.sum(weights, axis=-1, keepdims=True)
            no_expert = wsum < 1e-08
            fb = jnp.exp(-distance / 0.3)
            _, top2 = jax.lax.top_k(fb, 2)
            fb_mask = jnp.sum(jax.nn.one_hot(top2, weights.shape[-1], dtype=x.dtype), axis=-2)
            fb_w = fb * fb_mask
            fb_w = fb_w / jnp.maximum(jnp.sum(fb_w, axis=-1, keepdims=True), 1e-08)
            weights = jnp.where(no_expert, fb_w, weights)
            weights = weights / jnp.maximum(jnp.sum(weights, axis=-1, keepdims=True), 1e-08)
            return weights
        weights = _golden_weights(x, Wr, temperature)
        gate = jnp.einsum('btd,edf->betf', x, Wg)
        up = jnp.einsum('btd,edf->betf', x, Wu)
        h = jax.nn.silu(gate) * up
        e_out = jnp.einsum('betf,efd->betd', h, Wd)
        out = jnp.einsum('bte,betd->btd', weights, e_out)
        return out

    def _L1_attn_ref(x, Wq, bq, Wk, bk, Wv, bv, Wo, bo):
        import jax, jax.numpy as jnp
        import numpy as np
        D_MODEL = 256
        N_HEADS = 16
        HEAD_DIM = D_MODEL // N_HEADS
        B, T = (2, 256)
        Bn, Tn, C = x.shape
        H, _, D = Wq.shape
        scale = D ** (-0.5)
        q = jnp.einsum('btc,hcd->bhtd', x, Wq) + bq[None, :, None, :]
        k = jnp.einsum('btc,hcd->bhtd', x, Wk) + bk[None, :, None, :]
        v = jnp.einsum('btc,hcd->bhtd', x, Wv) + bv[None, :, None, :]
        scores = jnp.einsum('bhtd,bhsd->bhts', q, k) * scale
        neg = jnp.finfo(scores.dtype).min
        causal = jnp.triu(jnp.full((Tn, Tn), neg, dtype=scores.dtype), k=1)
        probs = jax.nn.softmax(scores + causal, axis=-1)
        y = jnp.einsum('bhts,bhsd->bhtd', probs, v)
        y = y.transpose(0, 2, 1, 3).reshape(Bn, Tn, H * D)
        return y @ Wo + bo

    def _L1_ffn_ref(x, W1, b1, W2, b2):
        import jax, jax.numpy as jnp
        import numpy as np
        THRESHOLD = 0.05
        ACT_BITS = 4
        QMAX = 2 ** (ACT_BITS - 1) - 1
        EPS = 1e-08

        def ternarize(W, threshold):
            absW = jnp.abs(W)
            delta = threshold * jnp.max(absW)
            mask = absW > delta
            n = jnp.maximum(jnp.sum(mask), 1)
            alpha = jnp.sum(jnp.where(mask, absW, 0.0)) / n
            Wt = alpha * jnp.sign(W) * mask
            return W + jax.lax.stop_gradient(Wt - W)

        def ternary_linear(x, W, b, threshold=THRESHOLD):
            Wq = ternarize(W, threshold)
            return jnp.einsum('bsd,hd->bsh', x, Wq) + b

        def fp4_activation(x):
            scale = jnp.max(jnp.abs(x)) / QMAX + EPS
            q = jnp.clip(jnp.round(x / scale), -QMAX, QMAX) * scale
            return x + jax.lax.stop_gradient(q - x)
        h = ternary_linear(x, W1, b1)
        h = jax.nn.gelu(h, approximate=False)
        y = ternary_linear(h, W2, b2)
        return fp4_activation(y)
    x = L0_attn_qkv
    xn = _layernorm(x, axis=-1)
    x = x + _L0_attn_ref(xn, L0_attn_in_proj, L0_attn_in_proj_bias, L0_attn_out_w, L0_attn_out_b, L0_attn_alibi_slopes) + _L0_ffn_ref(xn, L0_ffn_Wg, L0_ffn_Wu, L0_ffn_Wd, L0_ffn_Wr, L0_ffn_temperature)
    xn = _layernorm(x, axis=-1)
    x = x + _L1_attn_ref(xn, L1_attn_Wq, L1_attn_bq, L1_attn_Wk, L1_attn_bk, L1_attn_Wv, L1_attn_bv, L1_attn_Wo, L1_attn_bo) + _L1_ffn_ref(xn, L1_ffn_W1, L1_ffn_b1, L1_ffn_W2, L1_ffn_b2)
    return x

_drawn_inputs = setup_inputs


def setup_inputs(seed=0):
    import zlib

    import numpy as np

    out = dict(_drawn_inputs(seed))
    spreads = {'L0_attn_in_proj_bias': (0.0, 0.1), 'L0_attn_out_b': (0.0, 0.1)}
    factors = {'L1_attn_Wq': 8.0,
     'L1_attn_bq': 8.0,
     'L1_attn_Wk': 8.0,
     'L1_attn_bk': 8.0,
     'L1_attn_Wv': 3.0,
     'L1_attn_bv': 8.0,
     'L1_attn_Wo': 2.885,
     'L1_attn_bo': 3.712}
    for name, (base, spread) in spreads.items():
        noise = np.random.default_rng([zlib.crc32(name.encode()), seed]).standard_normal(out[name].shape)
        drawn = base * np.exp(spread * noise) if base else spread * noise
        out[name] = jnp.asarray(drawn.astype(out[name].dtype))
    for name, factor in factors.items():
        out[name] = (out[name] * factor).astype(out[name].dtype)
    return out
```

```python
from contextlib import ExitStack

import numpy as np
import concourse.bass as bass
from concourse import mybir

F32 = mybir.dt.float32
F16 = mybir.dt.float16
BF16 = mybir.dt.bfloat16
I32 = mybir.dt.int32
ALU = mybir.AluOpType
ACT = mybir.ActivationFunctionType
AX = mybir.AxisListType
R_MAX = bass.bass_isa.ReduceOp.max
R_ADD = bass.bass_isa.ReduceOp.add

P = 128
B, S, D = 8, 256, 256
H, C = 16, 16
NT = S // P
NK = D // P
E, F = 8, 256
NF = F // P
HID = 1024
NH = HID // P
PAD = 32
G4 = P // PAD
SPLITS = 6
KR = SPLITS * C
EPS = 1e-5
CLAMP = 1e-10
MASKED = -1e30
BIG = 3e38
WSCALE = 16.0
GOLD_C = 1.0 / np.e
GOLD_LO = 0.5 - np.log(4.0 / 3.0)
GOLD_HI = 0.5
QMAX = 7.0
ROUND = 1.5 * 2.0 ** 23

BANKED = {"tr0", "q0", "k0", "v0", "gate", "up", "down", "op0",
          "tr1", "w1", "q1", "k1", "v1", "w2", "op1"}
RING = 3


def with_heads(order, last):
    out = []
    for item in order:
        if isinstance(item, int):
            out.append(("score", item, 0))
            first = order[[isinstance(x, int) for x in order].index(True)]
            if item - 1 >= first:
                out.append(("norm", item - 1, 0))
            if item - 2 >= first:
                out.append(("turn", item - 2, 0))
                if (item - 2) % G4 == G4 - 1:
                    out.append(("value", (item - 2) // G4, 0))
        elif item == "flush_a":
            out += [("norm", last, 0), ("turn", last - 1, 0)]
        elif item == "flush_b":
            out += [("turn", last, 0), ("value", last // G4, 0)]
        else:
            out.append(item)
    return out


def front(d):
    return {n: (n, 0, d) for n in ("ln0a", "ln0b", "tr0", "q0", "k0", "r0", "m0", "l0", "xe")} | \
           {"v0a": ("v0", 0, d), "v0b": ("v0", 1, d)}


def main_stage(name, arg=0):
    return (name, arg, 0)


def block1(name, arg=0):
    return (name, arg, -1)


def first_pass():
    f, g = front(0), front(1)
    gate, up, down = ([main_stage(n, e) for e in range(E)] for n in ("gate", "up", "down"))
    sp = [("split", i, 0) for i in range(2 + E)]
    order = [("setup", 0, 0), f["ln0a"], ("setup", 2, 0), sp[0], f["ln0b"], f["tr0"], sp[1], f["q0"], f["k0"], f["xe"], f["r0"], f["v0a"], f["m0"],
             f["v0b"], f["l0"], ("setup", 1, 0), main_stage("rt1"), sp[2], gate[0], up[0], main_stage("rt2"), sp[3], gate[1], up[1],
             16, down[0], 17, sp[4], gate[2], 18, up[2], 19, down[1], 20, sp[5], gate[3], 21, up[3], 22, down[2], 23,
             sp[6], gate[4], 24, up[4], 25, down[3], 26, ("tern", 0, 0), sp[7], gate[5], 27, up[5], 28, down[4], 29,
             sp[8], gate[6], 30, up[6], g["ln0a"], 31, down[5], sp[9], ("tern", 1, 0), gate[7], "flush_a", g["ln0b"], up[7], "flush_b", g["tr0"],
             down[6], g["q0"], g["k0"], g["r0"], g["v0a"], g["m0"], g["v0b"], g["l0"], g["xe"], down[7],
             main_stage("op0")]
    return with_heads(order, 31)


def steady_pass(with_front):
    g = front(1)
    gate, up, down = ([main_stage(n, e) for e in range(E)] for n in ("gate", "up", "down"))
    w1 = [block1("w1", a) for a in range(NH // 2)]
    order = [block1("ln1a"), main_stage("rt1"), 0, gate[0], block1("ln1b"), 1, up[0], main_stage("rt2"), 2, block1("tr1"),
             3, gate[1], block1("q1"), block1("k1"), 4, up[1], block1("r1"), 5, down[0], block1("m1"), block1("v1"),
             6, block1("l1"), 7, *w1, gate[2], up[2], down[1], 8, 9, gate[3], 10, 11, up[3], 12, 13, down[2], 14, 15,
             gate[4], 16, up[4], 17, down[3], block1("w2", 0), 18, block1("w2", 1), 19, gate[5], main_stage("op0"), 20, up[5], 21, down[4],
             g["ln0a"], 22, g["ln0b"], 23, gate[6], g["tr0"], 24, up[6], g["q0"], g["k0"], 25, down[5], g["r0"], g["v0a"], 26,
             g["m0"], g["v0b"], 27, gate[7], g["l0"], 28, up[7], g["xe"], 29, down[6], 30, 31, "flush_a", down[7], "flush_b",
             block1("op1", 0), block1("op1", 1)]
    if not with_front:
        gone = set(g.values())
        order = [x for x in order if not (isinstance(x, tuple) and x in gone)]
    return with_heads(order, 31)


def final_pass():
    w1 = [block1("w1", a) for a in range(NH // 2)]
    order = [block1("ln1a"), block1("ln1b"), block1("tr1"), block1("q1"), block1("k1"), block1("r1"), block1("v1"), block1("m1"), block1("l1"),
             *w1, 0, block1("w2", 0), 1, block1("w2", 1), *range(2, 16), "flush_a", "flush_b", block1("op1", 0), block1("op1", 1)]
    return with_heads(order, 15)


def uses(order):
    return sum(s[0] in BANKED for s in order)


ORDERS = {"first": first_pass(), "steady": steady_pass(True), "last": steady_pass(False), "final": final_pass()}
USES_STEADY = uses(ORDERS["steady"])
assert USES_STEADY % RING == 0
ROUNDS = USES_STEADY // RING
STEADY = B - 2
USES_BEFORE = {"first": 0, "steady": uses(ORDERS["first"]), "last": uses(ORDERS["first"]) + USES_STEADY * STEADY}
USES_BEFORE["final"] = USES_BEFORE["last"] + uses(ORDERS["last"])
PASS_OF = {"first": 0, "steady": 1, "last": B - 1, "final": B}
ACC_STEPS = E + 1


class Index:

    def __init__(self, reg, off):
        self.reg, self.off = reg, off

    def plus(self, d):
        return Index(self.reg, self.off + d)

    def at(self, per, extra=0):
        v = self.off * per + extra
        return v if self.reg is None else self.reg * per + v


class Stage:

    def __init__(self, kind, step, it):
        self.name, self.arg, d = step
        self.kind, self.it, self.n = kind, it, it.plus(d)
        self.bank = self.filled = self.before = self.place = None


def stages(kind, it):
    out, users, place = [], [None] * RING, 0
    use = USES_BEFORE[kind]
    for step in ORDERS[kind]:
        st = Stage(kind, step, it)
        if st.name in BANKED:
            st.bank = use % RING
            st.filled = it.at(ROUNDS, use // RING + 1 - ROUNDS * PASS_OF[kind])
            st.before, users[st.bank] = users[st.bank], st
            use += 1
        if st.name in ("down", "op0"):
            st.place = place
            place += 1
        out.append(st)
    return out


def head_block(st):
    return {"first": 0, "final": 1}.get(st.kind, st.arg // H)


def group_block(st):
    return {"first": 0, "final": 1}.get(st.kind, st.arg // (H // G4))


def batch_of(st, block):
    return st.it if block == 0 else st.it.plus(-1)


def heads_before(st, extra=0):
    return st.it.at(2 * H, st.arg - H + extra)


def groups_before(st, extra=0):
    return st.it.at(2 * H // G4, st.arg - H // G4 + extra)


def groups_of_block(st, block):
    end = 2 * H // G4 if (block == 1) != (st.kind in ("first", "final")) else H // G4
    return st.it.at(2 * H // G4, end - H // G4)


def ahead(n):
    return n.plus(1)


def wait(eng, sem, value):
    if not (isinstance(value, int) and value <= 0):
        eng.wait_ge(sem, value)


def settle(eng, passed):
    eng.sem_inc(passed, 1)


def run_passes(eng, do, before_block1):
    for st in stages("first", Index(None, 0)):
        do(st)
    before_block1()
    with eng.Fori(0, STEADY) as j:
        for st in stages("steady", Index(j, 1)):
            do(st)
    for st in stages("last", Index(None, B - 1)):
        do(st)
    for st in stages("final", Index(None, B)):
        do(st)


def two_blocks(nc, x, wqk0, bqk0, wv0, vb0, wo0, ob0, slopes, wg, wu, wd, temp,
               wqk1, bqk1, wv1, vb1, wo1, ob1, w1t, b1c, w2t, b2, out):
    with ExitStack() as ctx:
        def sb(name, shape, dt=F32):
            return ctx.enter_context(nc.sbuf_tensor(name, shape, dt))

        def sem(name):
            return ctx.enter_context(nc.semaphore(name))

        score_ps = [ctx.enter_context(nc.psum_tensor(f"score_ps{i}", [P, 512], F32)) for i in range(2)]
        turn_ps = [ctx.enter_context(nc.psum_tensor(f"turn_ps{i}", [P, 512], F32)) for i in range(2)]
        value_ps = ctx.enter_context(nc.psum_tensor("value_ps", [P, 512], F32))
        gen_ps = [ctx.enter_context(nc.psum_tensor(f"gen_ps{i}", [P, 512], F32)) for i in range(RING)]

        gu_hi = sb("gu_hi", [P, E, 2, NK, F], F16)
        gu_lo = sb("gu_lo", [P, E, 2, NK, F], F16)
        wd_sb = sb("wd_sb", [P, E, NF, D])
        qk_hi = [sb(f"qk_hi{l}", [P, NK, 2 * D], F16) for l in range(2)]
        qk_lo = [sb(f"qk_lo{l}", [P, NK, 2 * D], F16) for l in range(2)]
        wv_sb = [sb("wv0_sb", [P, NK, D + E]), sb("wv1_sb", [P, NK, D])]
        wo_sb = [sb(f"wo{l}_sb", [P, G4, D]) for l in range(2)]
        t1_sb = sb("t1_sb", [P, NK, HID], F16)
        t2_sb = sb("t2_sb", [P, NH, D])
        bqk = [sb(f"bqk{l}", [P, 4]) for l in range(2)]
        vb = [sb(f"vb{l}_sb", [P, D]) for l in range(2)]
        ob = [sb(f"ob{l}_sb", [P, D]) for l in range(2)]
        b2_sb = sb("b2_sb", [P, D])
        b1_sb = sb("b1_sb", [P, NH])
        slope_sb = sb("slope_sb", [P, H])
        half_t = sb("half_t", [P, 1])
        minus_half = sb("minus_half", [P, NT])
        before = sb("before", [P, E, E])
        ident = sb("ident", [P, P])
        bias0 = sb("bias0", [P, H, S])
        bias1 = sb("bias1", [P, S])
        x0 = sb("x0", [P, NT, D])
        acc = sb("acc", [P, NT, D])
        xb = [sb(f"xb{l}", [P, NT, D]) for l in range(2)]
        stats = sb("stats", [P, NT, 6])
        mv = [sb(f"mv{l}", [P, NT, 2]) for l in range(2)]
        var = [sb(f"var{l}", [P, NT]) for l in range(2)]
        rstd = [sb(f"rstd{l}", [P, NT]) for l in range(2)]
        xt = [sb(f"xt{l}", [P, NK, S]) for l in range(2)]
        xt_hi = [sb(f"xt_hi{l}", [P, NK, S], F16) for l in range(2)]
        xt_lo = [sb(f"xt_lo{l}", [P, NK, S], F16) for l in range(2)]
        xe_hi = sb("xe_hi", [P, NK, S], F16)
        xe_lo = sb("xe_lo", [P, NK, S], F16)
        rest = sb("rest", [P, 2, 2, S])
        parts = sb("parts", [P, 2, 3, 2, S], BF16)
        q_stack = [sb(f"q_stack{i}", [KR, H // 2, S], BF16) for i in range(2)]
        k_stack = [sb(f"k_stack{i}", [KR, H // 2, S], BF16) for i in range(2)]
        v_sb = [sb(f"v{l}_sb", [P, NT, H, PAD]) for l in range(2)]
        probs = sb("probs", [P, 4, 3 * P])
        nmax = sb("nmax", [P, 4, 2])
        esum = sb("esum", [P, 4, 2])
        rsum = sb("rsum", [P, 4, 2])
        pt = sb("pt", [P, 8, 4 * P])
        at = [sb(f"at{l}", [P, G4, S]) for l in range(2)]
        tanh_sb = sb("tanh_sb", [P, NF * S])
        gated = sb("gated", [P, NF * S])
        hid0 = sb("hid0", [P, 2, NF, S])
        hid1 = sb("hid1", [P, NH, S])
        y_sb = sb("y_sb", [P, NT, D])
        x2_sb = sb("x2_sb", [P, NT, D])
        r_tanh = sb("r_tanh", [P, NT, E])
        r_in = sb("r_in", [P, NT, E])
        r_zone = sb("r_zone", [P, NT, E])
        r_zone2 = sb("r_zone2", [P, NT, E])
        r_d = sb("r_d", [P, NT, E])
        r_dist = sb("r_dist", [P, NT, E])
        r_e1 = sb("r_e1", [P, NT, E])
        r_e2 = sb("r_e2", [P, NT, E])
        r_w = sb("r_w", [P, NT, E])
        r_fb = sb("r_fb", [P, NT, E])
        r_rank = sb("r_rank", [P, NT, E])
        r_gt = sb("r_gt", [P, NT, E, E])
        r_eq = sb("r_eq", [P, NT, E, E])
        r_s = sb("r_s", [P, 6, NT, 1])
        w8 = sb("w8", [P, NT, E])
        t_max = sb("t_max", [P, 2])
        t_amax = sb("t_amax", [P, 2])
        t_delta = sb("t_delta", [P, 2, 2])
        t_sum = sb("t_sum", [P, 2, 2])
        t_tot = sb("t_tot", [P, 2, 2])
        alpha = sb("alpha", [P, 2])
        ymax = sb("ymax", [P, B * NT])
        yred = sb("yred", [P, 4])

        raw = [v_sb[1][:].rearrange("p t h c -> p (t h c)"), at[1][:].rearrange("p g s -> p (g s)")]
        w1_raw = t2_sb[:].rearrange("p a d -> p (a d)")
        w2_raw = hid1[:].rearrange("p a s -> p (a s)")
        y_all = gu_hi[:].rearrange("p e m k f -> p (e m k f)").bitcast(F32).rearrange("p (t d) -> p t d", d=D)
        x_all = gu_lo[:].rearrange("p e m k f -> p (e m k f)").bitcast(F32).rearrange("p (t d) -> p t d", d=D)
        rel_i = hid0[:, 0, 0, :].bitcast(I32)
        rel = hid0[:, 1, 0, :]

        scr = [[nc.dram_tensor(f"scr_{n}{l}", (SPLITS, C * H, S), BF16).ap() for n in "qk"] for l in range(2)]
        y_dram = nc.dram_tensor("y_dram", (B * NT, P, D), F32).ap()
        x2_dram = nc.dram_tensor("x2_dram", (B * NT, P, D), F32).ap()
        x_tiles = x.rearrange("b (t p) d -> p (b t) d", p=P)
        out_tiles = out.rearrange("b (t p) d -> p (b t) d", p=P)
        y_tiles = y_dram.rearrange("t p d -> p t d")
        x2_tiles = x2_dram.rearrange("t p d -> p t d")

        s_x = sem("s_x")
        s_c = sem("s_c")
        s_wv0 = sem("s_wv0")
        s_wd = sem("s_wd")
        s_wo = sem("s_wo")
        s_w1 = sem("s_w1")
        s_raw = [sem(f"s_raw{i}") for i in range(2)]
        s_scr = [sem(f"s_scr{l}") for l in range(2)]
        s_stack = [sem(f"s_stack{i}") for i in range(2)]
        s_yw = sem("s_yw")
        s_x2w = sem("s_x2w")
        s_fin = sem("s_fin")
        s_out = sem("s_out")
        s_pool = sem("s_pool")
        s_set = sem("s_set")
        s_hi = sem("s_hi")
        s_lo = sem("s_lo")
        s_t = sem("s_t")
        s_tp = sem("s_tp")
        s_v1z = sem("s_v1z")
        s_dve = sem("s_dve")
        s_gps = sem("s_gps")
        s_sp = sem("s_sp")
        full = [sem(f"full{i}") for i in range(RING)]
        s_st = [sem(f"s_st{l}") for l in range(2)]
        s_rstd = [sem(f"s_rstd{l}") for l in range(2)]
        s_xb = [sem(f"s_xb{l}") for l in range(2)]
        s_xn = [sem(f"s_xn{l}") for l in range(2)]
        s_xh = [sem(f"s_xh{l}") for l in range(2)]
        s_xl = [sem(f"s_xl{l}") for l in range(2)]
        s_ph = [sem(f"s_ph{l}") for l in range(2)]
        s_pr = [sem(f"s_pr{l}") for l in range(2)]
        s_pm = [sem(f"s_pm{l}") for l in range(2)]
        s_pl = [sem(f"s_pl{l}") for l in range(2)]
        s_v = [sem(f"s_v{l}") for l in range(2)]
        s_th = sem("s_th")
        s_rt = sem("s_rt")
        s_re = sem("s_re")
        s_w8 = sem("s_w8")
        s_xe = sem("s_xe")
        s_tg = sem("s_tg")
        s_ga = sem("s_ga")
        s_h0 = sem("s_h0")
        s_acc = sem("s_acc")
        s_h1 = sem("s_h1")
        s_y = sem("s_y")
        s_ym = sem("s_ym")
        s_x2 = sem("s_x2")
        s_sc = sem("s_sc")
        s_mx = sem("s_mx")
        s_ex = sem("s_ex")
        s_rz = sem("s_rz")
        s_nm = sem("s_nm")
        s_tn = sem("s_tn")
        s_ev = sem("s_ev")
        s_pv = sem("s_pv")
        s_at = sem("s_at")
        s_q = sem("s_q")
        s_qp = sem("s_qp")
        s_qa = sem("s_qa")
        s_qo = sem("s_qo")

        RT = 25
        TERN = 10
        NC = 11
        POOL_IDENT, POOL_BEFORE, POOL_BIAS1, POOL_REL, POOL_WO, POOL_MH, POOL_PT = 2, 4, 6, 7, 9, 10, 11
        SET_V0, SET_HALF, SET_BQ, SET_REL, SET_BIAS0 = 1, 3, 5, 6, 6 + H

        def read_by(st):
            n, a, l = st.n, st.arg, int(st.name[-1]) if st.name[-1] in "01" else None
            return {
                "tr": lambda: (s_xl[l], n.at(1, 1)),
                "q": lambda: (s_ph[l], n.at(8, 4)),
                "k": lambda: (s_ph[l], n.at(8, 8)),
                "v": lambda: (s_v[0], n.at(NT, a + 1)) if l == 0 else (s_v[1], ahead(n).at(NT, NT)),
                "gate": lambda: (s_ga, n.at(E, a + 1)),
                "up": lambda: (s_h0, n.at(E, a + 1)),
                "down": lambda: (s_acc, n.at(NT * ACC_STEPS, NT * st.place + NT)),
                "w1": lambda: (s_h1, n.at(NH, 2 * a + 2)),
                "w2": lambda: (s_y, ahead(n).at(NT, a + 1)),
                "op": lambda: (s_x2, ahead(n).at(NT, a + 1)) if l else (s_acc, n.at(NT * ACC_STEPS, NT * st.place + NT)),
            }[st.name if st.name in ("w1", "w2") else st.name.rstrip("01")]()

        block = ctx.enter_context(nc.Block())

        @block.sync
        def _(sp):
            def load_x(n):
                wait(sp, s_xl[0], n.at(1))
                if n.reg is not None:
                    settle(sp, s_sp)
                sp.dma_start(x0[:], x_tiles[:, bass.ds(n.at(NT), NT), :]).then_inc(s_x, 16)

            def load_raw(i):
                if i >= 2:
                    wait(sp, s_lo, i - 1)
                dst = raw[i % 2]
                if i in (0, E + 1):
                    sp.dma_start(dst.rearrange("p (k n) -> p k n", k=NK),
                                 (wqk0, wqk1)[i // E].rearrange("(k p) n -> p k n", p=P)).then_inc(s_raw[i % 2], 16)
                else:
                    d = dst.rearrange("p (m k f) -> p m k f", m=2, k=NK)
                    for m, w in enumerate((wg, wu)):
                        sp.dma_start(d[:, m], w[i - 1].rearrange("(k p) f -> p k f", p=P)).then_inc(s_raw[i % 2], 16)

            def store_parts(l, n):
                wait(sp, s_pl[l], n.at(1, 1))
                flat = parts[:].rearrange("p a s m n -> p a s (m n)")
                for a, (lo, hi) in enumerate(((0, 3), (3, 5), (5, 6))):
                    sp.dma_start(scr[l][0][lo:hi].rearrange("s (p m) n -> p s (m n)", p=P),
                                 flat[:, 0, 0:hi - lo]).then_inc(s_scr[l], 16)
                    sp.dma_start(scr[l][1][lo:hi].rearrange("s (p m) n -> p s (m n)", p=P),
                                 flat[:, 1, a:a + 1].broadcast_to([P, hi - lo, 2 * S])).then_inc(s_scr[l], 16)

            def load_stack(l, n, it, u):
                wait(sp, s_scr[l], (n if l == 0 else ahead(n)).at(96, 96))
                if n.reg is not None:
                    settle(sp, s_sp)
                wait(sp, s_sc, it.at(2 * H, 8 * (u - 1) - H))
                half = slice(8 * (u % 2), 8 * (u % 2) + 8)
                for src, dst in zip(scr[l], (q_stack, k_stack)):
                    sp.dma_start(dst[u % 2][:], src.rearrange("s (c h) n -> (s c) h n", h=H)[:, half, :])\
                      .then_inc(s_stack[u % 2], 16)

            def do(st):
                n, name, it = st.n, st.name, st.it
                if name == "split" and st.arg < E:
                    load_raw(st.arg + 2)
                if name in ("l0", "l1"):
                    store_parts(int(name[1]), n)
                if name == "l1":
                    for u in (0, 1) if st.kind == "final" else (2, 3):
                        load_stack(1, n, it, u)
                if name == "l0":
                    for u in (2, 3) if st.kind == "first" and n.off == 0 else (0, 1):
                        load_stack(0, n, n, u)
                if name == "w2" and st.arg == NT - 1:
                    wait(sp, s_y, ahead(n).at(NT, NT))
                    if n.reg is not None:
                        settle(sp, s_sp)
                    sp.dma_start(y_tiles[:, bass.ds(n.at(NT), NT), :], y_sb[:]).then_inc(s_yw, 16)
                if name == "op1" and st.arg == NT - 1:
                    wait(sp, s_x2, ahead(n).at(NT, NT))
                    if n.reg is not None:
                        settle(sp, s_sp)
                    sp.dma_start(x2_tiles[:, bass.ds(n.at(NT), NT), :], x2_sb[:]).then_inc(s_x2w, 16)

            load_x(Index(None, 0))
            load_raw(0)
            load_raw(1)
            for st in stages("first", Index(None, 0)):
                if st.name == "ln0a" and st.n.off == 1:
                    load_x(st.n)
                do(st)
            for counts, batch in ((s_yw, 16), (s_x2w, 16), (s_scr[1], 96)):
                sp.sem_inc(counts, batch)
            with sp.Fori(0, STEADY) as j:
                it = Index(j, 1)
                load_x(it.plus(1))
                for st in stages("steady", it):
                    do(st)
            for st in stages("last", Index(None, B - 1)):
                do(st)
            sp.wait_ge(s_acc, NT * ACC_STEPS * B)
            sp.wait_ge(s_yw, 16 * B)
            sp.wait_ge(s_x2w, 16 * B)
            done = NT * (B - 1)
            for st in stages("final", Index(None, B)):
                do(st)
                if st.name == "l1":
                    sp.dma_start(y_all[:, 0:done, :], y_tiles[:, 0:done, :]).then_inc(s_fin, 16)
                    sp.dma_start(x_all[:, 0:done, :], x2_tiles[:, 0:done, :]).then_inc(s_fin, 16)
            for c in range(B):
                wait(sp, s_qo, c + 1)
                src = y_all[:, NT * c:NT * c + NT, :] if c < B - 1 else y_sb[:]
                sp.dma_start(out_tiles[:, NT * c:NT * c + NT, :], src).then_inc(s_out, 16)
            sp.wait_ge(s_out, 16 * B)
            sp.wait_ge(s_yw, 16 * (B + 1))
            sp.wait_ge(s_x2w, 16 * (B + 1))
            sp.wait_ge(s_scr[0], 96 * B)
            sp.wait_ge(s_scr[1], 96 * (B + 1))

        @block.gpsimd
        def _(pool):
            pool.memset(ident[:], 0.0).then_inc(s_pool, 1)
            pool.wait_ge(s_pool, 1)
            pool.affine_select(out=ident[:], in_=ident[:], compare_op=ALU.not_equal, fill=1.0, base=0,
                               pattern=[[-1, P]], channel_multiplier=1).then_inc(s_pool, 1)
            pool.memset(before[:], 1.0).then_inc(s_pool, 1)
            pool.wait_ge(s_pool, 3)
            pool.affine_select(out=before[:], in_=before[:], compare_op=ALU.is_gt, fill=0.0, base=0,
                               pattern=[[1, E], [-1, E]], channel_multiplier=0).then_inc(s_pool, 1)
            pool.memset(bias1[:], 0.0).then_inc(s_pool, 1)
            pool.wait_ge(s_pool, 5)
            pool.affine_select(out=bias1[:, P:S], in_=bias1[:, P:S], compare_op=ALU.is_ge, fill=MASKED, base=0,
                               pattern=[[-1, P]], channel_multiplier=1).then_inc(s_pool, 1)
            pool.iota(rel_i, pattern=[[1, S]], base=-P, channel_multiplier=-1).then_inc(s_pool, 1)
            for l in range(2):
                pool.memset(wo_sb[l][:], 0.0).then_inc(s_pool, 1)
            pool.memset(minus_half[:], -0.5).then_inc(s_pool, 1)
            pool.memset(pt[:, :, 0:P], CLAMP).then_inc(s_pool, 1)
            pool.wait_ge(s_pool, POOL_PT)
            for t in range(NF * 2):
                pool.dma_start(wd_sb[:, 2 * t:2 * t + 2], wd[2 * t:2 * t + 2].rearrange("e (k p) d -> p e k d", p=P))\
                    .then_inc(s_wd, 16)
            for l, w in enumerate((wo0, wo1)):
                for j in range(G4):
                    pool.dma_start(wo_sb[l][PAD * j:PAD * j + C, :, :],
                                   w.rearrange("(g j c) d -> j c g d", j=G4, c=C)[j]).then_inc(s_wo, 16)
            pool.dma_start(w1_raw.rearrange("p (k n) -> p k n", k=NK),
                           w1t.rearrange("(k p) n -> p k n", p=P)).then_inc(s_w1, 16)
            pool.dma_start(w2_raw.rearrange("p (a n) -> p a n", a=NH),
                           w2t.rearrange("(a p) n -> p a n", p=P)).then_inc(s_w1, 16)

            def do(st):
                n, name = st.n, st.name
                if name in ("ln0a", "ln1a"):
                    l = int(name[2])
                    src = (x0, acc)[l]
                    wait(pool, s_st[l], n.at(5, 5))
                    pool.tensor_tensor(rstd[l][:], var[l][:], minus_half[:], ALU.pow).then_inc(s_rstd[l], 1)
                    if st.kind == "first":
                        pool.wait_ge(s_c, 16 * NC)
                    if l == 0:
                        wait(pool, s_x, n.at(16, 16))
                        wait(pool, s_acc, n.at(NT * ACC_STEPS, NT - NT * ACC_STEPS))
                    else:
                        wait(pool, s_x2, ahead(n).at(NT))
                    for t in range(NT):
                        pool.tensor_tensor(xb[l][:, t], src[:, t], ob[l][:], ALU.add).then_inc(s_xb[l], 1)
                if name == "xe":
                    wait(pool, s_xl[0], n.at(1, 1))
                    wait(pool, s_acc, n.at(NT * ACC_STEPS, -NT))
                    if st.kind == "steady":
                        settle(pool, s_gps)
                    pool.tensor_copy(xe_hi[:].bitcast(I32), xt_hi[0][:].bitcast(I32)).then_inc(s_xe, 1)
                    pool.tensor_copy(xe_lo[:].bitcast(I32), xt_lo[0][:].bitcast(I32)).then_inc(s_xe, 1)
                if name == "tern":
                    i = st.arg
                    pool.wait_ge(s_t, TERN * i + 1)
                    pool.partition_all_reduce(t_amax[:, i:i + 1], t_max[:, i:i + 1], P, R_MAX).then_inc(s_tp, 1)
                    pool.wait_ge(s_t, TERN * i + 7)
                    pool.partition_all_reduce(t_tot[:, i], t_sum[:, i], P, R_ADD).then_inc(s_tp, 1)
                    if i == 1:
                        pool.wait_ge(s_lo, 2 + E)
                        pool.wait_ge(s_hi, 2 + E)
                        pool.memset(v_sb[1][:], 0.0).then_inc(s_v1z, 1)

            run_passes(pool, do, lambda: None)
            pool.wait_ge(s_q, 1)
            pool.partition_all_reduce(yred[:, 1:2], yred[:, 0:1], P, R_MAX).then_inc(s_qp, 1)

        @block.scalar
        def _(act):
            small = [(bqk[0][:], bqk0), (vb[0][:], vb0.partition_broadcast(P)), (half_t[:], temp.partition_broadcast(P)),
                     (slope_sb[:], slopes.partition_broadcast(P)), (ob[0][:], ob0.partition_broadcast(P)),
                     (bqk[1][:], bqk1), (vb[1][:], vb1.partition_broadcast(P)), (ob[1][:], ob1.partition_broadcast(P)),
                     (b1_sb[:], b1c), (b2_sb[:], b2.partition_broadcast(P)),
                     (wv_sb[1][:], wv1.rearrange("(k p) n -> p k n", p=P))]
            act.dma_start(wv_sb[0][:], wv0.rearrange("(k p) n -> p k n", p=P)).then_inc(s_wv0, 16)
            for dst, src in small:
                act.dma_start(dst, src).then_inc(s_c, 16)
            act.wait_ge(s_c, 16 * len(small))
            assert NC == len(small)

            def do(st):
                n, name, b = st.n, st.name, st.bank
                g = gen_ps[b] if b is not None else None
                if name == "split":
                    i = st.arg
                    act.wait_ge(s_raw[i % 2], 16 * sum(1 if a in (0, E + 1) else 2 for a in range(i % 2, i + 1, 2)))
                    hi = qk_hi[i // E][:].rearrange("p k n -> p (k n)") if i in (0, E + 1) else \
                        gu_hi[:, i - 1].rearrange("p m k f -> p (m k f)")
                    act.activation(hi, raw[i % 2], ACT.Copy, scale=WSCALE).then_inc(s_hi, 1)
                if name in ("tr0", "tr1"):
                    l = int(name[2])
                    wait(act, full[b], st.filled)
                    if l == 1:
                        wait(act, s_v[1], ahead(n).at(NT))
                    act.activation(xt[l][:].rearrange("p k s -> p (k s)"), g[:, :], ACT.Copy).then_inc(s_xh[l], 1)
                    if l == 0:
                        wait(act, s_xe, n.at(2))
                    act.activation(xt_hi[l][:].rearrange("p k s -> p (k s)"), g[:, :], ACT.Copy).then_inc(s_xh[l], 1)
                if name in ("q0", "k0", "q1", "k1"):
                    l, a = int(name[1]), "qk".index(name[0])
                    if n.reg is None and n.off == 0 and l == 0 and a == 0:
                        act.wait_ge(s_set, SET_BQ)
                    if a == 0:
                        if l == 0:
                            wait(act, s_scr[0], n.at(96))
                            wait(act, s_scr[1], n.at(96) if n.reg is not None or n.off > 1 else 0)
                        else:
                            wait(act, s_scr[1], ahead(n).at(96))
                            wait(act, s_scr[0], n.at(96, 192) if not (n.reg is None and n.off == B - 1) else 96 * B)
                    wait(act, full[b], st.filled)
                    scale = (float(C) ** -0.5 if a == 0 else 1.0) / WSCALE
                    for m in range(2):
                        bias = bqk[l][:, 2 * a + m:2 * a + m + 1]
                        act.activation(rest[:, a, m], g[:, S * m:S * m + S], ACT.Identity, bias=bias, scale=scale)\
                           .then_inc(s_ph[l], 1)
                        act.activation(parts[:, a, 0, m], g[:, S * m:S * m + S], ACT.Identity, bias=bias, scale=scale)\
                           .then_inc(s_ph[l], 1)
                if name in ("m0", "m1"):
                    l = int(name[1])
                    wait(act, s_pr[l], n.at(1, 1))
                    act.activation(parts[:, :, 1], rest[:], ACT.Copy).then_inc(s_pm[l], 1)
                if name == "v0":
                    t = st.arg
                    if t == 0 and n.reg is None and n.off == 0:
                        act.wait_ge(s_set, SET_HALF)
                    wait(act, full[b], st.filled)
                    if t == 0:
                        wait(act, s_rt, n.at(RT))
                    act.activation(r_tanh[:, t], g[:, D:D + E], ACT.Tanh, scale=half_t[:, 0:1]).then_inc(s_th, 1)
                if name == "rt2":
                    wait(act, s_rt, n.at(RT, 5))
                    act.activation(r_e1[:], r_dist[:], ACT.Exp, scale=-1.0 / 0.1).then_inc(s_re, 1)
                    act.activation(r_e2[:], r_dist[:], ACT.Exp, scale=-1.0 / 0.3).then_inc(s_re, 1)
                if name == "gate":
                    wait(act, full[b], st.filled)
                    if st.arg == 0:
                        wait(act, s_acc, n.at(NT * ACC_STEPS))
                    else:
                        wait(act, s_ga, n.at(E, st.arg))
                    act.activation(tanh_sb[:], g[:, :], ACT.Tanh, scale=0.5 / WSCALE).then_inc(s_tg, 1)
                if name == "w1":
                    if st.arg == 0:
                        wait(act, s_y, ahead(n).at(NT))
                    wait(act, full[b], st.filled)
                    for j in range(2):
                        a = 2 * st.arg + j
                        last = act.activation(hid1[:, a], g[:, S * j:S * j + S], ACT.Gelu,
                                              bias=b1_sb[:, a:a + 1], scale=alpha[:, 0:1])
                        last.then_inc(s_h1, 1)
                if name == "score":
                    s = st.arg
                    k = s % 4
                    wait(act, s_mx, heads_before(st, 1))
                    for lo, hi, j in ((0, S, 0), (S, S + P, 1)):
                        last = act.activation(probs[:, k, lo:hi], probs[:, k, lo:hi], ACT.Exp, scale=-1.0,
                                              bias=nmax[:, k, j:j + 1], accum_out=esum[:, k, j:j + 1])
                    last.then_inc(s_ex, 1)
                if name == "turn":
                    s = st.arg
                    wait(act, s_tn, heads_before(st, 1))
                    wait(act, s_pv, st.it.at(2 * H // G4, s // G4 - H // G4 - 1))
                    act.activation(pt[:, s % 8, P:4 * P], turn_ps[s % 2][:, 0:3 * P], ACT.Copy).then_inc(s_ev, 1)
                if name == "value":
                    l = group_block(st)
                    gg = st.arg % G4
                    wait(act, s_pv, groups_before(st, 1))
                    if gg == 0:
                        nb = batch_of(st, l)
                        wait(act, *((s_acc, nb.at(NT * ACC_STEPS)) if l == 0 else (s_x2, ahead(nb).at(NT))))
                    act.activation(at[l][:, gg], value_ps[:, 0:S], ACT.Copy).then_inc(s_at, 1)

            def before_block1():
                act.wait_ge(s_t, 2 * TERN)
                act.wait_ge(s_v1z, 1)

            run_passes(act, do, before_block1)
            act.wait_ge(s_q, 3)
            act.wait_ge(s_fin, 32)
            for c in range(B):
                src = y_all[:, NT * c:NT * c + NT, :] if c < B - 1 else y_sb[:]
                if c == B - 1:
                    act.wait_ge(s_yw, 16 * (B + 1))
                act.activation(src, src, ACT.Copy, scale=yred[:, 3:4]).then_inc(s_qa, 1)

        @block.tensor
        def _(pe):
            def take(st):
                if st.before is not None:
                    wait(pe, *read_by(st.before))
                elif st.kind != "first":
                    wait(pe, s_acc, st.it.at(NT * ACC_STEPS))
                    wait(pe, s_x2, ahead(batch_of(st, 1)).at(NT))
                return gen_ps[st.bank]

            def do(st):
                n, name = st.n, st.name
                first = n.reg is None and n.off == 0
                if name in ("tr0", "tr1"):
                    l = int(name[2])
                    src = (x0, acc)[l]
                    if first and l == 0:
                        pe.wait_ge(s_pool, POOL_IDENT)
                    wait(pe, s_xn[l], n.at(NT, NT))
                    g = take(st)
                    for t in range(NT):
                        for k in range(NK):
                            last = pe.transpose(g[:, S * k + P * t:S * k + P * t + P], src[:, t, P * k:P * k + P], ident[:])
                    last.then_inc(full[st.bank], 1)
                if name in ("q0", "k0", "q1", "k1"):
                    l, a = int(name[1]), "qk".index(name[0])
                    if first and l == 0 and a == 0:
                        pe.wait_ge(s_lo, 1)
                    wait(pe, s_xl[l], n.at(1, 1))
                    g = take(st)
                    for m in range(2):
                        cols = slice(D * a + P * m, D * a + P * m + P)
                        terms = [(w, xx, k) for w, xx in ((qk_hi, xt_hi), (qk_hi, xt_lo), (qk_lo, xt_hi)) for k in range(NK)]
                        for i, (w, xx, k) in enumerate(terms):
                            last = pe.matmul(g[:, S * m:S * m + S], w[l][:, k, cols], xx[l][:, k, :],
                                             start=(i == 0), stop=(i == len(terms) - 1))
                    last.then_inc(full[st.bank], 1)
                if name in ("v0", "v1"):
                    l = int(name[1])
                    if first and l == 0 and st.arg == 0:
                        pe.wait_ge(s_wv0, 16)
                    wait(pe, s_xl[l], n.at(1, 1))
                    g = take(st)
                    for t in ([st.arg] if l == 0 else range(NT)):
                        o = g[:, 0:D + E] if l == 0 else g[:, D * t:D * t + D]
                        for k in range(NK):
                            last = pe.matmul(o, xt[l][:, k, P * t:P * t + P], wv_sb[l][:, k, :],
                                             start=(k == 0), stop=(k == NK - 1))
                    last.then_inc(full[st.bank], 1)
                if name in ("gate", "up"):
                    m = ("gate", "up").index(name)
                    if st.arg == 0 and m == 0:
                        wait(pe, s_xe, n.at(2, 2))
                    if first and m == 0:
                        pe.wait_ge(s_lo, 2 + st.arg)
                    g = take(st)
                    for f in range(NF):
                        cols = slice(P * f, P * f + P)
                        terms = [(w, xx, k) for w, xx in ((gu_hi, xe_hi), (gu_hi, xe_lo), (gu_lo, xe_hi)) for k in range(NK)]
                        for i, (w, xx, k) in enumerate(terms):
                            last = pe.matmul(g[:, S * f:S * f + S], w[:, st.arg, m, k, cols], xx[:, k, :],
                                             start=(i == 0), stop=(i == len(terms) - 1))
                    last.then_inc(full[st.bank], 1)
                if name == "down":
                    if first and st.arg == 0:
                        pe.wait_ge(s_wd, 16 * 4)
                    wait(pe, s_h0, n.at(E, st.arg + 1))
                    g = take(st)
                    for t in range(NT):
                        for f in range(NF):
                            last = pe.matmul(g[:, D * t:D * t + D], hid0[:, st.arg % 2, f, P * t:P * t + P],
                                             wd_sb[:, st.arg, f, :], start=(f == 0), stop=(f == NF - 1))
                    last.then_inc(full[st.bank], 1)
                if name == "w1":
                    if st.arg == 0:
                        wait(pe, s_xl[1], n.at(1, 1))
                    g = take(st)
                    for j in range(2):
                        a = 2 * st.arg + j
                        terms = [(xx, k) for xx in (xt_hi, xt_lo) for k in range(NK)]
                        for i, (xx, k) in enumerate(terms):
                            last = pe.matmul(g[:, S * j:S * j + S], t1_sb[:, k, P * a:P * a + P], xx[1][:, k, :],
                                             start=(i == 0), stop=(i == len(terms) - 1))
                    last.then_inc(full[st.bank], 1)
                if name == "w2":
                    if st.arg == 0:
                        wait(pe, s_h1, n.at(NH, NH))
                    g = take(st)
                    for a in range(NH):
                        last = pe.matmul(g[:, 0:D], hid1[:, a, P * st.arg:P * st.arg + P], t2_sb[:, a, :],
                                         start=(a == 0), stop=(a == NH - 1))
                    last.then_inc(full[st.bank], 1)
                if name in ("op0", "op1"):
                    l = int(name[2])
                    if first and l == 0:
                        pe.wait_ge(s_wo, 16 * 2 * G4)
                    wait(pe, s_at, groups_of_block(st, l))
                    g = take(st)
                    for t in (range(NT) if l == 0 else [st.arg]):
                        o = g[:, D * t:D * t + D] if l == 0 else g[:, 0:D]
                        for q in range(G4):
                            last = pe.matmul(o, at[l][:, q, P * t:P * t + P], wo_sb[l][:, q, :],
                                             start=(q == 0), stop=(q == G4 - 1))
                    last.then_inc(full[st.bank], 1)
                if name == "score":
                    s = st.arg
                    u, hh = s // 8, s % 8
                    if hh == 0:
                        wait(pe, s_stack[u % 2], st.it.at(64, 32 * (u // 2)))
                    wait(pe, s_mx, heads_before(st, -1))
                    g, q, k = score_ps[s % 2], q_stack[u % 2], k_stack[u % 2]
                    pe.matmul(g[:, 0:S], q[:, hh, P:S], k[:, hh, :], start=True, stop=True)
                    pe.matmul(g[:, S:S + P], q[:, hh, 0:P], k[:, hh, 0:P], start=True, stop=True).then_inc(s_sc, 1)
                if name == "turn":
                    s = st.arg
                    wait(pe, s_nm, heads_before(st, 1))
                    wait(pe, s_ev, heads_before(st, -1))
                    g, p = turn_ps[s % 2], probs[:, s % 4]
                    pe.transpose(g[:, 0:P], p[:, P:S], ident[:])
                    pe.transpose(g[:, P:2 * P], p[:, S:S + P], ident[:])
                    pe.transpose(g[:, 2 * P:3 * P], p[:, 0:P], ident[:]).then_inc(s_tn, 1)
                if name == "value":
                    l = group_block(st)
                    nb = batch_of(st, l)
                    gg = st.arg % G4
                    if gg == 0:
                        wait(pe, s_v[l], (nb if l == 0 else ahead(nb)).at(NT, NT))
                        if st.kind == "first":
                            pe.wait_ge(s_pool, POOL_PT)
                    wait(pe, s_ev, st.it.at(2 * H, G4 * (st.arg + 1) - H))
                    wait(pe, s_at, groups_before(st))
                    for j in range(G4):
                        s = G4 * st.arg + j
                        pe.matmul(value_ps[PAD * j:PAD * j + PAD, 0:S], v_sb[l][:, 0, G4 * gg + j, :],
                                  pt[:, s % 8, S:2 * S], start=True, stop=False)
                    for j in range(G4):
                        s = G4 * st.arg + j
                        lo = 0 if l == 0 else P
                        last = pe.matmul(value_ps[PAD * j:PAD * j + PAD, lo:S], v_sb[l][:, 1, G4 * gg + j, :],
                                         pt[:, s % 8, lo:S], start=False, stop=True)
                    last.then_inc(s_pv, 1)

            def before_block1():
                pe.wait_ge(s_lo, 2 + E)
                pe.wait_ge(s_t, 2 * TERN)
                pe.wait_ge(s_c, 16 * NC)

            run_passes(pe, do, before_block1)

        @block.vector
        def _(dve):
            def do(st):
                n, name, b = st.n, st.name, st.bank
                g = gen_ps[b] if b is not None else None
                if name == "setup" and st.arg == 0:
                    dve.memset(v_sb[0][:], 0.0).then_inc(s_set, 1)
                if name == "setup" and st.arg == 2:
                    dve.wait_ge(s_c, 16 * NC)
                    dve.reciprocal(half_t[:], half_t[:]).then_inc(s_set, 1)
                    dve.wait_ge(s_set, 2)
                    dve.tensor_scalar(half_t[:], half_t[:], 0.5, None, ALU.mult).then_inc(s_set, 1)
                    dve.tensor_scalar(bqk[0][:, 0:2], bqk[0][:, 0:2], float(C) ** -0.5, None, ALU.mult)\
                       .then_inc(s_set, 1)
                    dve.tensor_scalar(bqk[1][:, 0:2], bqk[1][:, 0:2], float(C) ** -0.5, None, ALU.mult)\
                       .then_inc(s_set, 1)
                if name == "setup" and st.arg == 1:
                    dve.wait_ge(s_pool, POOL_REL)
                    dve.tensor_copy(rel, rel_i).then_inc(s_set, 1)
                    dve.wait_ge(s_set, SET_REL)
                    for h in range(H):
                        dve.scalar_tensor_tensor(bias0[:, h], rel, slope_sb[:, h:h + 1], bias1[:], ALU.mult, ALU.add)\
                           .then_inc(s_set, 1)
                if name == "split":
                    i = st.arg
                    dve.wait_ge(s_hi, i + 1)
                    qk = i in (0, E + 1)
                    hi, lo = (qk_hi[i // E][:], qk_lo[i // E][:]) if qk else (gu_hi[:, i - 1], gu_lo[:, i - 1])
                    flat = "p k n -> p (k n)" if qk else "p m k f -> p (m k f)"
                    dve.scalar_tensor_tensor(lo.rearrange(flat), raw[i % 2], WSCALE, hi.rearrange(flat),
                                             ALU.mult, ALU.subtract)\
                       .then_inc(s_lo, 1)
                if name == "tern":
                    i, t0 = st.arg, TERN * st.arg
                    w = (w1_raw, w2_raw)[i]
                    t = (t1_sb[:].rearrange("p k n -> p (k n)"), t2_sb[:].rearrange("p a d -> p (a d)"))[i]
                    dve.wait_ge(s_w1, 32)
                    dve.tensor_reduce(t_max[:, i:i + 1], w, AX.X, ALU.max, apply_absolute_value=True).then_inc(s_t, 1)
                    dve.wait_ge(s_tp, 2 * i + 1)
                    dve.tensor_scalar(t_delta[:, i, 0:1], t_amax[:, i:i + 1], 0.05, None, ALU.mult).then_inc(s_t, 1)
                    dve.tensor_scalar(t_delta[:, i, 1:2], t_amax[:, i:i + 1], -0.05, None, ALU.mult).then_inc(s_t, 1)
                    dve.wait_ge(s_t, t0 + 3)
                    dve.tensor_scalar(t, w, t_delta[:, i, 1:2], None, ALU.is_lt).then_inc(s_t, 1)
                    dve.wait_ge(s_t, t0 + 4)
                    dve.scalar_tensor_tensor(t, w, t_delta[:, i, 0:1], t, ALU.is_gt, ALU.subtract).then_inc(s_t, 1)
                    dve.wait_ge(s_t, t0 + 5)
                    dve.tensor_tensor_reduce(out=w, in0=w, in1=t, scale=1.0, scalar=0.0, op0=ALU.mult, op1=ALU.add,
                                             accum_out=t_sum[:, i, 0:1]).then_inc(s_t, 1)
                    dve.wait_ge(s_t, t0 + 6)
                    dve.tensor_tensor_reduce(out=w, in0=t, in1=t, scale=1.0, scalar=0.0, op0=ALU.mult, op1=ALU.add,
                                             accum_out=t_sum[:, i, 1:2]).then_inc(s_t, 1)
                    dve.wait_ge(s_tp, 2 * i + 2)
                    dve.tensor_scalar(t_tot[:, i, 1:2], t_tot[:, i, 1:2], 1.0, None, ALU.max).then_inc(s_t, 1)
                    dve.wait_ge(s_t, t0 + 8)
                    dve.reciprocal(t_tot[:, i, 1:2], t_tot[:, i, 1:2]).then_inc(s_t, 1)
                    dve.wait_ge(s_t, t0 + 9)
                    dve.tensor_tensor(alpha[:, i:i + 1], t_tot[:, i, 0:1], t_tot[:, i, 1:2], ALU.mult).then_inc(s_t, 1)
                if name in ("ln0a", "ln1a"):
                    l = int(name[2])
                    if l == 0:
                        wait(dve, s_x, n.at(16, 16))
                    else:
                        wait(dve, s_acc, n.at(NT * ACC_STEPS, NT * ACC_STEPS))
                    src = (x0, acc)[l]
                    for t in range(NT):
                        dve.bn_stats(stats[:, t], src[:, t]).then_inc(s_st[l], 1)
                    wait(dve, s_st[l], n.at(5, 2))
                    if st.kind == "steady":
                        settle(dve, s_dve)
                    for t in range(NT):
                        dve.bn_aggr(mv[l][:, t], stats[:, t]).then_inc(s_st[l], 1)
                    wait(dve, s_st[l], n.at(5, 4))
                    dve.tensor_scalar(var[l][:], mv[l][:, :, 1], EPS, None, ALU.add).then_inc(s_st[l], 1)
                if name in ("ln0b", "ln1b"):
                    l = int(name[2])
                    src = (x0, acc)[l]
                    wait(dve, s_rstd[l], n.at(1, 1))
                    wait(dve, s_xb[l], n.at(NT, NT))
                    for t in range(NT):
                        dve.tensor_scalar(src[:, t], src[:, t], mv[l][:, t, 0:1], rstd[l][:, t:t + 1],
                                          ALU.subtract, ALU.mult).then_inc(s_xn[l], 1)
                if name in ("tr0", "tr1"):
                    l = int(name[2])
                    wait(dve, s_xh[l], n.at(2, 2))
                    if l == 0:
                        wait(dve, s_xe, n.at(2))
                    dve.tensor_tensor(xt_lo[l][:].rearrange("p k s -> p (k s)"), g[:, :],
                                      xt_hi[l][:].rearrange("p k s -> p (k s)"), ALU.subtract).then_inc(s_xl[l], 1)
                if name in ("r0", "r1"):
                    l = int(name[1])
                    wait(dve, s_ph[l], n.at(8, 8))
                    dve.tensor_tensor(rest[:], rest[:], parts[:, :, 0], ALU.subtract).then_inc(s_pr[l], 1)
                if name in ("l0", "l1"):
                    l = int(name[1])
                    wait(dve, s_pm[l], n.at(1, 1))
                    dve.tensor_tensor(parts[:, :, 2], rest[:], parts[:, :, 1], ALU.subtract).then_inc(s_pl[l], 1)
                if name in ("v0", "v1"):
                    l = int(name[1])
                    for t in ([st.arg] if l == 0 else range(NT)):
                        if l == 0:
                            wait(dve, s_th, n.at(NT, t + 1))
                        elif t == 0:
                            wait(dve, full[b], st.filled)
                        if t == 0:
                            if l == 0:
                                wait(dve, s_pv, n.at(8, -8) if n.reg is not None or n.off > 1 else 4 * n.off)
                            else:
                                wait(dve, s_pv, n.at(8, 4))
                        o = g[:, 0:D] if l == 0 else g[:, D * t:D * t + D]
                        dve.tensor_tensor(v_sb[l][:, t, :, 0:C], o.rearrange("p (h c) -> p h c", c=C),
                                          vb[l][:].rearrange("p (h c) -> p h c", c=C), ALU.add).then_inc(s_v[l], 1)
                if name == "rt1":
                    def zone(ins):
                        ins.then_inc(s_rt, 1)
                    wait(dve, s_th, n.at(NT, NT))
                    zone(dve.tensor_scalar(r_in[:], r_tanh[:], 0.5, 0.5, ALU.mult, ALU.add))
                    wait(dve, s_rt, n.at(RT, 1))
                    zone(dve.tensor_scalar(r_zone[:], r_in[:], float(GOLD_LO), None, ALU.is_ge))
                    zone(dve.tensor_scalar(r_d[:], r_in[:], float(GOLD_C), None, ALU.subtract))
                    wait(dve, s_rt, n.at(RT, 3))
                    zone(dve.scalar_tensor_tensor(r_zone2[:], r_in[:], GOLD_HI, r_zone[:], ALU.is_le, ALU.mult))
                    wait(dve, s_re, n.at(2))
                    zone(dve.scalar_tensor_tensor(r_dist[:], r_d[:], -1.0, r_d[:], ALU.mult, ALU.max))
                if name == "rt2":
                    per_token = [P, NT, E]
                    pairs = [P, NT, E, E]

                    def route(k, ins):
                        ins.then_inc(s_rt, 1)

                    def after(k):
                        wait(dve, s_rt, n.at(RT, 5 + k))
                    if st.kind == "first":
                        dve.wait_ge(s_pool, POOL_BEFORE)
                    wait(dve, s_re, n.at(2, 2))
                    route(1, dve.tensor_tensor(r_gt[:], r_e2[:].unsqueeze(2).broadcast_to(pairs),
                                               r_e2[:].unsqueeze(3).broadcast_to(pairs), ALU.is_gt))
                    route(2, dve.tensor_tensor(r_eq[:], r_e2[:].unsqueeze(2).broadcast_to(pairs),
                                               r_e2[:].unsqueeze(3).broadcast_to(pairs), ALU.is_equal))
                    route(3, dve.tensor_tensor(r_w[:], r_e1[:], r_zone2[:], ALU.mult))
                    after(2)
                    route(4, dve.tensor_tensor(r_eq[:], r_eq[:], before[:].unsqueeze(1).broadcast_to(pairs), ALU.mult))
                    after(3)
                    route(5, dve.tensor_reduce(r_s[:, 0], r_w[:], AX.X, ALU.add))
                    after(4)
                    route(6, dve.tensor_tensor(r_gt[:], r_gt[:], r_eq[:], ALU.add))
                    after(5)
                    route(7, dve.tensor_scalar(r_s[:, 1], r_s[:, 0], 1e-8, None, ALU.is_lt))
                    after(6)
                    route(8, dve.tensor_reduce(r_rank[:].unsqueeze(3), r_gt[:], AX.X, ALU.add))
                    after(7)
                    route(9, dve.tensor_scalar(r_s[:, 2], r_s[:, 1], -1.0, 1.0, ALU.mult, ALU.add))
                    after(8)
                    route(10, dve.scalar_tensor_tensor(r_fb[:], r_rank[:], 2.0, r_e2[:], ALU.is_lt, ALU.mult))
                    after(10)
                    route(11, dve.tensor_reduce(r_s[:, 3], r_fb[:], AX.X, ALU.add))
                    route(12, dve.tensor_tensor(r_w[:], r_w[:], r_s[:, 2].broadcast_to(per_token), ALU.mult))
                    after(11)
                    route(13, dve.tensor_scalar(r_s[:, 3], r_s[:, 3], 1e-8, None, ALU.max))
                    after(13)
                    route(14, dve.reciprocal(r_s[:, 4], r_s[:, 3]))
                    after(14)
                    route(15, dve.tensor_tensor(r_fb[:], r_fb[:], r_s[:, 4].broadcast_to(per_token), ALU.mult))
                    after(15)
                    route(16, dve.tensor_tensor(r_fb[:], r_fb[:], r_s[:, 1].broadcast_to(per_token), ALU.mult))
                    after(16)
                    route(17, dve.tensor_tensor(r_w[:], r_w[:], r_fb[:], ALU.add))
                    after(17)
                    route(18, dve.tensor_reduce(r_s[:, 5], r_w[:], AX.X, ALU.add))
                    after(18)
                    route(19, dve.tensor_scalar(r_s[:, 5], r_s[:, 5], 1e-8, None, ALU.max))
                    after(19)
                    route(20, dve.reciprocal(r_s[:, 0], r_s[:, 5]))
                    after(20)
                    dve.tensor_tensor(w8[:], r_w[:], r_s[:, 0].broadcast_to(per_token), ALU.mult).then_inc(s_w8, 1)
                if name == "gate":
                    wait(dve, s_tg, n.at(E, st.arg + 1))
                    dve.scalar_tensor_tensor(gated[:], tanh_sb[:], 1.0, g[:, :], ALU.add, ALU.mult).then_inc(s_ga, 1)
                if name == "up":
                    wait(dve, full[b], st.filled)
                    wait(dve, s_ga, n.at(E, st.arg + 1))
                    dve.scalar_tensor_tensor(hid0[:, st.arg % 2].rearrange("p f s -> p (f s)"), gated[:],
                                             0.5 / (WSCALE * WSCALE), g[:, :], ALU.mult, ALU.mult).then_inc(s_h0, 1)
                if name == "down":
                    e = st.arg
                    wait(dve, full[b], st.filled)
                    if st.place == 0:
                        wait(dve, s_w8, n.at(1, 1))
                        wait(dve, s_xb[0], n.at(NT, NT))
                    wait(dve, s_acc, n.at(NT * ACC_STEPS, NT * st.place))
                    for t in range(NT):
                        dve.scalar_tensor_tensor(acc[:, t], g[:, D * t:D * t + D], w8[:, t, e:e + 1],
                                                 (xb[0] if st.place == 0 else acc)[:, t], ALU.mult, ALU.add)\
                           .then_inc(s_acc, 1)
                if name == "op0":
                    wait(dve, full[b], st.filled)
                    wait(dve, s_acc, n.at(NT * ACC_STEPS, NT * st.place))
                    for t in range(NT):
                        dve.tensor_tensor(acc[:, t], g[:, D * t:D * t + D], acc[:, t], ALU.add).then_inc(s_acc, 1)
                if name == "w2":
                    t = st.arg
                    wait(dve, full[b], st.filled)
                    if t == 0:
                        wait(dve, s_yw, ahead(n).at(16))
                    dve.scalar_tensor_tensor(y_sb[:, t], g[:, 0:D], alpha[:, 1:2], b2_sb[:], ALU.mult, ALU.add)\
                       .then_inc(s_y, 1)
                    wait(dve, s_y, ahead(n).at(NT, t + 1))
                    dve.tensor_reduce(ymax[:, bass.ds(n.at(NT, t), 1)], y_sb[:, t], AX.X, ALU.max,
                                      apply_absolute_value=True).then_inc(s_ym, 1)
                if name == "op1":
                    t = st.arg
                    wait(dve, full[b], st.filled)
                    if t == 0:
                        wait(dve, s_xb[1], n.at(NT, NT))
                        wait(dve, s_x2w, ahead(n).at(16))
                    dve.tensor_tensor(x2_sb[:, t], g[:, 0:D], xb[1][:, t], ALU.add).then_inc(s_x2, 1)
                if name == "score":
                    s, l = st.arg, head_block(st)
                    k, g = s % 4, score_ps[s % 2]
                    wait(dve, s_sc, heads_before(st, 1))
                    wait(dve, s_tn, heads_before(st, -3))
                    if st.kind == "steady":
                        settle(dve, s_dve)
                    if st.kind == "first":
                        dve.wait_ge(s_set, SET_BIAS0)
                    bias = bias0[:, s % H] if l == 0 else bias1[:]
                    for lo, hi, blo, j in ((0, S, 0, 0), (S, S + P, P, 1)):
                        last = dve.tensor_tensor_reduce(out=probs[:, k, lo:hi], in0=g[:, lo:hi], in1=bias[:, blo:S],
                                                        scale=-1.0, scalar=BIG, op0=ALU.add, op1=ALU.min,
                                                        accum_out=nmax[:, k, j:j + 1])
                    last.then_inc(s_mx, 1)
                if name == "norm":
                    s, l = st.arg, head_block(st)
                    k = s % 4
                    wait(dve, s_ex, heads_before(st, 1))
                    dve.reciprocal(rsum[:, k], esum[:, k]).then_inc(s_rz, 1)
                    wait(dve, s_rz, heads_before(st, 1))
                    for lo, hi, j in ((0, S, 0), (S, S + P, 1)):
                        clamp = (CLAMP, ALU.mult, ALU.max) if l == 0 else (None, ALU.mult)
                        last = dve.tensor_scalar(probs[:, k, lo:hi], probs[:, k, lo:hi], rsum[:, k, j:j + 1], *clamp)
                    last.then_inc(s_nm, 1)

            def before_block1():
                dve.wait_ge(s_v1z, 1)
                for counts in (s_v[1], s_y, s_x2):
                    dve.sem_inc(counts, NT)

            run_passes(dve, do, before_block1)

            dve.wait_ge(s_ym, B * NT)
            dve.tensor_reduce(yred[:, 0:1], ymax[:], AX.X, ALU.max).then_inc(s_q, 1)
            dve.wait_ge(s_qp, 1)
            dve.tensor_scalar(yred[:, 2:3], yred[:, 1:2], 1.0 / QMAX, 1e-8, ALU.mult, ALU.add).then_inc(s_q, 1)
            dve.wait_ge(s_q, 2)
            dve.reciprocal(yred[:, 3:4], yred[:, 2:3]).then_inc(s_q, 1)
            for c in range(B):
                y_c = y_all[:, NT * c:NT * c + NT, :] if c < B - 1 else y_sb[:]
                x_c = x_all[:, NT * c:NT * c + NT, :] if c < B - 1 else x2_sb[:]
                dve.wait_ge(s_qa, c + 1)
                dve.tensor_scalar(y_c, y_c, QMAX, -QMAX, ALU.min, ALU.max).then_inc(s_q, 1)
                dve.wait_ge(s_q, 4 + 2 * c)
                dve.tensor_scalar(y_c, y_c, ROUND, ROUND, ALU.add, ALU.subtract).then_inc(s_q, 1)
                dve.wait_ge(s_q, 5 + 2 * c)
                dve.scalar_tensor_tensor(y_c, y_c, yred[:, 2:3], x_c, ALU.mult, ALU.add).then_inc(s_qo, 1)


def kernel(L0_attn_qkv, L0_attn_in_proj, L0_attn_in_proj_bias, L0_attn_out_w, L0_attn_out_b, L0_attn_alibi_slopes,
           L0_ffn_Wg, L0_ffn_Wu, L0_ffn_Wd, L0_ffn_Wr, L0_ffn_temperature, L1_attn_Wq, L1_attn_bq, L1_attn_Wk,
           L1_attn_bk, L1_attn_Wv, L1_attn_bv, L1_attn_Wo, L1_attn_bo, L1_ffn_W1, L1_ffn_b1, L1_ffn_W2, L1_ffn_b2):
    import concourse.bacc as bacc
    from concourse.bass_utils import run_bass_kernel_spmd

    def by_channel(w):
        w = w.reshape(-1, H, C).transpose(0, 2, 1)
        return w.reshape(-1, P, 2).transpose(0, 2, 1).reshape(-1, H * C)

    def columns(q, k):
        return np.concatenate([by_channel(q.reshape(1, -1)), by_channel(k.reshape(1, -1))], 1).reshape(4, P).T

    proj, pb = np.asarray(L0_attn_in_proj), np.asarray(L0_attn_in_proj_bias)
    a = {k: np.asarray(v) for k, v in locals().items() if k.startswith("L")}
    heads = {k: a["L1_attn_W" + k].transpose(1, 0, 2).reshape(D, D) for k in "qkv"}
    arrays = {
        "x": a["L0_attn_qkv"],
        "wqk0": np.concatenate([by_channel(proj[0:D].T), by_channel(proj[D:2 * D].T)], 1),
        "bqk0": columns(pb[0:D], pb[D:2 * D]),
        "wv0": np.concatenate([proj[2 * D:].T, a["L0_ffn_Wr"]], 1),
        "vb0": pb[2 * D:],
        "wo0": a["L0_attn_out_w"].T,
        "ob0": a["L0_attn_out_b"],
        "slopes": a["L0_attn_alibi_slopes"],
        "wg": a["L0_ffn_Wg"],
        "wu": a["L0_ffn_Wu"],
        "wd": a["L0_ffn_Wd"],
        "temp": a["L0_ffn_temperature"],
        "wqk1": np.concatenate([by_channel(heads["q"]), by_channel(heads["k"])], 1),
        "bqk1": columns(a["L1_attn_bq"], a["L1_attn_bk"]),
        "wv1": heads["v"],
        "vb1": a["L1_attn_bv"].reshape(-1),
        "wo1": a["L1_attn_Wo"],
        "ob1": a["L1_attn_bo"],
        "w1t": a["L1_ffn_W1"].T,
        "b1c": a["L1_ffn_b1"].reshape(NH, P).T,
        "w2t": a["L1_ffn_W2"].T,
        "b2": a["L1_ffn_b2"],
    }
    arrays = {k: np.ascontiguousarray(v) for k, v in arrays.items()}
    nc = bacc.Bacc("TRN2", target_bir_lowering=False, num_devices=1)
    args = [nc.dram_tensor("in_" + k, v.shape, mybir.dt.from_np(v.dtype), kind="ExternalInput").ap() for k, v in arrays.items()]
    out = nc.dram_tensor("out_dram", (B, S, D), F32, kind="ExternalOutput").ap()
    two_blocks(nc, *args, out)
    r = run_bass_kernel_spmd(nc, [{"in_" + k: v for k, v in arrays.items()}], core_ids=[0])
    return r.results[0]["out_dram"]
```

```python
from contextlib import ExitStack

import numpy as np
import concourse.bass as bass
from concourse import mybir

F32 = mybir.dt.float32
F16 = mybir.dt.float16
BF16 = mybir.dt.bfloat16
I32 = mybir.dt.int32
ALU = mybir.AluOpType
ACT = mybir.ActivationFunctionType
AX = mybir.AxisListType
R_MAX = bass.bass_isa.ReduceOp.max
R_ADD = bass.bass_isa.ReduceOp.add

P = 128
B, S, D = 8, 256, 256
H, C = 16, 16
NT = S // P
NK = D // P
E, F = 8, 256
NF = F // P
HID = 1024
NH = HID // P
PAD = 32
G4 = P // PAD
VB = P + C
SPLITS = 6
KR = SPLITS * C
EPS = 1e-5
CLAMP = 1e-10
MASKED = -1e30
BIG = 3e38
WSCALE = 16.0
GOLD_C = 1.0 / np.e
GOLD_LO = 0.5 - np.log(4.0 / 3.0)
GOLD_HI = 0.5
QMAX = 7.0
ROUND = 1.5 * 2.0 ** 23

BANKED = {"tr0", "q0", "k0", "v0", "gate", "up", "down", "op0",
          "tr1", "w1", "q1", "k1", "v1", "w2", "op1"}
RING = 3


NORM_LAG, TURN_LAG, VALUE_LAG = 1, 3, 1
TURNED = 8
FLUSH = TURN_LAG + VALUE_LAG
PROBS = 8

LAG = {"scalar": {},
       "vector": {"gate": 1, "up": 1, "down": 1, "op0": 1, "w2": 2, "l1": 2, "qmax": 2}}


def with_heads(order, last):
    first = next(x for x in order if isinstance(x, int))
    out = []

    def head(s):
        if s <= last:
            out.append(("score", s, 0))
        if first <= s - NORM_LAG <= last:
            out.append(("norm", s - NORM_LAG, 0))
        t = s - TURN_LAG
        if first <= t <= last:
            out.append(("turn", t, 0))
        t -= VALUE_LAG
        if first <= t <= last and t % G4 == G4 - 1:
            out.append(("value", t // G4, 0))

    for item in order:
        if isinstance(item, int):
            head(item)
        else:
            out.append(item)
    return out


FIRST_ORDER = """
    setup:0 ln0a setup:2 split:0 ln0b tr0 split:1 q0 k0 xe r0 v0:0 m0 v0:1 l0 setup:1 rt1 split:2 gate:0 up:0
    rt2 split:3 gate:1 up:1 16 down:0 17 split:4 gate:2 18 up:2 19 down:1 20 split:5 gate:3 21 up:3 down:2 22 23
    split:6 gate:4 24 up:4 25 down:3 26 tern:0 split:7 gate:5 27 up:5 28 down:4 29 split:8 gate:6 30 up:6 +ln0a
    31 down:5 gate:7 32 +ln0b up:7 split:9 tern:1 33 +tr0 34 35 down:6 +q0 +k0 +r0 +v0:0 +m0 +l0 +v0:1 +xe
    down:7 op0
"""
STEADY_ORDER = """
    ln1a rt1 0 gate:0 ln1b 1 up:0 rt2 tr1 2 3 gate:1 q1 k1 4 up:1 r1 5 down:0 m1 v1 6 l1 7 w1:0 w1:1 w1:2 w1:3
    down:1 gate:2 up:2 8 9 10 gate:3 11 12 up:3 13 14 down:2 15 gate:4 16 up:4 17 down:3 w2:0 18 w2:1 19 gate:5
    op0 20 up:5 21 +ln0a 22 down:4 +ln0b 23 +tr0 gate:6 24 +q0 +k0 25 down:5 up:6 +r0 +v0:0 +m0 26 27 +l0 28
    gate:7 +v0:1 29 30 up:7 +xe 31 down:6 32 down:7 33 34 35 op1:0 op1:1
"""
FINAL_ORDER = """
    ln1a ln1b tr1 q1 k1 r1 v1 m1 l1 w1:0 w1:1 w1:2 w1:3 0 w2:0 1 w2:1 2 3 qmax 4 5 quant:0 6 quant:1 7 quant:2 8
    quant:3 9 quant:4 10 quant:5 11 quant:6 12 quant:7 13 14 15 16 17 18 19 op1:0 op1:1
"""
BLOCK1 = {"ln1a", "ln1b", "tr1", "q1", "k1", "r1", "m1", "l1", "v1", "w1", "w2", "op1", "qmax", "quant"}


def order_of(text, last, with_next=True):
    out = []
    for word in text.split():
        if word.startswith("+") and not with_next:
            continue
        name, _, arg = word.lstrip("+").partition(":")
        if name.isdigit():
            out.append(int(name))
        else:
            out.append((name, int(arg or 0), -1 if name in BLOCK1 else int(word.startswith("+"))))
    return with_heads(out, last)


def uses(order):
    return sum(s[0] in BANKED for s in order)


ORDERS = {"first": order_of(FIRST_ORDER, 31), "steady": order_of(STEADY_ORDER, 31),
          "last": order_of(STEADY_ORDER, 31, with_next=False), "final": order_of(FINAL_ORDER, 15)}
USES_STEADY = uses(ORDERS["steady"])
assert USES_STEADY % RING == 0
ROUNDS = USES_STEADY // RING
STEADY = B - 2
USES_BEFORE = {"first": 0, "steady": uses(ORDERS["first"]), "last": uses(ORDERS["first"]) + USES_STEADY * STEADY}
USES_BEFORE["final"] = USES_BEFORE["last"] + uses(ORDERS["last"])
PASS_OF = {"first": 0, "steady": 1, "last": B - 1, "final": B}
ACC_STEPS = E + 1


class Index:

    def __init__(self, reg, off):
        self.reg, self.off = reg, off

    def plus(self, d):
        return Index(self.reg, self.off + d)

    def at(self, per, extra=0):
        v = self.off * per + extra
        return v if self.reg is None else self.reg * per + v


class Stage:

    def __init__(self, kind, step, it):
        self.name, self.arg, d = step
        self.kind, self.it, self.n = kind, it, it.plus(d)
        self.bank = self.filled = self.before = self.place = None


def stages(kind, it, lag):
    out, users, place = [], [None] * RING, 0
    use = USES_BEFORE[kind]
    for step in ORDERS[kind]:
        st = Stage(kind, step, it)
        if st.name in BANKED:
            st.bank = use % RING
            st.filled = it.at(ROUNDS, use // RING + 1 - ROUNDS * PASS_OF[kind])
            st.before, users[st.bank] = users[st.bank], st
            use += 1
        if st.name in ("down", "op0"):
            st.place = place
            place += 1
        out.append(st)
    late = [i + lag.get(st.name, 0) for i, st in enumerate(out)]
    return [out[i] for i in sorted(range(len(out)), key=lambda i: (late[i], i))]


def head_block(st):
    return {"first": 0, "final": 1}.get(st.kind, st.arg // H)


def set_block(st):
    return {"first": 0, "final": 1}.get(st.kind, st.arg // (H // G4))


def batch_of(st, block):
    return st.it if block == 0 else st.it.plus(-1)


def heads_before(st, extra=0):
    return st.it.at(2 * H, st.arg - H + extra)


def sets_before(st, extra=0):
    return st.it.at(2 * H // G4, st.arg - H // G4 + extra)


def at_before(st):
    return st.it.at(2 * NK, st.arg // 2 - NK)


def at_of_block(st, block):
    end = 2 * NK if (block == 1) != (st.kind in ("first", "final")) else NK
    return st.it.at(2 * NK, end - NK)


def ahead(n):
    return n.plus(1)


def wait(eng, sem, value):
    if not (isinstance(value, int) and value <= 0):
        eng.wait_ge(sem, value)


def settle(eng, passed):
    eng.sem_inc(passed, 1)


def run_passes(eng, do, before_block1, lag):
    for st in stages("first", Index(None, 0), lag):
        do(st)
    before_block1()
    with eng.Fori(0, STEADY) as j:
        for st in stages("steady", Index(j, 1), lag):
            do(st)
    for st in stages("last", Index(None, B - 1), lag):
        do(st)
    for st in stages("final", Index(None, B), lag):
        do(st)


def two_blocks(nc, x, wqk0, bqk0, wv0, vb0, wo0, ob0, slopes, wg, wu, wd, temp,
               wqk1, bqk1, wv1, vb1, wo1, ob1, w1t, b1c, w2t, b2, out):
    with ExitStack() as ctx:
        def sb(name, shape, dt=F32):
            return ctx.enter_context(nc.sbuf_tensor(name, shape, dt))

        def sem(name):
            return ctx.enter_context(nc.semaphore(name))

        score_ps = [ctx.enter_context(nc.psum_tensor(f"score_ps{i}", [P, 512], F32)) for i in range(2)]
        turn_ps = [ctx.enter_context(nc.psum_tensor(f"turn_ps{i}", [P, 512], F32)) for i in range(2)]
        value_ps = ctx.enter_context(nc.psum_tensor("value_ps", [P, 512], F32))
        gen_ps = [ctx.enter_context(nc.psum_tensor(f"gen_ps{i}", [P, 512], F32)) for i in range(RING)]

        gu_hi = sb("gu_hi", [P, E, 2, NK, F], F16)
        gu_lo = sb("gu_lo", [P, E, 2, NK, F], F16)
        wd_sb = sb("wd_sb", [P, E, NF, D])
        qk_hi = [sb(f"qk_hi{l}", [P, NK, 2 * D], F16) for l in range(2)]
        qk_lo = [sb(f"qk_lo{l}", [P, NK, 2 * D], F16) for l in range(2)]
        wv_sb = [sb("wv0_sb", [P, NK, D + E]), sb("wv1_sb", [P, NK, D])]
        wo_sb = [sb(f"wo{l}_sb", [P, NK, D]) for l in range(2)]
        t1_sb = sb("t1_sb", [P, NK, HID], F16)
        t2_hid = sb("t2_hid", [P, 2, NH * D // 2])
        t2_sb = t2_hid[:, 0].bitcast(F16).rearrange("p (a d) -> p a d", d=D)
        hid1 = t2_hid[:, 1].rearrange("p (a s) -> p a s", s=S)
        bqk = [sb(f"bqk{l}", [P, 4]) for l in range(2)]
        vb = [sb(f"vb{l}_sb", [P, D]) for l in range(2)]
        ob = [sb(f"ob{l}_sb", [P, D]) for l in range(2)]
        b2_sb = sb("b2_sb", [P, D])
        b1_sb = sb("b1_sb", [P, NH])
        slope_sb = sb("slope_sb", [P, H])
        half_t = sb("half_t", [P, 1])
        minus_half = sb("minus_half", [P, NT])
        before = sb("before", [P, E, E])
        ident = sb("ident", [P, P])
        bias0 = sb("bias0", [P, H, S])
        bias1 = sb("bias1", [P, S])
        x0 = sb("x0", [P, NT, D])
        acc = sb("acc", [P, NT, D])
        xb = [sb(f"xb{l}", [P, NT, D]) for l in range(2)]
        stats = sb("stats", [P, NT, 6])
        mv = [sb(f"mv{l}", [P, NT, 2]) for l in range(2)]
        var = [sb(f"var{l}", [P, NT]) for l in range(2)]
        rstd = [sb(f"rstd{l}", [P, NT]) for l in range(2)]
        xt = sb("xt", [P, NK, S])
        xt_hi = sb("xt_hi", [P, NK, S], F16)
        xt_lo = sb("xt_lo", [P, NK, S], F16)
        xe_hi = sb("xe_hi", [P, NK, S], F16)
        xe_lo = sb("xe_lo", [P, NK, S], F16)
        rest = sb("rest", [P, 2, 2, S])
        parts = sb("parts", [P, 2, 3, 2, S], BF16)
        q_stack = [sb(f"q_stack{i}", [KR, H // 2, S], BF16) for i in range(2)]
        k_stack = [sb(f"k_stack{i}", [KR, H // 2, S], BF16) for i in range(2)]
        v_sb = [sb(f"v{l}_sb", [P, NT, H // G4, VB]) for l in range(2)]
        probs = sb("probs", [P, PROBS, 3 * P])
        nmax = sb("nmax", [P, PROBS, 2])
        esum = sb("esum", [P, PROBS, 2])
        rsum = sb("rsum", [P, PROBS, 2])
        pt = sb("pt", [P, 1 + 3 * TURNED, P])
        at = [sb(f"at{l}", [P, NK, S]) for l in range(2)]
        tanh_sb = sb("tanh_sb", [P, NF * S])
        gated = sb("gated", [P, NF * S])
        hid0 = sb("hid0", [P, 2, NF, S])
        h1_parts = sb("h1_parts", [P, 2, NH, S], F16)
        yx_sb = sb("yx_sb", [P, 2, NT, D])
        y_sb, x2_sb = yx_sb[:, 0], yx_sb[:, 1]
        r_tanh = sb("r_tanh", [P, NT, E])
        r_in = sb("r_in", [P, NT, E])
        r_zone = sb("r_zone", [P, NT, E])
        r_zone2 = sb("r_zone2", [P, NT, E])
        r_d = sb("r_d", [P, NT, E])
        r_dist = sb("r_dist", [P, NT, E])
        r_e1 = sb("r_e1", [P, NT, E])
        r_e2 = sb("r_e2", [P, NT, E])
        r_w = sb("r_w", [P, NT, E])
        r_fb = sb("r_fb", [P, NT, E])
        r_rank = sb("r_rank", [P, NT, E])
        r_gt = sb("r_gt", [P, NT, E, E])
        r_eq = sb("r_eq", [P, NT, E, E])
        r_s = sb("r_s", [P, 6, NT, 1])
        w8 = sb("w8", [P, NT, E])
        t_max = sb("t_max", [P, 2])
        t_amax = sb("t_amax", [P, 2])
        t_delta = sb("t_delta", [P, 2, 2])
        t_sum = sb("t_sum", [P, 2, 2])
        t_tot = sb("t_tot", [P, 2, 2])
        alpha = sb("alpha", [P, 2])
        ymax = sb("ymax", [P, B * NT])
        yred = sb("yred", [P, 4])

        raw = [v_sb[1][:].rearrange("p t b c -> p (t b c)")[:, 0:2 * NK * D], yx_sb[:].rearrange("p a t d -> p (a t d)")]
        w1_raw = t2_hid[:].rearrange("p a d -> p (a d)")
        w2_raw = h1_parts[:].rearrange("p i a s -> p (i a s)").bitcast(F32)
        y_all = gu_hi[:].rearrange("p e m k f -> p (e m k f)").bitcast(F32).rearrange("p (t d) -> p t d", d=D)
        x_all = gu_lo[:].rearrange("p e m k f -> p (e m k f)").bitcast(F32).rearrange("p (t d) -> p t d", d=D)
        rel_i = hid0[:, 0, 0, :].bitcast(I32)
        rel = hid0[:, 1, 0, :]

        scr = [[nc.dram_tensor(f"scr_{n}{l}", (SPLITS, C * H, S), BF16).ap() for n in "qk"] for l in range(2)]
        y_dram = nc.dram_tensor("y_dram", (B * NT, P, D), F32).ap()
        x2_dram = nc.dram_tensor("x2_dram", (B * NT, P, D), F32).ap()
        x_tiles = x.rearrange("b (t p) d -> p (b t) d", p=P)
        out_tiles = out.rearrange("b (t p) d -> p (b t) d", p=P)
        y_tiles = y_dram.rearrange("t p d -> p t d")
        x2_tiles = x2_dram.rearrange("t p d -> p t d")

        s_x = sem("s_x")
        s_c = sem("s_c")
        s_wv0 = sem("s_wv0")
        s_wd = sem("s_wd")
        s_wo = sem("s_wo")
        s_w1 = sem("s_w1")
        s_raw = [sem(f"s_raw{i}") for i in range(2)]
        s_scr = [sem(f"s_scr{l}") for l in range(2)]
        s_stack = [sem(f"s_stack{i}") for i in range(2)]
        s_yw = sem("s_yw")
        s_x2w = sem("s_x2w")
        s_fin = sem("s_fin")
        s_out = sem("s_out")
        s_pool = sem("s_pool")
        s_set = sem("s_set")
        s_hi = sem("s_hi")
        s_lo = sem("s_lo")
        s_t = sem("s_t")
        s_tp = sem("s_tp")
        s_v1z = sem("s_v1z")
        s_dve = sem("s_dve")
        s_gps = sem("s_gps")
        s_sp = sem("s_sp")
        full = [sem(f"full{i}") for i in range(RING)]
        s_st = [sem(f"s_st{l}") for l in range(2)]
        s_rstd = [sem(f"s_rstd{l}") for l in range(2)]
        s_xb = [sem(f"s_xb{l}") for l in range(2)]
        s_xn = [sem(f"s_xn{l}") for l in range(2)]
        s_xh = [sem(f"s_xh{l}") for l in range(2)]
        s_xl = [sem(f"s_xl{l}") for l in range(2)]
        s_ph = [sem(f"s_ph{l}") for l in range(2)]
        s_pr = [sem(f"s_pr{l}") for l in range(2)]
        s_pm = [sem(f"s_pm{l}") for l in range(2)]
        s_pl = [sem(f"s_pl{l}") for l in range(2)]
        s_v = [sem(f"s_v{l}") for l in range(2)]
        s_th = sem("s_th")
        s_rt = sem("s_rt")
        s_re = sem("s_re")
        s_w8 = sem("s_w8")
        s_xe = sem("s_xe")
        s_tg = sem("s_tg")
        s_ga = sem("s_ga")
        s_h0 = sem("s_h0")
        s_acc = sem("s_acc")
        s_h1 = sem("s_h1")
        s_h1l = sem("s_h1l")
        s_y = sem("s_y")
        s_ym = sem("s_ym")
        s_x2 = sem("s_x2")
        s_sc = sem("s_sc")
        s_mx = sem("s_mx")
        s_ex = sem("s_ex")
        s_rz = sem("s_rz")
        s_nm = sem("s_nm")
        s_tn = sem("s_tn")
        s_ev = sem("s_ev")
        s_pv = sem("s_pv")
        s_at = sem("s_at")
        s_q = sem("s_q")
        s_qp = sem("s_qp")
        s_qa = sem("s_qa")
        s_qo = sem("s_qo")

        RT = 25
        TERN = 10
        NC = 11
        POOL_IDENT, POOL_BEFORE, POOL_REL, POOL_PT = 2, 4, 7, 9
        SET_HALF, SET_BQ, SET_REL, SET_BIAS0 = 3, 5, 6, 6 + H

        def read_by(st):
            n, a, l = st.n, st.arg, int(st.name[-1]) if st.name[-1] in "01" else None
            return {
                "tr": lambda: (s_xl[l], n.at(1, 1)),
                "q": lambda: (s_ph[l], n.at(8, 4)),
                "k": lambda: (s_ph[l], n.at(8, 8)),
                "v": lambda: (s_v[0], n.at(NT, a + 1)) if l == 0 else (s_v[1], ahead(n).at(NT, NT)),
                "gate": lambda: (s_ga, n.at(E, a + 1)),
                "up": lambda: (s_h0, n.at(E, a + 1)),
                "down": lambda: (s_acc, n.at(NT * ACC_STEPS, NT * st.place + NT)),
                "w1": lambda: (s_h1, n.at(2 * NH, 4 * a + 4)),
                "w2": lambda: (s_y, ahead(n).at(NT, a + 1)),
                "op": lambda: (s_x2, ahead(n).at(NT, a + 1)) if l else (s_acc, n.at(NT * ACC_STEPS, NT * st.place + NT)),
            }[st.name if st.name in ("w1", "w2") else st.name.rstrip("01")]()

        block = ctx.enter_context(nc.Block())

        @block.sync
        def _(sp):
            def load_x(n):
                wait(sp, s_xl[0], n.at(1))
                if n.reg is not None:
                    settle(sp, s_sp)
                sp.dma_start(x0[:], x_tiles[:, bass.ds(n.at(NT), NT), :]).then_inc(s_x, 16)

            def load_raw(i):
                if i >= 2:
                    wait(sp, s_lo, i - 1)
                dst = raw[i % 2]
                if i in (0, E + 1):
                    sp.dma_start(dst.rearrange("p (k n) -> p k n", k=NK),
                                 (wqk0, wqk1)[i // E].rearrange("(k p) n -> p k n", p=P)).then_inc(s_raw[i % 2], 16)
                else:
                    d = dst.rearrange("p (m k f) -> p m k f", m=2, k=NK)
                    for m, w in enumerate((wg, wu)):
                        sp.dma_start(d[:, m], w[i - 1].rearrange("(k p) f -> p k f", p=P)).then_inc(s_raw[i % 2], 16)

            def store_parts(l, n):
                wait(sp, s_pl[l], n.at(1, 1))
                flat = parts[:].rearrange("p a s m n -> p a s (m n)")
                for a, (lo, hi) in enumerate(((0, 3), (3, 5), (5, 6))):
                    sp.dma_start(scr[l][0][lo:hi].rearrange("s (p m) n -> p s (m n)", p=P),
                                 flat[:, 0, 0:hi - lo]).then_inc(s_scr[l], 16)
                    sp.dma_start(scr[l][1][lo:hi].rearrange("s (p m) n -> p s (m n)", p=P),
                                 flat[:, 1, a:a + 1].broadcast_to([P, hi - lo, 2 * S])).then_inc(s_scr[l], 16)

            def load_stack(l, n, it, u):
                wait(sp, s_scr[l], (n if l == 0 else ahead(n)).at(96, 96))
                if n.reg is not None:
                    settle(sp, s_sp)
                wait(sp, s_sc, it.at(2 * H, 8 * (u - 1) - H))
                half = slice(8 * (u % 2), 8 * (u % 2) + 8)
                for src, dst in zip(scr[l], (q_stack, k_stack)):
                    sp.dma_start(dst[u % 2][:], src.rearrange("s (c h) n -> (s c) h n", h=H)[:, half, :])\
                      .then_inc(s_stack[u % 2], 16)

            def do(st):
                n, name, it = st.n, st.name, st.it
                if name == "split" and st.arg < E:
                    load_raw(st.arg + 2)
                if name in ("l0", "l1"):
                    store_parts(int(name[1]), n)
                if name == "l1":
                    for u in (0, 1) if st.kind == "final" else (2, 3):
                        load_stack(1, n, it, u)
                if name == "l0":
                    for u in (2, 3) if st.kind == "first" and n.off == 0 else (0, 1):
                        load_stack(0, n, n, u)
                if name == "l1" and st.kind == "final":
                    sp.wait_ge(s_acc, NT * ACC_STEPS * B)
                    sp.wait_ge(s_yw, 16 * B)
                    sp.wait_ge(s_x2w, 16 * B)
                    done = NT * (B - 1)
                    sp.dma_start(y_all[:, 0:done, :], y_tiles[:, 0:done, :]).then_inc(s_fin, 16)
                    sp.dma_start(x_all[:, 0:done, :], x2_tiles[:, 0:done, :]).then_inc(s_fin, 16)
                if name == "quant" and st.arg < B - 1:
                    t = NT * st.arg
                    sp.wait_ge(s_qo, st.arg + 1)
                    sp.dma_start(out_tiles[:, t:t + NT, :], y_all[:, t:t + NT, :]).then_inc(s_out, 16)
                if name == "w2" and st.arg == NT - 1 and st.kind != "final":
                    wait(sp, s_y, ahead(n).at(NT, NT))
                    if n.reg is not None:
                        settle(sp, s_sp)
                    sp.dma_start(y_tiles[:, bass.ds(n.at(NT), NT), :], y_sb).then_inc(s_yw, 16)
                if name == "op1" and st.arg == NT - 1:
                    wait(sp, s_x2, ahead(n).at(NT, NT))
                    if st.kind == "final":
                        sp.dma_start(out_tiles[:, NT * (B - 1):NT * B, :], x2_sb).then_inc(s_out, 16)
                        return
                    if n.reg is not None:
                        settle(sp, s_sp)
                    sp.dma_start(x2_tiles[:, bass.ds(n.at(NT), NT), :], x2_sb).then_inc(s_x2w, 16)

            load_x(Index(None, 0))
            load_raw(0)
            load_raw(1)
            for st in stages("first", Index(None, 0), {}):
                if st.name == "ln0a" and st.n.off == 1:
                    load_x(st.n)
                do(st)
            for counts, batch in ((s_yw, 16), (s_x2w, 16), (s_scr[1], 96)):
                sp.sem_inc(counts, batch)
            with sp.Fori(0, STEADY) as j:
                it = Index(j, 1)
                load_x(it.plus(1))
                for st in stages("steady", it, {}):
                    do(st)
            for st in stages("last", Index(None, B - 1), {}):
                do(st)
            for st in stages("final", Index(None, B), {}):
                do(st)
            sp.wait_ge(s_out, 16 * B)
            sp.wait_ge(s_yw, 16 * B)
            sp.wait_ge(s_x2w, 16 * B)
            sp.wait_ge(s_scr[0], 96 * B)
            sp.wait_ge(s_scr[1], 96 * (B + 1))

        @block.gpsimd
        def _(pool):
            pool.memset(ident[:], 0.0).then_inc(s_pool, 1)
            pool.wait_ge(s_pool, 1)
            pool.affine_select(out=ident[:], in_=ident[:], compare_op=ALU.not_equal, fill=1.0, base=0,
                               pattern=[[-1, P]], channel_multiplier=1).then_inc(s_pool, 1)
            pool.memset(before[:], 1.0).then_inc(s_pool, 1)
            pool.wait_ge(s_pool, 3)
            pool.affine_select(out=before[:], in_=before[:], compare_op=ALU.is_gt, fill=0.0, base=0,
                               pattern=[[1, E], [-1, E]], channel_multiplier=0).then_inc(s_pool, 1)
            pool.memset(bias1[:], 0.0).then_inc(s_pool, 1)
            pool.wait_ge(s_pool, 5)
            pool.affine_select(out=bias1[:, P:S], in_=bias1[:, P:S], compare_op=ALU.is_ge, fill=MASKED, base=0,
                               pattern=[[-1, P]], channel_multiplier=1).then_inc(s_pool, 1)
            pool.iota(rel_i, pattern=[[1, S]], base=-P, channel_multiplier=-1).then_inc(s_pool, 1)
            pool.memset(minus_half[:], -0.5).then_inc(s_pool, 1)
            pool.memset(pt[:, 0], CLAMP).then_inc(s_pool, 1)
            pool.wait_ge(s_pool, POOL_PT)
            for t in range(NF * 2):
                pool.dma_start(wd_sb[:, 2 * t:2 * t + 2], wd[2 * t:2 * t + 2].rearrange("e (k p) d -> p e k d", p=P))\
                    .then_inc(s_wd, 16)
            for l, w in enumerate((wo0, wo1)):
                for r in range(2):
                    for j in range(G4):
                        row = PAD * j + C * r
                        pool.dma_start(wo_sb[l][row:row + C, :, :],
                                       w.rearrange("(g r j c) d -> r j c g d", r=2, j=G4, c=C)[r, j]).then_inc(s_wo, 16)
            pool.dma_start(w1_raw.rearrange("p (k n) -> p k n", k=NK),
                           w1t.rearrange("(k p) n -> p k n", p=P)).then_inc(s_w1, 16)
            pool.dma_start(w2_raw.rearrange("p (a n) -> p a n", a=NH),
                           w2t.rearrange("(a p) n -> p a n", p=P)).then_inc(s_w1, 16)

            def do(st):
                n, name = st.n, st.name
                if name in ("ln0a", "ln1a"):
                    l = int(name[2])
                    src = (x0, acc)[l]
                    wait(pool, s_st[l], n.at(5, 5))
                    pool.tensor_tensor(rstd[l][:], var[l][:], minus_half[:], ALU.pow).then_inc(s_rstd[l], 1)
                    if st.kind == "first":
                        pool.wait_ge(s_c, 16 * NC)
                    if l == 0:
                        wait(pool, s_x, n.at(16, 16))
                        wait(pool, s_acc, n.at(NT * ACC_STEPS, NT - NT * ACC_STEPS))
                    else:
                        wait(pool, s_x2, ahead(n).at(NT))
                    for t in range(NT):
                        pool.tensor_tensor(xb[l][:, t], src[:, t], ob[l][:], ALU.add).then_inc(s_xb[l], 1)
                if name == "xe":
                    wait(pool, s_xl[0], n.at(1, 1))
                    wait(pool, s_acc, n.at(NT * ACC_STEPS, -NT))
                    if st.kind == "steady":
                        settle(pool, s_gps)
                    pool.tensor_copy(xe_hi[:].bitcast(I32), xt_hi[:].bitcast(I32)).then_inc(s_xe, 1)
                    pool.tensor_copy(xe_lo[:].bitcast(I32), xt_lo[:].bitcast(I32)).then_inc(s_xe, 1)
                if name == "w1":
                    a = 2 * st.arg
                    wait(pool, s_h1, n.at(2 * NH, 2 * a + 4))
                    pool.tensor_tensor(h1_parts[:, 1, a:a + 2], hid1[:, a % 4:a % 4 + 2], h1_parts[:, 0, a:a + 2],
                                       ALU.subtract).then_inc(s_h1l, 1)
                if name == "qmax":
                    pool.wait_ge(s_q, 1)
                    pool.partition_all_reduce(yred[:, 1:2], yred[:, 0:1], P, R_MAX).then_inc(s_qp, 1)
                if name == "tern":
                    i = st.arg
                    pool.wait_ge(s_t, TERN * i + 1)
                    pool.partition_all_reduce(t_amax[:, i:i + 1], t_max[:, i:i + 1], P, R_MAX).then_inc(s_tp, 1)
                    pool.wait_ge(s_t, TERN * i + 7)
                    pool.partition_all_reduce(t_tot[:, i], t_sum[:, i], P, R_ADD).then_inc(s_tp, 1)
                    if i == 1:
                        pool.wait_ge(s_lo, 2 + E)
                        pool.wait_ge(s_hi, 2 + E)
                        pool.memset(v_sb[1][:], 0.0).then_inc(s_v1z, 1)

            run_passes(pool, do, lambda: pool.sem_inc(s_h1l, NH // 2), {})

        @block.scalar
        def _(act):
            small = [(bqk[0][:], bqk0), (vb[0][:], vb0.partition_broadcast(P)), (half_t[:], temp.partition_broadcast(P)),
                     (slope_sb[:], slopes.partition_broadcast(P)), (ob[0][:], ob0.partition_broadcast(P)),
                     (bqk[1][:], bqk1), (vb[1][:], vb1.partition_broadcast(P)), (ob[1][:], ob1.partition_broadcast(P)),
                     (b1_sb[:], b1c), (b2_sb[:], b2.partition_broadcast(P)),
                     (wv_sb[1][:], wv1.rearrange("(k p) n -> p k n", p=P))]
            act.dma_start(wv_sb[0][:], wv0.rearrange("(k p) n -> p k n", p=P)).then_inc(s_wv0, 16)
            for dst, src in small:
                act.dma_start(dst, src).then_inc(s_c, 16)
            act.wait_ge(s_c, 16 * len(small))
            assert NC == len(small)

            def do(st):
                n, name, b = st.n, st.name, st.bank
                g = gen_ps[b] if b is not None else None
                if name == "split":
                    i = st.arg
                    act.wait_ge(s_raw[i % 2], 16 * sum(1 if a in (0, E + 1) else 2 for a in range(i % 2, i + 1, 2)))
                    hi = qk_hi[i // E][:].rearrange("p k n -> p (k n)") if i in (0, E + 1) else \
                        gu_hi[:, i - 1].rearrange("p m k f -> p (m k f)")
                    act.activation(hi, raw[i % 2], ACT.Copy, scale=WSCALE).then_inc(s_hi, 1)
                if name in ("tr0", "tr1"):
                    l = int(name[2])
                    wait(act, full[b], st.filled)
                    wait(act, s_xe, n.at(2) if l == 0 else n.at(2, 4 if st.kind != "final" else 2))
                    act.activation(xt[:].rearrange("p k s -> p (k s)"), g[:, :], ACT.Copy).then_inc(s_xh[l], 1)
                    act.activation(xt_hi[:].rearrange("p k s -> p (k s)"), g[:, :], ACT.Copy).then_inc(s_xh[l], 1)
                if name in ("q0", "k0", "q1", "k1"):
                    l, a = int(name[1]), "qk".index(name[0])
                    if n.reg is None and n.off == 0 and l == 0 and a == 0:
                        act.wait_ge(s_set, SET_BQ)
                    if a == 0:
                        if l == 0:
                            wait(act, s_scr[0], n.at(96))
                            wait(act, s_scr[1], n.at(96) if n.reg is not None or n.off > 1 else 0)
                        else:
                            wait(act, s_scr[1], ahead(n).at(96))
                            wait(act, s_scr[0], n.at(96, 192) if not (n.reg is None and n.off == B - 1) else 96 * B)
                    wait(act, full[b], st.filled)
                    scale = (float(C) ** -0.5 if a == 0 else 1.0) / WSCALE
                    for m in range(2):
                        bias = bqk[l][:, 2 * a + m:2 * a + m + 1]
                        act.activation(rest[:, a, m], g[:, S * m:S * m + S], ACT.Identity, bias=bias, scale=scale)\
                           .then_inc(s_ph[l], 1)
                        act.activation(parts[:, a, 0, m], g[:, S * m:S * m + S], ACT.Identity, bias=bias, scale=scale)\
                           .then_inc(s_ph[l], 1)
                if name in ("m0", "m1"):
                    l = int(name[1])
                    wait(act, s_pr[l], n.at(1, 1))
                    act.activation(parts[:, :, 1], rest[:], ACT.Copy).then_inc(s_pm[l], 1)
                if name == "v0":
                    t = st.arg
                    if t == 0 and n.reg is None and n.off == 0:
                        act.wait_ge(s_set, SET_HALF)
                    wait(act, full[b], st.filled)
                    if t == 0:
                        wait(act, s_rt, n.at(RT))
                    act.activation(r_tanh[:, t], g[:, D:D + E], ACT.Tanh, scale=half_t[:, 0:1]).then_inc(s_th, 1)
                if name == "rt2":
                    wait(act, s_rt, n.at(RT, 5))
                    act.activation(r_e1[:], r_dist[:], ACT.Exp, scale=-1.0 / 0.1).then_inc(s_re, 1)
                    act.activation(r_e2[:], r_dist[:], ACT.Exp, scale=-1.0 / 0.3).then_inc(s_re, 1)
                if name == "gate":
                    wait(act, full[b], st.filled)
                    if st.arg == 0:
                        wait(act, s_acc, n.at(NT * ACC_STEPS))
                    else:
                        wait(act, s_ga, n.at(E, st.arg))
                    act.activation(tanh_sb[:], g[:, :], ACT.Tanh, scale=0.5 / WSCALE).then_inc(s_tg, 1)
                if name == "w1":
                    if st.arg == 0:
                        wait(act, s_y, ahead(n).at(NT))
                    wait(act, s_h1l, ahead(n).at(NH // 2, st.arg - 1))
                    wait(act, full[b], st.filled)
                    for j in range(2):
                        a = 2 * st.arg + j
                        for dst in (hid1[:, a % 4], h1_parts[:, 0, a]):
                            act.activation(dst, g[:, S * j:S * j + S], ACT.Gelu,
                                           bias=b1_sb[:, a:a + 1], scale=alpha[:, 0:1]).then_inc(s_h1, 1)
                if name == "score":
                    s = st.arg
                    k = s % PROBS
                    wait(act, s_mx, heads_before(st, 1))
                    for lo, hi, j in ((0, S, 0), (S, S + P, 1)):
                        last = act.activation(probs[:, k, lo:hi], probs[:, k, lo:hi], ACT.Exp, scale=-1.0,
                                              bias=nmax[:, k, j:j + 1], accum_out=esum[:, k, j:j + 1])
                    last.then_inc(s_ex, 1)
                if name == "turn":
                    s = st.arg
                    wait(act, s_tn, heads_before(st, 1))
                    wait(act, s_pv, st.it.at(2 * H // G4, s // G4 - H // G4 - 1))
                    slot = 1 + 3 * (s % TURNED)
                    act.activation(pt[:, slot:slot + 3].rearrange("p t q -> p (t q)"), turn_ps[s % 2][:, 0:3 * P],
                                   ACT.Copy).then_inc(s_ev, 1)
                if name == "value" and st.arg % 2 == 1:
                    l = set_block(st)
                    g = st.arg // 2 % NK
                    wait(act, s_pv, sets_before(st, 1))
                    if g == 0:
                        nb = batch_of(st, l)
                        wait(act, *((s_acc, nb.at(NT * ACC_STEPS)) if l == 0 else (s_x2, ahead(nb).at(NT))))
                    act.activation(at[l][:, g], value_ps[:, 0:S], ACT.Copy).then_inc(s_at, 1)

                if name == "quant":
                    if st.arg == 0:
                        act.wait_ge(s_q, 3)
                        act.wait_ge(s_fin, 32)
                    y = y_all[:, NT * st.arg:NT * st.arg + NT, :] if st.arg < B - 1 else y_sb
                    act.activation(y, y, ACT.Copy, scale=yred[:, 3:4]).then_inc(s_qa, 1)

            def before_block1():
                act.wait_ge(s_t, 2 * TERN)
                act.wait_ge(s_v1z, 1)

            run_passes(act, do, before_block1, LAG["scalar"])

        @block.tensor
        def _(pe):
            def take(st):
                if st.before is not None:
                    wait(pe, *read_by(st.before))
                elif st.kind != "first":
                    wait(pe, s_acc, st.it.at(NT * ACC_STEPS))
                    wait(pe, s_x2, ahead(batch_of(st, 1)).at(NT))
                return gen_ps[st.bank]

            def do(st):
                n, name = st.n, st.name
                first = n.reg is None and n.off == 0
                if name in ("tr0", "tr1"):
                    l = int(name[2])
                    src = (x0, acc)[l]
                    if first and l == 0:
                        pe.wait_ge(s_pool, POOL_IDENT)
                    wait(pe, s_xn[l], n.at(NT, NT))
                    g = take(st)
                    for t in range(NT):
                        for k in range(NK):
                            last = pe.transpose(g[:, S * k + P * t:S * k + P * t + P], src[:, t, P * k:P * k + P], ident[:])
                    last.then_inc(full[st.bank], 1)
                if name in ("q0", "k0", "q1", "k1"):
                    l, a = int(name[1]), "qk".index(name[0])
                    if first and l == 0 and a == 0:
                        pe.wait_ge(s_lo, 1)
                    wait(pe, s_xl[l], n.at(1, 1))
                    g = take(st)
                    for m in range(2):
                        cols = slice(D * a + P * m, D * a + P * m + P)
                        terms = [(w, xx, k) for w, xx in ((qk_hi, xt_hi), (qk_hi, xt_lo), (qk_lo, xt_hi)) for k in range(NK)]
                        for i, (w, xx, k) in enumerate(terms):
                            last = pe.matmul(g[:, S * m:S * m + S], w[l][:, k, cols], xx[:, k, :],
                                             start=(i == 0), stop=(i == len(terms) - 1))
                    last.then_inc(full[st.bank], 1)
                if name in ("v0", "v1"):
                    l = int(name[1])
                    if first and l == 0 and st.arg == 0:
                        pe.wait_ge(s_wv0, 16)
                    wait(pe, s_xl[l], n.at(1, 1))
                    g = take(st)
                    for t in ([st.arg] if l == 0 else range(NT)):
                        o = g[:, 0:D + E] if l == 0 else g[:, D * t:D * t + D]
                        for k in range(NK):
                            last = pe.matmul(o, xt[:, k, P * t:P * t + P], wv_sb[l][:, k, :],
                                             start=(k == 0), stop=(k == NK - 1))
                    last.then_inc(full[st.bank], 1)
                if name in ("gate", "up"):
                    m = ("gate", "up").index(name)
                    if st.arg == 0 and m == 0:
                        wait(pe, s_xe, n.at(2, 2))
                    if first and m == 0:
                        pe.wait_ge(s_lo, 2 + st.arg)
                    g = take(st)
                    for f in range(NF):
                        cols = slice(P * f, P * f + P)
                        terms = [(w, xx, k) for w, xx in ((gu_hi, xe_hi), (gu_hi, xe_lo), (gu_lo, xe_hi)) for k in range(NK)]
                        for i, (w, xx, k) in enumerate(terms):
                            last = pe.matmul(g[:, S * f:S * f + S], w[:, st.arg, m, k, cols], xx[:, k, :],
                                             start=(i == 0), stop=(i == len(terms) - 1))
                    last.then_inc(full[st.bank], 1)
                if name == "down":
                    if first and st.arg == 0:
                        pe.wait_ge(s_wd, 16 * 4)
                    wait(pe, s_h0, n.at(E, st.arg + 1))
                    g = take(st)
                    for t in range(NT):
                        for f in range(NF):
                            last = pe.matmul(g[:, D * t:D * t + D], hid0[:, st.arg % 2, f, P * t:P * t + P],
                                             wd_sb[:, st.arg, f, :], start=(f == 0), stop=(f == NF - 1))
                    last.then_inc(full[st.bank], 1)
                if name == "w1":
                    if st.arg == 0:
                        wait(pe, s_xl[1], n.at(1, 1))
                    g = take(st)
                    for j in range(2):
                        a = 2 * st.arg + j
                        terms = [(xx, k) for xx in (xt_hi, xt_lo) for k in range(NK)]
                        for i, (xx, k) in enumerate(terms):
                            last = pe.matmul(g[:, S * j:S * j + S], t1_sb[:, k, P * a:P * a + P], xx[:, k, :],
                                             start=(i == 0), stop=(i == len(terms) - 1))
                    last.then_inc(full[st.bank], 1)
                if name == "w2":
                    if st.arg == 0:
                        wait(pe, s_h1l, ahead(n).at(NH // 2, NH // 2))
                    g = take(st)
                    terms = [(i, a) for i in range(2) for a in range(NH)]
                    for i, a in terms:
                        last = pe.matmul(g[:, 0:D], h1_parts[:, i, a, P * st.arg:P * st.arg + P], t2_sb[:, a, :],
                                         start=((i, a) == terms[0]), stop=((i, a) == terms[-1]))
                    last.then_inc(full[st.bank], 1)
                if name in ("op0", "op1"):
                    l = int(name[2])
                    if first and l == 0:
                        pe.wait_ge(s_wo, 16 * 4 * G4)
                    wait(pe, s_at, at_of_block(st, l))
                    g = take(st)
                    for t in (range(NT) if l == 0 else [st.arg]):
                        o = g[:, D * t:D * t + D] if l == 0 else g[:, 0:D]
                        for q in range(NK):
                            last = pe.matmul(o, at[l][:, q, P * t:P * t + P], wo_sb[l][:, q, :],
                                             start=(q == 0), stop=(q == NK - 1))
                    last.then_inc(full[st.bank], 1)
                if name == "score":
                    s = st.arg
                    u, hh = s // 8, s % 8
                    if hh == 0:
                        wait(pe, s_stack[u % 2], st.it.at(64, 32 * (u // 2)))
                    wait(pe, s_mx, heads_before(st, -1))
                    g, q, k = score_ps[s % 2], q_stack[u % 2], k_stack[u % 2]
                    pe.matmul(g[:, 0:S], q[:, hh, P:S], k[:, hh, :], start=True, stop=True)
                    pe.matmul(g[:, S:S + P], q[:, hh, 0:P], k[:, hh, 0:P], start=True, stop=True).then_inc(s_sc, 1)
                if name == "turn":
                    s = st.arg
                    wait(pe, s_nm, heads_before(st, 1))
                    wait(pe, s_ev, heads_before(st, -1))
                    g, p = turn_ps[s % 2], probs[:, s % PROBS]
                    pe.transpose(g[:, 0:P], p[:, P:S], ident[:])
                    pe.transpose(g[:, P:2 * P], p[:, S:S + P], ident[:])
                    pe.transpose(g[:, 2 * P:3 * P], p[:, 0:P], ident[:]).then_inc(s_tn, 1)
                if name == "value":
                    l = set_block(st)
                    nb = batch_of(st, l)
                    b, r = st.arg % G4, st.arg % 2
                    if b == 0:
                        wait(pe, s_v[l], (nb if l == 0 else ahead(nb)).at(NT, NT))
                        if st.kind == "first":
                            pe.wait_ge(s_pool, POOL_PT)
                    wait(pe, s_ev, st.it.at(2 * H, G4 * (st.arg + 1) - H))
                    if r == 0:
                        wait(pe, s_at, at_before(st))
                    for t in range(NT):
                        for j in range(G4):
                            slot = 1 + 3 * ((G4 * st.arg + j) % TURNED)
                            first_col = VB * b + PAD * j - C * r
                            v = v_sb[l][:, t].rearrange("p b c -> p (b c)")[:, first_col:first_col + PAD]
                            lo, seen = (0, pt[:, slot + 1:slot + 3]) if t == 0 else \
                                (0, pt[:, 0:slot + 1:slot]) if l == 0 else (P, pt[:, slot])
                            last = pe.matmul(value_ps[PAD * j:PAD * j + PAD, lo:S], v, seen,
                                             start=(t == 0 and r == 0), stop=(t == 1 and r == 1))
                    last.then_inc(s_pv, 1)

            def before_block1():
                pe.wait_ge(s_lo, 2 + E)
                pe.wait_ge(s_t, 2 * TERN)
                pe.wait_ge(s_c, 16 * NC)

            run_passes(pe, do, before_block1, {})

        @block.vector
        def _(dve):
            def do(st):
                n, name, b = st.n, st.name, st.bank
                g = gen_ps[b] if b is not None else None
                if name == "setup" and st.arg == 0:
                    dve.memset(v_sb[0][:], 0.0).then_inc(s_set, 1)
                if name == "setup" and st.arg == 2:
                    dve.wait_ge(s_c, 16 * NC)
                    dve.reciprocal(half_t[:], half_t[:]).then_inc(s_set, 1)
                    dve.wait_ge(s_set, 2)
                    dve.tensor_scalar(half_t[:], half_t[:], 0.5, None, ALU.mult).then_inc(s_set, 1)
                    dve.tensor_scalar(bqk[0][:, 0:2], bqk[0][:, 0:2], float(C) ** -0.5, None, ALU.mult)\
                       .then_inc(s_set, 1)
                    dve.tensor_scalar(bqk[1][:, 0:2], bqk[1][:, 0:2], float(C) ** -0.5, None, ALU.mult)\
                       .then_inc(s_set, 1)
                if name == "setup" and st.arg == 1:
                    dve.wait_ge(s_pool, POOL_REL)
                    dve.tensor_copy(rel, rel_i).then_inc(s_set, 1)
                    dve.wait_ge(s_set, SET_REL)
                    for h in range(H):
                        dve.scalar_tensor_tensor(bias0[:, h], rel, slope_sb[:, h:h + 1], bias1[:], ALU.mult, ALU.add)\
                           .then_inc(s_set, 1)
                if name == "split":
                    i = st.arg
                    dve.wait_ge(s_hi, i + 1)
                    qk = i in (0, E + 1)
                    hi, lo = (qk_hi[i // E][:], qk_lo[i // E][:]) if qk else (gu_hi[:, i - 1], gu_lo[:, i - 1])
                    flat = "p k n -> p (k n)" if qk else "p m k f -> p (m k f)"
                    dve.scalar_tensor_tensor(lo.rearrange(flat), raw[i % 2], WSCALE, hi.rearrange(flat),
                                             ALU.mult, ALU.subtract)\
                       .then_inc(s_lo, 1)
                if name == "tern":
                    i, t0 = st.arg, TERN * st.arg
                    w = (w1_raw, w2_raw)[i]
                    t = (t1_sb[:].rearrange("p k n -> p (k n)"), t2_hid[:, 0].bitcast(F16))[i]
                    dve.wait_ge(s_w1, 32)
                    dve.tensor_reduce(t_max[:, i:i + 1], w, AX.X, ALU.max, apply_absolute_value=True).then_inc(s_t, 1)
                    dve.wait_ge(s_tp, 2 * i + 1)
                    dve.tensor_scalar(t_delta[:, i, 0:1], t_amax[:, i:i + 1], 0.05, None, ALU.mult).then_inc(s_t, 1)
                    dve.tensor_scalar(t_delta[:, i, 1:2], t_amax[:, i:i + 1], -0.05, None, ALU.mult).then_inc(s_t, 1)
                    dve.wait_ge(s_t, t0 + 3)
                    dve.tensor_scalar(t, w, t_delta[:, i, 1:2], None, ALU.is_lt).then_inc(s_t, 1)
                    dve.wait_ge(s_t, t0 + 4)
                    dve.scalar_tensor_tensor(t, w, t_delta[:, i, 0:1], t, ALU.is_gt, ALU.subtract).then_inc(s_t, 1)
                    dve.wait_ge(s_t, t0 + 5)
                    dve.tensor_tensor_reduce(out=w, in0=w, in1=t, scale=1.0, scalar=0.0, op0=ALU.mult, op1=ALU.add,
                                             accum_out=t_sum[:, i, 0:1]).then_inc(s_t, 1)
                    dve.wait_ge(s_t, t0 + 6)
                    dve.tensor_tensor_reduce(out=w, in0=t, in1=t, scale=1.0, scalar=0.0, op0=ALU.mult, op1=ALU.add,
                                             accum_out=t_sum[:, i, 1:2]).then_inc(s_t, 1)
                    dve.wait_ge(s_tp, 2 * i + 2)
                    dve.tensor_scalar(t_tot[:, i, 1:2], t_tot[:, i, 1:2], 1.0, None, ALU.max).then_inc(s_t, 1)
                    dve.wait_ge(s_t, t0 + 8)
                    dve.reciprocal(t_tot[:, i, 1:2], t_tot[:, i, 1:2]).then_inc(s_t, 1)
                    dve.wait_ge(s_t, t0 + 9)
                    dve.tensor_tensor(alpha[:, i:i + 1], t_tot[:, i, 0:1], t_tot[:, i, 1:2], ALU.mult).then_inc(s_t, 1)
                if name in ("ln0a", "ln1a"):
                    l = int(name[2])
                    if l == 0:
                        wait(dve, s_x, n.at(16, 16))
                    else:
                        wait(dve, s_acc, n.at(NT * ACC_STEPS, NT * ACC_STEPS))
                    src = (x0, acc)[l]
                    for t in range(NT):
                        dve.bn_stats(stats[:, t], src[:, t]).then_inc(s_st[l], 1)
                    wait(dve, s_st[l], n.at(5, 2))
                    if st.kind == "steady":
                        settle(dve, s_dve)
                    for t in range(NT):
                        dve.bn_aggr(mv[l][:, t], stats[:, t]).then_inc(s_st[l], 1)
                    wait(dve, s_st[l], n.at(5, 4))
                    dve.tensor_scalar(var[l][:], mv[l][:, :, 1], EPS, None, ALU.add).then_inc(s_st[l], 1)
                if name in ("ln0b", "ln1b"):
                    l = int(name[2])
                    src = (x0, acc)[l]
                    wait(dve, s_rstd[l], n.at(1, 1))
                    wait(dve, s_xb[l], n.at(NT, NT))
                    for t in range(NT):
                        dve.tensor_scalar(src[:, t], src[:, t], mv[l][:, t, 0:1], rstd[l][:, t:t + 1],
                                          ALU.subtract, ALU.mult).then_inc(s_xn[l], 1)
                if name in ("tr0", "tr1"):
                    l = int(name[2])
                    wait(dve, s_xh[l], n.at(2, 2))
                    dve.tensor_tensor(xt_lo[:].rearrange("p k s -> p (k s)"), g[:, :],
                                      xt_hi[:].rearrange("p k s -> p (k s)"), ALU.subtract).then_inc(s_xl[l], 1)
                if name in ("r0", "r1"):
                    l = int(name[1])
                    wait(dve, s_ph[l], n.at(8, 8))
                    dve.tensor_tensor(rest[:], rest[:], parts[:, :, 0], ALU.subtract).then_inc(s_pr[l], 1)
                if name in ("l0", "l1"):
                    l = int(name[1])
                    wait(dve, s_pm[l], n.at(1, 1))
                    dve.tensor_tensor(parts[:, :, 2], rest[:], parts[:, :, 1], ALU.subtract).then_inc(s_pl[l], 1)
                if name in ("v0", "v1"):
                    l = int(name[1])
                    for t in ([st.arg] if l == 0 else range(NT)):
                        if l == 0:
                            wait(dve, s_th, n.at(NT, t + 1))
                        elif t == 0:
                            wait(dve, full[b], st.filled)
                        if t == 0:
                            if l == 0:
                                wait(dve, s_pv, n.at(8, -8) if n.reg is not None or n.off > 1 else 4 * n.off)
                            else:
                                wait(dve, s_pv, n.at(8, 4))
                        o = g[:, 0:D] if l == 0 else g[:, D * t:D * t + D]
                        four = dict(j=G4, c=C)
                        dve.tensor_tensor(v_sb[l][:, t, :, 0:P].rearrange("p b (j x) -> p b j x", x=PAD)[:, :, :, 0:C],
                                          o.rearrange("p (b j c) -> p b j c", **four),
                                          vb[l][:].rearrange("p (b j c) -> p b j c", **four), ALU.add).then_inc(s_v[l], 1)
                if name == "rt1":
                    def zone(ins):
                        ins.then_inc(s_rt, 1)
                    wait(dve, s_th, n.at(NT, NT))
                    zone(dve.tensor_scalar(r_in[:], r_tanh[:], 0.5, 0.5, ALU.mult, ALU.add))
                    wait(dve, s_rt, n.at(RT, 1))
                    zone(dve.tensor_scalar(r_zone[:], r_in[:], float(GOLD_LO), None, ALU.is_ge))
                    zone(dve.tensor_scalar(r_d[:], r_in[:], float(GOLD_C), None, ALU.subtract))
                    wait(dve, s_rt, n.at(RT, 3))
                    zone(dve.scalar_tensor_tensor(r_zone2[:], r_in[:], GOLD_HI, r_zone[:], ALU.is_le, ALU.mult))
                    wait(dve, s_re, n.at(2))
                    zone(dve.scalar_tensor_tensor(r_dist[:], r_d[:], -1.0, r_d[:], ALU.mult, ALU.max))
                if name == "rt2":
                    per_token = [P, NT, E]
                    pairs = [P, NT, E, E]

                    def route(k, ins):
                        ins.then_inc(s_rt, 1)

                    def after(k):
                        wait(dve, s_rt, n.at(RT, 5 + k))
                    if st.kind == "first":
                        dve.wait_ge(s_pool, POOL_BEFORE)
                    wait(dve, s_re, n.at(2, 2))
                    route(1, dve.tensor_tensor(r_gt[:], r_e2[:].unsqueeze(2).broadcast_to(pairs),
                                               r_e2[:].unsqueeze(3).broadcast_to(pairs), ALU.is_gt))
                    route(2, dve.tensor_tensor(r_eq[:], r_e2[:].unsqueeze(2).broadcast_to(pairs),
                                               r_e2[:].unsqueeze(3).broadcast_to(pairs), ALU.is_equal))
                    route(3, dve.tensor_tensor(r_w[:], r_e1[:], r_zone2[:], ALU.mult))
                    after(2)
                    route(4, dve.tensor_tensor(r_eq[:], r_eq[:], before[:].unsqueeze(1).broadcast_to(pairs), ALU.mult))
                    after(3)
                    route(5, dve.tensor_reduce(r_s[:, 0], r_w[:], AX.X, ALU.add))
                    after(4)
                    route(6, dve.tensor_tensor(r_gt[:], r_gt[:], r_eq[:], ALU.add))
                    after(5)
                    route(7, dve.tensor_scalar(r_s[:, 1], r_s[:, 0], 1e-8, None, ALU.is_lt))
                    after(6)
                    route(8, dve.tensor_reduce(r_rank[:].unsqueeze(3), r_gt[:], AX.X, ALU.add))
                    after(7)
                    route(9, dve.tensor_scalar(r_s[:, 2], r_s[:, 1], -1.0, 1.0, ALU.mult, ALU.add))
                    after(8)
                    route(10, dve.scalar_tensor_tensor(r_fb[:], r_rank[:], 2.0, r_e2[:], ALU.is_lt, ALU.mult))
                    after(10)
                    route(11, dve.tensor_reduce(r_s[:, 3], r_fb[:], AX.X, ALU.add))
                    route(12, dve.tensor_tensor(r_w[:], r_w[:], r_s[:, 2].broadcast_to(per_token), ALU.mult))
                    after(11)
                    route(13, dve.tensor_scalar(r_s[:, 3], r_s[:, 3], 1e-8, None, ALU.max))
                    after(13)
                    route(14, dve.reciprocal(r_s[:, 4], r_s[:, 3]))
                    after(14)
                    route(15, dve.tensor_tensor(r_fb[:], r_fb[:], r_s[:, 4].broadcast_to(per_token), ALU.mult))
                    after(15)
                    route(16, dve.tensor_tensor(r_fb[:], r_fb[:], r_s[:, 1].broadcast_to(per_token), ALU.mult))
                    after(16)
                    route(17, dve.tensor_tensor(r_w[:], r_w[:], r_fb[:], ALU.add))
                    after(17)
                    route(18, dve.tensor_reduce(r_s[:, 5], r_w[:], AX.X, ALU.add))
                    after(18)
                    route(19, dve.tensor_scalar(r_s[:, 5], r_s[:, 5], 1e-8, None, ALU.max))
                    after(19)
                    route(20, dve.reciprocal(r_s[:, 0], r_s[:, 5]))
                    after(20)
                    dve.tensor_tensor(w8[:], r_w[:], r_s[:, 0].broadcast_to(per_token), ALU.mult).then_inc(s_w8, 1)
                if name == "gate":
                    wait(dve, s_tg, n.at(E, st.arg + 1))
                    dve.scalar_tensor_tensor(gated[:], tanh_sb[:], 1.0, g[:, :], ALU.add, ALU.mult).then_inc(s_ga, 1)
                if name == "up":
                    wait(dve, full[b], st.filled)
                    wait(dve, s_ga, n.at(E, st.arg + 1))
                    dve.scalar_tensor_tensor(hid0[:, st.arg % 2].rearrange("p f s -> p (f s)"), gated[:],
                                             0.5 / (WSCALE * WSCALE), g[:, :], ALU.mult, ALU.mult).then_inc(s_h0, 1)
                if name == "down":
                    e = st.arg
                    wait(dve, full[b], st.filled)
                    if st.place == 0:
                        wait(dve, s_w8, n.at(1, 1))
                        wait(dve, s_xb[0], n.at(NT, NT))
                    wait(dve, s_acc, n.at(NT * ACC_STEPS, NT * st.place))
                    for t in range(NT):
                        dve.scalar_tensor_tensor(acc[:, t], g[:, D * t:D * t + D], w8[:, t, e:e + 1],
                                                 (xb[0] if st.place == 0 else acc)[:, t], ALU.mult, ALU.add)\
                           .then_inc(s_acc, 1)
                if name == "op0":
                    wait(dve, full[b], st.filled)
                    wait(dve, s_acc, n.at(NT * ACC_STEPS, NT * st.place))
                    for t in range(NT):
                        dve.tensor_tensor(acc[:, t], g[:, D * t:D * t + D], acc[:, t], ALU.add).then_inc(s_acc, 1)
                if name == "w2":
                    t = st.arg
                    wait(dve, full[b], st.filled)
                    if t == 0:
                        wait(dve, s_yw, ahead(n).at(16))
                    dve.scalar_tensor_tensor(y_sb[:, t], g[:, 0:D], alpha[:, 1:2], b2_sb[:], ALU.mult, ALU.add)\
                       .then_inc(s_y, 1)
                    wait(dve, s_y, ahead(n).at(NT, t + 1))
                    dve.tensor_reduce(ymax[:, bass.ds(n.at(NT, t), 1)], y_sb[:, t], AX.X, ALU.max,
                                      apply_absolute_value=True).then_inc(s_ym, 1)
                if name == "op1":
                    t = st.arg
                    wait(dve, full[b], st.filled)
                    if t == 0:
                        wait(dve, s_xb[1], n.at(NT, NT))
                        wait(dve, s_x2w, ahead(n).at(16))
                    if st.kind == "final":
                        dve.wait_ge(s_qo, B)
                    rest_of_sum = y_sb if st.kind == "final" else xb[1]
                    dve.tensor_tensor(x2_sb[:, t], g[:, 0:D], rest_of_sum[:, t], ALU.add).then_inc(s_x2, 1)
                if name == "score":
                    s, l = st.arg, head_block(st)
                    k, g = s % PROBS, score_ps[s % 2]
                    wait(dve, s_sc, heads_before(st, 1))
                    wait(dve, s_tn, heads_before(st, 1 - PROBS))
                    if st.kind == "steady":
                        settle(dve, s_dve)
                    if st.kind == "first":
                        dve.wait_ge(s_set, SET_BIAS0)
                    bias = bias0[:, s % H] if l == 0 else bias1[:]
                    for lo, hi, blo, j in ((0, S, 0, 0), (S, S + P, P, 1)):
                        last = dve.tensor_tensor_reduce(out=probs[:, k, lo:hi], in0=g[:, lo:hi], in1=bias[:, blo:S],
                                                        scale=-1.0, scalar=BIG, op0=ALU.add, op1=ALU.min,
                                                        accum_out=nmax[:, k, j:j + 1])
                    last.then_inc(s_mx, 1)
                if name == "norm":
                    s, l = st.arg, head_block(st)
                    k = s % PROBS
                    wait(dve, s_ex, heads_before(st, 1))
                    dve.reciprocal(rsum[:, k], esum[:, k]).then_inc(s_rz, 1)
                    wait(dve, s_rz, heads_before(st, 1))
                    for lo, hi, j in ((0, S, 0), (S, S + P, 1)):
                        clamp = (CLAMP, ALU.mult, ALU.max) if l == 0 else (None, ALU.mult)
                        last = dve.tensor_scalar(probs[:, k, lo:hi], probs[:, k, lo:hi], rsum[:, k, j:j + 1], *clamp)
                    last.then_inc(s_nm, 1)

                if name == "qmax":
                    dve.wait_ge(s_ym, B * NT)
                    dve.tensor_reduce(yred[:, 0:1], ymax[:], AX.X, ALU.max).then_inc(s_q, 1)
                    dve.wait_ge(s_qp, 1)
                    dve.tensor_scalar(yred[:, 2:3], yred[:, 1:2], 1.0 / QMAX, 1e-8, ALU.mult, ALU.add).then_inc(s_q, 1)
                    dve.wait_ge(s_q, 2)
                    dve.reciprocal(yred[:, 3:4], yred[:, 2:3]).then_inc(s_q, 1)
                if name == "quant":
                    c = st.arg
                    y = y_all[:, NT * c:NT * c + NT, :] if c < B - 1 else y_sb
                    x = x_all[:, NT * c:NT * c + NT, :] if c < B - 1 else xb[1][:]
                    dve.wait_ge(s_qa, c + 1)
                    dve.tensor_scalar(y, y, QMAX, -QMAX, ALU.min, ALU.max).then_inc(s_q, 1)
                    dve.wait_ge(s_q, 4 + 2 * c)
                    dve.tensor_scalar(y, y, ROUND, ROUND, ALU.add, ALU.subtract).then_inc(s_q, 1)
                    dve.wait_ge(s_q, 5 + 2 * c)
                    dve.scalar_tensor_tensor(y, y, yred[:, 2:3], x, ALU.mult, ALU.add).then_inc(s_qo, 1)

            def before_block1():
                dve.wait_ge(s_v1z, 1)
                for counts in (s_v[1], s_y, s_x2):
                    dve.sem_inc(counts, NT)

            run_passes(dve, do, before_block1, LAG["vector"])


def kernel(L0_attn_qkv, L0_attn_in_proj, L0_attn_in_proj_bias, L0_attn_out_w, L0_attn_out_b, L0_attn_alibi_slopes,
           L0_ffn_Wg, L0_ffn_Wu, L0_ffn_Wd, L0_ffn_Wr, L0_ffn_temperature, L1_attn_Wq, L1_attn_bq, L1_attn_Wk,
           L1_attn_bk, L1_attn_Wv, L1_attn_bv, L1_attn_Wo, L1_attn_bo, L1_ffn_W1, L1_ffn_b1, L1_ffn_W2, L1_ffn_b2):
    import concourse.bacc as bacc
    from concourse.bass_utils import run_bass_kernel_spmd

    def by_channel(w):
        w = w.reshape(-1, H, C).transpose(0, 2, 1)
        return w.reshape(-1, P, 2).transpose(0, 2, 1).reshape(-1, H * C)

    def columns(q, k):
        return np.concatenate([by_channel(q.reshape(1, -1)), by_channel(k.reshape(1, -1))], 1).reshape(4, P).T

    proj, pb = np.asarray(L0_attn_in_proj), np.asarray(L0_attn_in_proj_bias)
    a = {k: np.asarray(v) for k, v in locals().items() if k.startswith("L")}
    heads = {k: a["L1_attn_W" + k].transpose(1, 0, 2).reshape(D, D) for k in "qkv"}
    arrays = {
        "x": a["L0_attn_qkv"],
        "wqk0": np.concatenate([by_channel(proj[0:D].T), by_channel(proj[D:2 * D].T)], 1),
        "bqk0": columns(pb[0:D], pb[D:2 * D]),
        "wv0": np.concatenate([proj[2 * D:].T, a["L0_ffn_Wr"]], 1),
        "vb0": pb[2 * D:],
        "wo0": a["L0_attn_out_w"].T,
        "ob0": a["L0_attn_out_b"],
        "slopes": a["L0_attn_alibi_slopes"],
        "wg": a["L0_ffn_Wg"],
        "wu": a["L0_ffn_Wu"],
        "wd": a["L0_ffn_Wd"],
        "temp": a["L0_ffn_temperature"],
        "wqk1": np.concatenate([by_channel(heads["q"]), by_channel(heads["k"])], 1),
        "bqk1": columns(a["L1_attn_bq"], a["L1_attn_bk"]),
        "wv1": heads["v"],
        "vb1": a["L1_attn_bv"].reshape(-1),
        "wo1": a["L1_attn_Wo"],
        "ob1": a["L1_attn_bo"],
        "w1t": a["L1_ffn_W1"].T,
        "b1c": a["L1_ffn_b1"].reshape(NH, P).T,
        "w2t": a["L1_ffn_W2"].T,
        "b2": a["L1_ffn_b2"],
    }
    arrays = {k: np.ascontiguousarray(v) for k, v in arrays.items()}
    nc = bacc.Bacc("TRN2", target_bir_lowering=False, num_devices=1)
    args = [nc.dram_tensor("in_" + k, v.shape, mybir.dt.from_np(v.dtype), kind="ExternalInput").ap() for k, v in arrays.items()]
    out = nc.dram_tensor("out_dram", (B, S, D), F32, kind="ExternalOutput").ap()
    two_blocks(nc, *args, out)
    r = run_bass_kernel_spmd(nc, [{"in_" + k: v for k, v in arrays.items()}], core_ids=[0])
    return r.results[0]["out_dram"]
```

```python
from contextlib import ExitStack

import numpy as np
import concourse.bass as bass
from concourse import mybir

F32 = mybir.dt.float32
F16 = mybir.dt.float16
BF16 = mybir.dt.bfloat16
I32 = mybir.dt.int32
ALU = mybir.AluOpType
ACT = mybir.ActivationFunctionType
AX = mybir.AxisListType
R_MAX = bass.bass_isa.ReduceOp.max
R_ADD = bass.bass_isa.ReduceOp.add

P = 128
B, S, D = 8, 256, 256
H, C = 16, 16
NT = S // P
NK = D // P
E, F = 8, 256
NF = F // P
HID = 1024
NH = HID // P
PAD = 32
G4 = P // PAD
VB = P + C
SPLITS = 6
KR = SPLITS * C
EPS = 1e-5
CLAMP = 1e-10
MASKED = -1e30
BIG = 3e38
WSCALE = 16.0
GOLD_C = 1.0 / np.e
GOLD_LO = 0.5 - np.log(4.0 / 3.0)
GOLD_HI = 0.5
QMAX = 7.0
ROUND = 1.5 * 2.0 ** 23

BANKED = {"tr0", "q0", "k0", "v0", "gate", "up", "down", "op0",
          "tr1", "w1", "q1", "k1", "v1", "w2", "op1"}
RING = 3

NORM_LAG, TURN_LAG, VALUE_LAG = 1, 3, 1
PROBS = 8
TURNED = 8

LAG = {"scalar": {"score": 4, "m1": 1, "up": 4, "q0": 1, "turn": 1, "up:1": 5, "value:1": 0, "turn:4": 0},
       "vector": {"gate": 1, "up": 1, "down": 2, "op0": 2, "w2": 8, "l1": 2, "qmax": 8, "r0": 1, "norm": 2,
                  "gate:3": 2, "gate:7": 2, "gate:6": 0, "score:0": 1, "norm:1": 4, "score:18": 2, "gate:5": 2,
                  "score:9": 2, "norm:9": 4, "up:0": 0, "score:3": 1}}


def with_heads(order, last):
    first = next(x for x in order if isinstance(x, int))
    out = []

    def head(s):
        if s <= last:
            out.append(("score", s, 0))
        if first <= s - NORM_LAG <= last:
            out.append(("norm", s - NORM_LAG, 0))
        t = s - TURN_LAG
        if first <= t <= last:
            out.append(("turn", t, 0))
        t -= VALUE_LAG
        if first <= t <= last and t % G4 == G4 - 1:
            out.append(("value", t // G4, 0))

    for item in order:
        if isinstance(item, int):
            head(item)
        else:
            out.append(item)
    return out


FIRST_ORDER = """
    setup:0 ln0a split:0 ln0b split:1 split:2 tr0 setup:2 split:3 q0 xe k0 setup:1 r0 split:4 split:5 v0:0 m0
    v0:1 rt1 l0 gate:0 up:0 rt2 gate:1 split:6 down:0 up:1 16 17 split:7 gate:2 down:1 18 split:8 up:2 19 20
    gate:3 21 split:9 up:3 down:2 split:10 22 tern:0 23 tern:1 split:11 gate:4 24 up:4 25 gate:5 down:3 26
    tern:2 27 28 down:4 tern:3 29 split:12 up:5 split:13 30 tern:4 tern:5 gate:6 up:6 +ln0a 31 gate:7 32 +ln0b
    down:5 up:7 33 tern:6 +tr0 tern:7 34 35 tern:8 down:6 +q0 +k0 +r0 tern:9 +v0:0 +m0 +v0:1 +l0 tern:10 +xe
    down:7 op0 tern:11
"""
STEADY_ORDER = """
    ln1a rt1 0 ln1b gate:0 1 up:0 tr1 2 3 rt2 gate:1 q1 k1 4 r1 down:0 5 6 v1 up:1 m1 7 gate:2 w1:0 w1:1 w1:2
    w1:3 l1 8 h1:0 up:2 9 h1:1 down:1 10 h1:2 gate:3 11 h1:3 12 up:3 13 14 down:2 gate:4 15 16 up:4 17 down:3
    w2:0 18 19 gate:5 +ln0a op0 20 21 up:5 +ln0b w2:1 22 23 +tr0 gate:6 down:4 24 +q0 +k0 25 +r0 up:6 +m0 26
    down:5 27 28 +l0 gate:7 29 up:7 +xe +v0:0 30 down:6 31 32 down:7 33 34 +v0:1 35 op1:0 op1:1
"""
LAST_ORDER = """
    ln1a rt1 0 rt2 gate:0 ln1b 1 up:0 tr1 2 3 gate:1 q1 k1 4 5 6 v1 up:1 r1 down:0 w1:0 m1 7 gate:2 w1:1 w1:2
    w1:3 l1 8 h1:0 up:2 9 h1:1 down:1 10 h1:2 gate:3 11 h1:3 12 up:3 13 14 down:2 gate:4 15 16 up:4 17 gate:5
    down:3 18 up:5 down:4 19 gate:6 up:6 20 down:5 gate:7 21 up:7 down:6 op0 22 down:7 23 +ln1a 24 25 w2:0 +ln1b
    +tr1 26 +q1 +k1 27 +r1 w2:1 28 29 30 +m1 +l1 31 32 +w1:0 33 +w1:1 34 +w1:2 35 +w1:3 op1:0 op1:1
"""
FINAL_ORDER = """
    fetch h1:0 h1:1 v1 0 h1:2 h1:3 1 2 w2:0 w2:1 3 qmax 4 5 6 7 quant:0 quant:1 8 quant:2 9 quant:3 10 quant:4
    11 quant:5 12 quant:6 13 quant:7 14 15 16 17 18 19 op1:0 op1:1
"""
BLOCK1 = {"ln1a", "ln1b", "tr1", "q1", "k1", "r1", "m1", "l1", "v1", "w1", "h1", "w2", "op1", "qmax", "quant", "fetch"}


def order_of(text, last):
    out = []
    for word in text.split():
        name, _, arg = word.lstrip("+").partition(":")
        if name.isdigit():
            out.append(int(name))
        else:
            out.append((name, int(arg or 0), int(word.startswith("+")) - int(name in BLOCK1)))
    return with_heads(out, last)


SPLIT = [("qk", 0), ("gu", 0), ("wd", 0), ("gu", 1), ("gu", 2), ("wd", 2), ("gu", 3), ("gu", 4), ("wd", 4), ("gu", 5),
         ("gu", 6), ("wd", 6), ("gu", 7), ("qk", 1)]


def uses(order):
    return sum(s[0] in BANKED for s in order)


ORDERS = {"first": order_of(FIRST_ORDER, 31), "steady": order_of(STEADY_ORDER, 31),
          "last": order_of(LAST_ORDER, 31), "final": order_of(FINAL_ORDER, 15)}
USES_STEADY = uses(ORDERS["steady"])
assert USES_STEADY % RING == 0
ROUNDS = USES_STEADY // RING
STEADY = B - 2
USES_BEFORE = {"first": 0, "steady": uses(ORDERS["first"]), "last": uses(ORDERS["first"]) + USES_STEADY * STEADY}
USES_BEFORE["final"] = USES_BEFORE["last"] + uses(ORDERS["last"])
PASS_OF = {"first": 0, "steady": 1, "last": B - 1, "final": B}
TERN_STEPS = 6
ACC_STEPS = E + 1


class Index:

    def __init__(self, reg, off):
        self.reg, self.off = reg, off

    def plus(self, d):
        return Index(self.reg, self.off + d)

    def at(self, per, extra=0):
        v = self.off * per + extra
        return v if self.reg is None else self.reg * per + v


class Stage:

    def __init__(self, kind, step, it):
        self.name, self.arg, d = step
        self.kind, self.it, self.n = kind, it, it.plus(d)
        self.bank = self.filled = self.before = self.place = None


def stages(kind, it, lag, users=None):
    if users is None:
        users = last_users(kind, it)
    out, place, after_down = [], 0, {}
    use = USES_BEFORE[kind]
    for step in ORDERS[kind]:
        st = Stage(kind, step, it)
        if st.name in BANKED:
            st.bank = use % RING
            st.filled = it.at(ROUNDS, use // RING + 1 - ROUNDS * PASS_OF[kind])
            st.before, users[st.bank] = users[st.bank], st
            use += 1
        if st.name == "up":
            st.place = after_down.get(st.arg - 2, 0)
        if st.name in ("down", "op0"):
            st.place = place
            place += 1
            if st.name == "down":
                after_down[st.arg] = place
        out.append(st)
    late = [i + lag.get(f"{st.name}:{st.arg}", lag.get(st.name, 0)) for i, st in enumerate(out)]
    return [out[i] for i in sorted(range(len(out)), key=lambda i: (late[i], i))]


def last_users(kind, it):
    users = [None] * RING
    if kind != "first":
        for st in stages("last" if kind == "final" else "steady", it.plus(-1), {}, [None] * RING):
            if st.bank is not None:
                users[st.bank] = st
    return users


def head_block(st):
    return {"first": 0, "final": 1}.get(st.kind, st.arg // H)


def set_block(st):
    return {"first": 0, "final": 1}.get(st.kind, st.arg // (H // G4))


def batch_of(st, block):
    return st.it if block == 0 else st.it.plus(-1)


def heads_before(st, extra=0):
    return st.it.at(2 * H, st.arg - H + extra)


def sets_before(st, extra=0):
    return st.it.at(2 * H // G4, st.arg - H // G4 + extra)


def at_before(st):
    return st.it.at(2 * NK, st.arg // 2 - NK)


def at_of_block(st, block):
    end = 2 * NK if (block == 1) != (st.kind in ("first", "final")) else NK
    return st.it.at(2 * NK, end - NK)


def ahead(n):
    return n.plus(1)


def wait(eng, sem, value):
    if not (isinstance(value, int) and value <= 0):
        eng.wait_ge(sem, value)


def settle(eng, passed):
    eng.sem_inc(passed, 1)


def run_passes(eng, do, before_block1, lag):
    for st in stages("first", Index(None, 0), lag):
        do(st)
    before_block1()
    with eng.Fori(0, STEADY) as j:
        for st in stages("steady", Index(j, 1), lag):
            do(st)
    for st in stages("last", Index(None, B - 1), lag):
        do(st)
    for st in stages("final", Index(None, B), lag):
        do(st)


def two_blocks(nc, x, wqk0, bqk0, wv0, vb0, wo0, ob0, slopes, wg, wu, wd, temp,
               wqk1, bqk1, wv1, vb1, wo1, ob1, w1t, b1c, w2t, b2, out):
    with ExitStack() as ctx:
        def sb(name, shape, dt=F32):
            return ctx.enter_context(nc.sbuf_tensor(name, shape, dt))

        def sem(name):
            return ctx.enter_context(nc.semaphore(name))

        score_ps = [ctx.enter_context(nc.psum_tensor(f"score_ps{i}", [P, 512], F32)) for i in range(2)]
        turn_ps = [ctx.enter_context(nc.psum_tensor(f"turn_ps{i}", [P, 512], F32)) for i in range(2)]
        value_ps = ctx.enter_context(nc.psum_tensor("value_ps", [P, 512], F32))
        gen_ps = [ctx.enter_context(nc.psum_tensor(f"gen_ps{i}", [P, 512], F32)) for i in range(RING)]

        gu_hi = sb("gu_hi", [P, E, 2, NK, F], F16)
        gu_lo = sb("gu_lo", [P, E, 2, NK, F], F16)
        wd_hi = sb("wd_hi", [P, E, NF, D], F16)
        wd_lo = sb("wd_lo", [P, E, NF, D], F16)
        qk_hi = [sb(f"qk_hi{l}", [P, NK, 2 * D], F16) for l in range(2)]
        qk_lo = [sb(f"qk_lo{l}", [P, NK, 2 * D], F16) for l in range(2)]
        wv_sb = [sb("wv0_sb", [P, NK, D + E]), sb("wv1_sb", [P, NK, D])]
        wo_sb = [sb(f"wo{l}_sb", [P, NK, D]) for l in range(2)]
        t1_sb = sb("t1_sb", [P, NK, HID], F16)
        t2_sb = sb("t2_sb", [P, NH, D], F16)
        bqk = [sb(f"bqk{l}", [P, 4]) for l in range(2)]
        vb = [sb(f"vb{l}_sb", [P, D]) for l in range(2)]
        ob = [sb(f"ob{l}_sb", [P, D]) for l in range(2)]
        b2_sb = sb("b2_sb", [P, D])
        b1_sb = sb("b1_sb", [P, NH])
        slope_sb = sb("slope_sb", [P, H])
        half_t = sb("half_t", [P, 1])
        minus_half = sb("minus_half", [P, NT])
        before = sb("before", [P, E, E])
        ident = sb("ident", [P, P])
        bias0 = sb("bias0", [P, H, S])
        bias1 = sb("bias1", [P, S])
        x0 = sb("x0", [P, NT, D])
        acc = sb("acc", [P, NT, D])
        xb = [sb(f"xb{l}", [P, NT, D]) for l in range(2)]
        stats = sb("stats", [P, NT, 6])
        mv = [sb(f"mv{l}", [P, NT, 2]) for l in range(2)]
        var = [sb(f"var{l}", [P, NT]) for l in range(2)]
        rstd = [sb(f"rstd{l}", [P, NT]) for l in range(2)]
        xt = sb("xt", [P, NK, S])
        xt_hi = sb("xt_hi", [P, NK, S], F16)
        xt_lo = sb("xt_lo", [P, NK, S], F16)
        xe_hi = sb("xe_hi", [P, NK, S], F16)
        xe_lo = sb("xe_lo", [P, NK, S], F16)
        rest = sb("rest", [P, 2, 2, S])
        parts = sb("parts", [P, 2, 3, 2, S], BF16)
        q_stack = [sb(f"q_stack{i}", [KR, H // 2, S], BF16) for i in range(2)]
        k_stack = [sb(f"k_stack{i}", [KR, H // 2, S], BF16) for i in range(2)]
        v_sb = [sb(f"v{l}_sb", [P, NT, H // G4, VB]) for l in range(2)]
        probs = sb("probs", [P, PROBS, 3 * P])
        nmax = sb("nmax", [P, PROBS, 2])
        esum = sb("esum", [P, PROBS, 2])
        rsum = sb("rsum", [P, PROBS, 2])
        pt = sb("pt", [P, 1 + 3 * TURNED, P])
        at = [sb(f"at{l}", [P, NK, S]) for l in range(2)]
        tanh_sb = sb("tanh_sb", [P, NF * S])
        gated = sb("gated", [P, NF * S])
        hid0 = sb("hid0", [P, 2, NF, S])
        h0_hi = sb("h0_hi", [P, 2, NF, S], F16)
        h0_lo = sb("h0_lo", [P, 2, NF, S], F16)
        hid1 = sb("hid1", [P, NH, S])
        h1_parts = sb("h1_parts", [P, 2, NH, S], F16)
        yx_sb = sb("yx_sb", [P, 2, NT, D])
        y_sb, x2_sb = yx_sb[:, 0], yx_sb[:, 1]
        r_tanh = sb("r_tanh", [P, NT, E])
        r_in = sb("r_in", [P, NT, E])
        r_zone = sb("r_zone", [P, NT, E])
        r_zone2 = sb("r_zone2", [P, NT, E])
        r_d = sb("r_d", [P, NT, E])
        r_dist = sb("r_dist", [P, NT, E])
        r_e1 = sb("r_e1", [P, NT, E])
        r_e2 = sb("r_e2", [P, NT, E])
        r_w = sb("r_w", [P, NT, E])
        r_fb = sb("r_fb", [P, NT, E])
        r_rank = sb("r_rank", [P, NT, E])
        r_gt = sb("r_gt", [P, NT, E, E])
        r_eq = sb("r_eq", [P, NT, E, E])
        r_s = sb("r_s", [P, 6, NT, 1])
        w8 = sb("w8", [P, NT, E])
        t_max = sb("t_max", [P, 2])
        t_amax = sb("t_amax", [P, 2])
        t_delta = sb("t_delta", [P, 2, 2])
        t_sum = sb("t_sum", [P, 2, 2])
        t_tot = sb("t_tot", [P, 2, 2])
        alpha = sb("alpha", [P, 2])
        ymax = sb("ymax", [P, B * NT])
        yred = sb("yred", [P, 4])

        raw = [v_sb[1][:].rearrange("p t b c -> p (t b c)")[:, 0:2 * NK * D], yx_sb[:].rearrange("p a t d -> p (a t d)")]
        w1_raw = hid1[:].rearrange("p a s -> p (a s)")
        w2_raw = h1_parts[:].rearrange("p i a s -> p (i a s)").bitcast(F32)
        y_all = gu_hi[:].rearrange("p e m k f -> p (e m k f)").bitcast(F32).rearrange("p (t d) -> p t d", d=D)
        x_all = gu_lo[:].rearrange("p e m k f -> p (e m k f)").bitcast(F32).rearrange("p (t d) -> p t d", d=D)
        rel_i = hid0[:, 0, 0, :].bitcast(I32)
        rel = hid0[:, 1, 0, :]

        scr = [[nc.dram_tensor(f"scr_{n}{l}", (SPLITS, C * H, S), BF16).ap() for n in "qk"] for l in range(2)]
        y_dram = nc.dram_tensor("y_dram", (B * NT, P, D), F32).ap()
        x2_dram = nc.dram_tensor("x2_dram", (B * NT, P, D), F32).ap()
        x_tiles = x.rearrange("b (t p) d -> p (b t) d", p=P)
        out_tiles = out.rearrange("b (t p) d -> p (b t) d", p=P)
        y_tiles = y_dram.rearrange("t p d -> p t d")
        x2_tiles = x2_dram.rearrange("t p d -> p t d")

        s_x = sem("s_x")
        s_c = sem("s_c")
        s_ob = sem("s_ob")
        s_wv0 = sem("s_wv0")
        s_wo = sem("s_wo")
        s_w1 = sem("s_w1")
        s_raw = [sem(f"s_raw{i}") for i in range(2)]
        s_scr = [sem(f"s_scr{l}") for l in range(2)]
        s_stack = [sem(f"s_stack{i}") for i in range(2)]
        s_yw = sem("s_yw")
        s_x2w = sem("s_x2w")
        s_fin = sem("s_fin")
        s_out = sem("s_out")
        s_pool = sem("s_pool")
        s_set = sem("s_set")
        s_hi = sem("s_hi")
        s_lo = sem("s_lo")
        s_t = sem("s_t")
        s_tp = sem("s_tp")
        s_v1z = sem("s_v1z")
        s_dve = sem("s_dve")
        s_gps = sem("s_gps")
        s_sp = sem("s_sp")
        full = [sem(f"full{i}") for i in range(RING)]
        s_st = [sem(f"s_st{l}") for l in range(2)]
        s_rstd = [sem(f"s_rstd{l}") for l in range(2)]
        s_xb = [sem(f"s_xb{l}") for l in range(2)]
        s_xn = [sem(f"s_xn{l}") for l in range(2)]
        s_xh = [sem(f"s_xh{l}") for l in range(2)]
        s_xl = [sem(f"s_xl{l}") for l in range(2)]
        s_ph = [sem(f"s_ph{l}") for l in range(2)]
        s_pr = [sem(f"s_pr{l}") for l in range(2)]
        s_pm = [sem(f"s_pm{l}") for l in range(2)]
        s_pl = [sem(f"s_pl{l}") for l in range(2)]
        s_v = [sem(f"s_v{l}") for l in range(2)]
        s_th = sem("s_th")
        s_rt = sem("s_rt")
        s_re = sem("s_re")
        s_w8 = sem("s_w8")
        s_xe = sem("s_xe")
        s_tg = sem("s_tg")
        s_ga = sem("s_ga")
        s_h0 = sem("s_h0")
        s_h0h = sem("s_h0h")
        s_h0l = sem("s_h0l")
        s_acc = sem("s_acc")
        s_h1 = sem("s_h1")
        s_h1h = sem("s_h1h")
        s_h1l = sem("s_h1l")
        s_y = sem("s_y")
        s_ym = sem("s_ym")
        s_x2 = sem("s_x2")
        s_sc = sem("s_sc")
        s_mx = sem("s_mx")
        s_ex = sem("s_ex")
        s_rz = sem("s_rz")
        s_nm = sem("s_nm")
        s_tn = sem("s_tn")
        s_ev = sem("s_ev")
        s_pv = sem("s_pv")
        s_at = sem("s_at")
        s_q = sem("s_q")
        s_qp = sem("s_qp")
        s_qa = sem("s_qa")
        s_qs = sem("s_qs")
        s_qo = sem("s_qo")

        RT = 25
        TERN = 10
        NC = 9
        POOL_IDENT, POOL_BEFORE, POOL_REL, POOL_PT = 2, 4, 7, 9
        SET_HALF, SET_BQ, SET_REL, SET_BIAS0 = 3, 5, 6, 6 + H

        def last_batch(n):
            return n.reg is None and n.off == B - 1

        def residual1(n):
            return xb[0] if last_batch(n) else xb[1]

        def split_parts(i):
            what, a = SPLIT[i]
            if what == "qk":
                return [w[a][:].rearrange("p k n -> p (k n)") for w in (qk_hi, qk_lo)]
            if what == "gu":
                return [w[:, a].rearrange("p m k f -> p (m k f)") for w in (gu_hi, gu_lo)]
            return [w[:, a:a + 2].rearrange("p e k d -> p (e k d)") for w in (wd_hi, wd_lo)]

        def read_by(st):
            n, a, l = st.n, st.arg, int(st.name[-1]) if st.name[-1] in "01" else None
            return {
                "tr": lambda: (s_xl[l], n.at(1, 1)),
                "q": lambda: (s_ph[l], n.at(6, 2)),
                "k": lambda: (s_ph[l], n.at(6, 5)),
                "v": lambda: (s_v[0], n.at(NT, a + 1)) if l == 0 else (s_v[1], ahead(n).at(NT, NT)),
                "gate": lambda: (s_ga, n.at(E, a + 1)),
                "up": lambda: (s_h0, n.at(E, a + 1)),
                "down": lambda: (s_acc, n.at(NT * ACC_STEPS, NT * st.place + NT)),
                "w1": lambda: (s_h1, n.at(NH, 2 * a + 2)),
                "w2": lambda: (s_y, ahead(n).at(NT, a + 1)),
                "op": lambda: (s_x2, ahead(n).at(NT, a + 1)) if l else (s_acc, n.at(NT * ACC_STEPS, NT * st.place + NT)),
            }[st.name if st.name in ("w1", "w2") else st.name.rstrip("01")]()

        block = ctx.enter_context(nc.Block())

        @block.sync
        def _(sp):
            def load_x(n):
                wait(sp, s_xl[0], n.at(1))
                if n.reg is not None:
                    settle(sp, s_sp)
                sp.dma_start(x0[:], x_tiles[:, bass.ds(n.at(NT), NT), :]).then_inc(s_x, 16)

            def load_raw(i):
                if i >= 2:
                    wait(sp, s_lo, i - 1)
                dst, (what, a) = raw[i % 2], SPLIT[i]
                if what == "qk":
                    sp.dma_start(dst.rearrange("p (k n) -> p k n", k=NK),
                                 (wqk0, wqk1)[a].rearrange("(k p) n -> p k n", p=P)).then_inc(s_raw[i % 2], 16)
                if what == "gu":
                    d = dst.rearrange("p (m k f) -> p m k f", m=2, k=NK)
                    for m, w in enumerate((wg, wu)):
                        sp.dma_start(d[:, m], w[a].rearrange("(k p) f -> p k f", p=P)).then_inc(s_raw[i % 2], 16)
                if what == "wd":
                    sp.dma_start(dst.rearrange("p (e k d) -> p e k d", e=2, k=NF),
                                 wd[a:a + 2].rearrange("e (k p) d -> p e k d", p=P)).then_inc(s_raw[i % 2], 16)

            def store_parts(l, n):
                wait(sp, s_pl[l], n.at(1, 1))
                flat = parts[:].rearrange("p a s m n -> p a s (m n)")
                for a, (lo, hi) in enumerate(((0, 3), (3, 5), (5, 6))):
                    sp.dma_start(scr[l][0][lo:hi].rearrange("s (p m) n -> p s (m n)", p=P),
                                 flat[:, 0, 0:hi - lo]).then_inc(s_scr[l], 16)
                    sp.dma_start(scr[l][1][lo:hi].rearrange("s (p m) n -> p s (m n)", p=P),
                                 flat[:, 1, a:a + 1].broadcast_to([P, hi - lo, 2 * S])).then_inc(s_scr[l], 16)

            def load_stack(l, n, it, u):
                wait(sp, s_scr[l], (n if l == 0 else ahead(n)).at(96, 96))
                if n.reg is not None:
                    settle(sp, s_sp)
                wait(sp, s_sc, it.at(2 * H, 8 * (u - 1) - H))
                half = slice(8 * (u % 2), 8 * (u % 2) + 8)
                for src, dst in zip(scr[l], (q_stack, k_stack)):
                    sp.dma_start(dst[u % 2][:], src.rearrange("s (c h) n -> (s c) h n", h=H)[:, half, :])\
                      .then_inc(s_stack[u % 2], 16)

            def do(st):
                n, name, it = st.n, st.name, st.it
                if name == "split" and st.arg + 2 < len(SPLIT):
                    load_raw(st.arg + 2)
                if name in ("l0", "l1"):
                    store_parts(int(name[1]), n)
                if name == "l1":
                    if last_batch(n):
                        for u in (0, 1):
                            load_stack(1, n, Index(None, B), u)
                    else:
                        for u in (2, 3):
                            load_stack(1, n, it, u)
                if name == "l0":
                    for u in (2, 3) if st.kind == "first" and n.off == 0 else (0, 1):
                        load_stack(0, n, n, u)
                if name == "fetch":
                    sp.wait_ge(s_acc, NT * ACC_STEPS * B)
                    sp.wait_ge(s_yw, 16 * B)
                    sp.wait_ge(s_x2w, 16 * B)
                    done = NT * (B - 1)
                    sp.dma_start(y_all[:, 0:done, :], y_tiles[:, 0:done, :]).then_inc(s_fin, 16)
                    sp.dma_start(x_all[:, 0:done, :], x2_tiles[:, 0:done, :]).then_inc(s_fin, 16)
                if name == "quant" and st.arg < B - 1:
                    t = NT * st.arg
                    sp.wait_ge(s_qo, st.arg + 1)
                    sp.dma_start(out_tiles[:, t:t + NT, :], y_all[:, t:t + NT, :]).then_inc(s_out, 16)
                if name == "w2" and st.arg == NT - 1 and st.kind != "final":
                    wait(sp, s_y, ahead(n).at(NT, NT))
                    if n.reg is not None:
                        settle(sp, s_sp)
                    sp.dma_start(y_tiles[:, bass.ds(n.at(NT), NT), :], y_sb).then_inc(s_yw, 16)
                if name == "op1" and st.arg == NT - 1:
                    wait(sp, s_x2, ahead(n).at(NT, NT))
                    if st.kind == "final":
                        sp.dma_start(out_tiles[:, NT * (B - 1):NT * B, :], x2_sb).then_inc(s_out, 16)
                        return
                    if n.reg is not None:
                        settle(sp, s_sp)
                    sp.dma_start(x2_tiles[:, bass.ds(n.at(NT), NT), :], x2_sb).then_inc(s_x2w, 16)

            load_x(Index(None, 0))
            load_raw(0)
            load_raw(1)
            for st in stages("first", Index(None, 0), {}):
                if st.name == "ln0a" and st.n.off == 1:
                    load_x(st.n)
                do(st)
            for counts, batch in ((s_yw, 16), (s_x2w, 16), (s_scr[1], 96)):
                sp.sem_inc(counts, batch)
            with sp.Fori(0, STEADY) as j:
                it = Index(j, 1)
                load_x(it.plus(1))
                for st in stages("steady", it, {}):
                    do(st)
            for st in stages("last", Index(None, B - 1), {}):
                do(st)
            for st in stages("final", Index(None, B), {}):
                do(st)
            sp.wait_ge(s_out, 16 * B)
            sp.wait_ge(s_yw, 16 * B)
            sp.wait_ge(s_x2w, 16 * B)
            sp.wait_ge(s_scr[0], 96 * B)
            sp.wait_ge(s_scr[1], 96 * (B + 1))

        @block.gpsimd
        def _(pool):
            pool.memset(ident[:], 0.0).then_inc(s_pool, 1)
            pool.wait_ge(s_pool, 1)
            pool.affine_select(out=ident[:], in_=ident[:], compare_op=ALU.not_equal, fill=1.0, base=0,
                               pattern=[[-1, P]], channel_multiplier=1).then_inc(s_pool, 1)
            pool.memset(before[:], 1.0).then_inc(s_pool, 1)
            pool.wait_ge(s_pool, 3)
            pool.affine_select(out=before[:], in_=before[:], compare_op=ALU.is_gt, fill=0.0, base=0,
                               pattern=[[1, E], [-1, E]], channel_multiplier=0).then_inc(s_pool, 1)
            pool.memset(bias1[:], 0.0).then_inc(s_pool, 1)
            pool.wait_ge(s_pool, 5)
            pool.affine_select(out=bias1[:, P:S], in_=bias1[:, P:S], compare_op=ALU.is_ge, fill=MASKED, base=0,
                               pattern=[[-1, P]], channel_multiplier=1).then_inc(s_pool, 1)
            pool.iota(rel_i, pattern=[[1, S]], base=-P, channel_multiplier=-1).then_inc(s_pool, 1)
            pool.memset(minus_half[:], -0.5).then_inc(s_pool, 1)
            pool.memset(pt[:, 0], CLAMP).then_inc(s_pool, 1)
            pool.wait_ge(s_pool, POOL_PT)

            def load_weights():
                for l, w in enumerate((wo0, wo1)):
                    for r in range(2):
                        for j in range(G4):
                            row = PAD * j + C * r
                            pool.dma_start(wo_sb[l][row:row + C, :, :],
                                           w.rearrange("(g r j c) d -> r j c g d", r=2, j=G4, c=C)[r, j]).then_inc(s_wo, 16)
                pool.dma_start(w1_raw.rearrange("p (k n) -> p k n", k=NK),
                               w1t.rearrange("(k p) n -> p k n", p=P)).then_inc(s_w1, 16)
                pool.dma_start(w2_raw.rearrange("p (a n) -> p a n", a=NH),
                               w2t.rearrange("(a p) n -> p a n", p=P)).then_inc(s_w1, 16)

            def do(st):
                n, name = st.n, st.name
                if name in ("ln0a", "ln1a"):
                    l = int(name[2])
                    src, total = (x0, xb[0]) if l == 0 else (acc, residual1(n))
                    if st.kind == "first":
                        pool.wait_ge(s_ob, 32)
                    if l == 0:
                        wait(pool, s_x, n.at(16, 16))
                        wait(pool, s_acc, n.at(NT * ACC_STEPS, NT - NT * ACC_STEPS))
                    else:
                        wait(pool, s_acc, n.at(NT * ACC_STEPS, NT * ACC_STEPS))
                        if not last_batch(n):
                            wait(pool, s_x2, ahead(n).at(NT))
                    for t in range(NT):
                        pool.tensor_tensor(total[:, t], src[:, t], ob[l][:], ALU.add).then_inc(s_xb[l], 1)
                    wait(pool, s_st[l], n.at(5, 5))
                    pool.tensor_tensor(rstd[l][:], var[l][:], minus_half[:], ALU.pow).then_inc(s_rstd[l], 1)
                    if st.kind == "first" and n.off == 0:
                        load_weights()
                if name == "xe":
                    wait(pool, s_xl[0], n.at(1, 1))
                    wait(pool, s_h0, n.at(E))
                    if st.kind == "steady":
                        settle(pool, s_gps)
                    pool.tensor_copy(xe_hi[:].bitcast(I32), xt_hi[:].bitcast(I32)).then_inc(s_xe, 1)
                    pool.tensor_copy(xe_lo[:].bitcast(I32), xt_lo[:].bitcast(I32)).then_inc(s_xe, 1)
                if name == "up":
                    e = st.arg % 2
                    wait(pool, s_h0h, n.at(E, st.arg + 1))
                    pool.tensor_tensor(h0_lo[:, e], hid0[:, e], h0_hi[:, e], ALU.subtract).then_inc(s_h0l, 1)
                if name == "h1":
                    a = 2 * st.arg
                    wait(pool, s_h1h, n.at(NH // 2, st.arg + 1))
                    pool.tensor_tensor(h1_parts[:, 1, a:a + 2], hid1[:, a:a + 2], h1_parts[:, 0, a:a + 2],
                                       ALU.subtract).then_inc(s_h1l, 1)
                if name == "quant":
                    c = st.arg
                    y = y_all[:, NT * c:NT * c + NT, :] if c < B - 1 else y_sb
                    x = x_all[:, NT * c:NT * c + NT, :] if c < B - 1 else residual1(n)[:]
                    pool.wait_ge(s_qs, c + 1)
                    if c == 0:
                        pool.wait_ge(s_fin, 32)
                    pool.tensor_tensor(y, y, x, ALU.add).then_inc(s_qo, 1)
                if name == "qmax":
                    pool.wait_ge(s_q, 1)
                    pool.partition_all_reduce(yred[:, 1:2], yred[:, 0:1], P, R_MAX).then_inc(s_qp, 1)
                if name == "tern":
                    i, step = st.arg // TERN_STEPS, st.arg % TERN_STEPS
                    if step == 0:
                        pool.wait_ge(s_t, TERN * i + 1)
                        pool.partition_all_reduce(t_amax[:, i:i + 1], t_max[:, i:i + 1], P, R_MAX).then_inc(s_tp, 1)
                    if step == 4:
                        pool.wait_ge(s_t, TERN * i + 7)
                        pool.partition_all_reduce(t_tot[:, i], t_sum[:, i], P, R_ADD).then_inc(s_tp, 1)
                    if i == 1 and step == 5:
                        pool.wait_ge(s_lo, len(SPLIT))
                        pool.wait_ge(s_hi, len(SPLIT))
                        pool.memset(v_sb[1][:], 0.0).then_inc(s_v1z, 1)

            run_passes(pool, do, lambda: pool.sem_inc(s_h1l, NH // 2), {})

        @block.scalar
        def _(act):
            for l, bias in enumerate((ob0, ob1)):
                act.dma_start(ob[l][:], bias.partition_broadcast(P)).then_inc(s_ob, 16)
            small = [(bqk[0][:], bqk0), (half_t[:], temp.partition_broadcast(P)), (vb[0][:], vb0.partition_broadcast(P)),
                     (slope_sb[:], slopes.partition_broadcast(P)), (bqk[1][:], bqk1), (vb[1][:], vb1.partition_broadcast(P)),
                     (b1_sb[:], b1c), (b2_sb[:], b2.partition_broadcast(P)),
                     (wv_sb[1][:], wv1.rearrange("(k p) n -> p k n", p=P))]
            act.dma_start(wv_sb[0][:], wv0.rearrange("(k p) n -> p k n", p=P)).then_inc(s_wv0, 16)
            for dst, src in small:
                act.dma_start(dst, src).then_inc(s_c, 16)
            assert NC == len(small)

            def do(st):
                n, name, b = st.n, st.name, st.bank
                g = gen_ps[b] if b is not None else None
                if name == "split":
                    i = st.arg
                    act.wait_ge(s_raw[i % 2], 16 * sum(2 if what == "gu" else 1 for what, _ in SPLIT[i % 2:i + 1:2]))
                    act.activation(split_parts(i)[0], raw[i % 2], ACT.Copy, scale=WSCALE).then_inc(s_hi, 1)
                if name in ("tr0", "tr1"):
                    l = int(name[2])
                    wait(act, full[b], st.filled)
                    wait(act, s_xe, n.at(2) if l == 0 else n.at(2, 2 if last_batch(n) else 4))
                    act.activation(xt[:].rearrange("p k s -> p (k s)"), g[:, :], ACT.Copy).then_inc(s_xh[l], 1)
                    act.activation(xt_hi[:].rearrange("p k s -> p (k s)"), g[:, :], ACT.Copy).then_inc(s_xh[l], 1)
                if name in ("q0", "k0", "q1", "k1"):
                    l, a = int(name[1]), "qk".index(name[0])
                    if n.reg is None and n.off == 0 and l == 0 and a == 0:
                        act.wait_ge(s_set, SET_BQ)
                    if a == 0:
                        if l == 0:
                            wait(act, s_scr[0], n.at(96))
                            wait(act, s_scr[1], n.at(96) if n.reg is not None or n.off > 1 else 0)
                        else:
                            wait(act, s_scr[1], ahead(n).at(96))
                            wait(act, s_scr[0], 96 * B if last_batch(n) else n.at(96, 192))
                    wait(act, full[b], st.filled)
                    scale = (float(C) ** -0.5 if a == 0 else 1.0) / WSCALE
                    for m in range(2):
                        act.activation(rest[:, a, m], g[:, S * m:S * m + S], ACT.Identity, scale=scale,
                                       bias=bqk[l][:, 2 * a + m:2 * a + m + 1]).then_inc(s_ph[l], 1)
                    wait(act, s_ph[l], n.at(6, 3 * a + 2))
                    act.activation(parts[:, a, 0], rest[:, a], ACT.Copy).then_inc(s_ph[l], 1)
                if name in ("m0", "m1"):
                    l = int(name[1])
                    wait(act, s_pr[l], n.at(1, 1))
                    act.activation(parts[:, :, 1], rest[:], ACT.Copy).then_inc(s_pm[l], 1)
                if name == "v0":
                    t = st.arg
                    if t == 0 and n.reg is None and n.off == 0:
                        act.wait_ge(s_set, SET_HALF)
                    wait(act, full[b], st.filled)
                    if t == 0:
                        wait(act, s_rt, n.at(RT))
                    act.activation(r_tanh[:, t], g[:, D:D + E], ACT.Tanh, scale=half_t[:, 0:1]).then_inc(s_th, 1)
                if name == "rt2":
                    wait(act, s_rt, n.at(RT, 5))
                    act.activation(r_e1[:], r_dist[:], ACT.Exp, scale=-1.0 / 0.1).then_inc(s_re, 1)
                    act.activation(r_e2[:], r_dist[:], ACT.Exp, scale=-1.0 / 0.3).then_inc(s_re, 1)
                if name == "gate":
                    wait(act, full[b], st.filled)
                    wait(act, s_ga, n.at(E, st.arg))
                    act.activation(tanh_sb[:], g[:, :], ACT.Tanh, scale=0.5 / WSCALE).then_inc(s_tg, 1)
                if name == "up":
                    wait(act, s_h0, n.at(E, st.arg + 1))
                    wait(act, s_acc, n.at(NT * ACC_STEPS, NT * st.place))
                    act.activation(h0_hi[:, st.arg % 2], hid0[:, st.arg % 2], ACT.Copy).then_inc(s_h0h, 1)
                if name == "w1":
                    if st.arg == 0:
                        wait(act, s_h1l, ahead(n).at(NH // 2))
                    wait(act, full[b], st.filled)
                    for j in range(2):
                        a = 2 * st.arg + j
                        act.activation(hid1[:, a], g[:, S * j:S * j + S], ACT.Gelu,
                                       bias=b1_sb[:, a:a + 1], scale=alpha[:, 0:1]).then_inc(s_h1, 1)
                if name == "h1":
                    a = 2 * st.arg
                    if a == 0:
                        wait(act, s_y, ahead(n).at(NT))
                    wait(act, s_h1, n.at(NH, a + 2))
                    act.activation(h1_parts[:, 0, a:a + 2], hid1[:, a:a + 2], ACT.Copy).then_inc(s_h1h, 1)
                if name == "score":
                    s = st.arg
                    k = s % PROBS
                    wait(act, s_mx, heads_before(st, 1))
                    for lo, hi, j in ((0, S, 0), (S, S + P, 1)):
                        last = act.activation(probs[:, k, lo:hi], probs[:, k, lo:hi], ACT.Exp, scale=-1.0,
                                              bias=nmax[:, k, j:j + 1], accum_out=esum[:, k, j:j + 1])
                    last.then_inc(s_ex, 1)
                if name == "turn":
                    s = st.arg
                    wait(act, s_tn, heads_before(st, 1))
                    wait(act, s_pv, st.it.at(2 * H // G4, s // G4 - H // G4 - 1))
                    slot = 1 + 3 * (s % TURNED)
                    act.activation(pt[:, slot:slot + 3].rearrange("p t q -> p (t q)"), turn_ps[s % 2][:, 0:3 * P],
                                   ACT.Copy).then_inc(s_ev, 1)
                if name == "value" and st.arg % 2 == 1:
                    l = set_block(st)
                    g = st.arg // 2 % NK
                    wait(act, s_pv, sets_before(st, 1))
                    if g == 0:
                        nb = batch_of(st, l)
                        wait(act, *((s_acc, nb.at(NT * ACC_STEPS)) if l == 0 else (s_x2, ahead(nb).at(NT))))
                    act.activation(at[l][:, g], value_ps[:, 0:S], ACT.Copy).then_inc(s_at, 1)

                if name == "quant":
                    if st.arg == 0:
                        act.wait_ge(s_q, 3)
                        act.wait_ge(s_fin, 32)
                    y = y_all[:, NT * st.arg:NT * st.arg + NT, :] if st.arg < B - 1 else y_sb
                    act.activation(y, y, ACT.Copy, scale=yred[:, 3:4], bias=ROUND).then_inc(s_qa, 1)

            def before_block1():
                act.wait_ge(s_t, 2 * TERN)
                act.wait_ge(s_v1z, 1)

            run_passes(act, do, before_block1, LAG["scalar"])

        @block.tensor
        def _(pe):
            def take(st):
                if st.before is not None:
                    wait(pe, *read_by(st.before))
                return gen_ps[st.bank]

            def do(st):
                n, name = st.n, st.name
                first = n.reg is None and n.off == 0
                if name in ("tr0", "tr1"):
                    l = int(name[2])
                    src = (x0, acc)[l]
                    if first and l == 0:
                        pe.wait_ge(s_pool, POOL_IDENT)
                    wait(pe, s_xn[l], n.at(NT, NT))
                    g = take(st)
                    for t in range(NT):
                        for k in range(NK):
                            last = pe.transpose(g[:, S * k + P * t:S * k + P * t + P], src[:, t, P * k:P * k + P], ident[:])
                    last.then_inc(full[st.bank], 1)
                if name in ("q0", "k0", "q1", "k1"):
                    l, a = int(name[1]), "qk".index(name[0])
                    if first and l == 0 and a == 0:
                        pe.wait_ge(s_lo, 1)
                    wait(pe, s_xl[l], n.at(1, 1))
                    g = take(st)
                    for m in range(2):
                        cols = slice(D * a + P * m, D * a + P * m + P)
                        terms = [(w, xx, k) for w, xx in ((qk_hi, xt_hi), (qk_hi, xt_lo), (qk_lo, xt_hi)) for k in range(NK)]
                        for i, (w, xx, k) in enumerate(terms):
                            last = pe.matmul(g[:, S * m:S * m + S], w[l][:, k, cols], xx[:, k, :],
                                             start=(i == 0), stop=(i == len(terms) - 1))
                    last.then_inc(full[st.bank], 1)
                if name in ("v0", "v1"):
                    l = int(name[1])
                    if first and l == 0 and st.arg == 0:
                        pe.wait_ge(s_wv0, 16)
                    wait(pe, s_xl[l], n.at(1, 1))
                    g = take(st)
                    for t in ([st.arg] if l == 0 else range(NT)):
                        o = g[:, 0:D + E] if l == 0 else g[:, D * t:D * t + D]
                        for k in range(NK):
                            last = pe.matmul(o, xt[:, k, P * t:P * t + P], wv_sb[l][:, k, :],
                                             start=(k == 0), stop=(k == NK - 1))
                    last.then_inc(full[st.bank], 1)
                if name in ("gate", "up"):
                    m = ("gate", "up").index(name)
                    if st.arg == 0 and m == 0:
                        wait(pe, s_xe, n.at(2, 2))
                    if first and m == 0:
                        pe.wait_ge(s_lo, 1 + SPLIT.index(("gu", st.arg)))
                    g = take(st)
                    for f in range(NF):
                        cols = slice(P * f, P * f + P)
                        terms = [(w, xx, k) for w, xx in ((gu_hi, xe_hi), (gu_hi, xe_lo), (gu_lo, xe_hi)) for k in range(NK)]
                        for i, (w, xx, k) in enumerate(terms):
                            last = pe.matmul(g[:, S * f:S * f + S], w[:, st.arg, m, k, cols], xx[:, k, :],
                                             start=(i == 0), stop=(i == len(terms) - 1))
                    last.then_inc(full[st.bank], 1)
                if name == "down":
                    if first:
                        pe.wait_ge(s_lo, 1 + SPLIT.index(("wd", st.arg // 2 * 2)))
                    wait(pe, s_h0l, n.at(E, st.arg + 1))
                    g = take(st)
                    for t in range(NT):
                        terms = [(h, w, f) for h, w in ((h0_hi, wd_hi), (h0_lo, wd_hi), (h0_hi, wd_lo)) for f in range(NF)]
                        for i, (h, w, f) in enumerate(terms):
                            last = pe.matmul(g[:, D * t:D * t + D], h[:, st.arg % 2, f, P * t:P * t + P],
                                             w[:, st.arg, f, :], start=(i == 0), stop=(i == len(terms) - 1))
                    last.then_inc(full[st.bank], 1)
                if name == "w1":
                    if st.arg == 0:
                        wait(pe, s_xl[1], n.at(1, 1))
                    g = take(st)
                    for j in range(2):
                        a = 2 * st.arg + j
                        terms = [(xx, k) for xx in (xt_hi, xt_lo) for k in range(NK)]
                        for i, (xx, k) in enumerate(terms):
                            last = pe.matmul(g[:, S * j:S * j + S], t1_sb[:, k, P * a:P * a + P], xx[:, k, :],
                                             start=(i == 0), stop=(i == len(terms) - 1))
                    last.then_inc(full[st.bank], 1)
                if name == "w2":
                    if st.arg == 0:
                        wait(pe, s_h1l, ahead(n).at(NH // 2, NH // 2))
                    g = take(st)
                    terms = [(i, a) for i in range(2) for a in range(NH)]
                    for i, a in terms:
                        last = pe.matmul(g[:, 0:D], h1_parts[:, i, a, P * st.arg:P * st.arg + P], t2_sb[:, a, :],
                                         start=((i, a) == terms[0]), stop=((i, a) == terms[-1]))
                    last.then_inc(full[st.bank], 1)
                if name in ("op0", "op1"):
                    l = int(name[2])
                    if first and l == 0:
                        pe.wait_ge(s_wo, 16 * 4 * G4)
                    wait(pe, s_at, at_of_block(st, l))
                    g = take(st)
                    for t in (range(NT) if l == 0 else [st.arg]):
                        o = g[:, D * t:D * t + D] if l == 0 else g[:, 0:D]
                        for q in range(NK):
                            last = pe.matmul(o, at[l][:, q, P * t:P * t + P], wo_sb[l][:, q, :],
                                             start=(q == 0), stop=(q == NK - 1))
                    last.then_inc(full[st.bank], 1)
                if name == "score":
                    s = st.arg
                    u, hh = s // 8, s % 8
                    if hh == 0:
                        wait(pe, s_stack[u % 2], st.it.at(64, 32 * (u // 2)))
                    wait(pe, s_mx, heads_before(st, -1))
                    g, q, k = score_ps[s % 2], q_stack[u % 2], k_stack[u % 2]
                    pe.matmul(g[:, 0:S], q[:, hh, P:S], k[:, hh, :], start=True, stop=True)
                    pe.matmul(g[:, S:S + P], q[:, hh, 0:P], k[:, hh, 0:P], start=True, stop=True).then_inc(s_sc, 1)
                if name == "turn":
                    s = st.arg
                    wait(pe, s_nm, heads_before(st, 1))
                    wait(pe, s_ev, heads_before(st, -1))
                    g, p = turn_ps[s % 2], probs[:, s % PROBS]
                    pe.transpose(g[:, 0:P], p[:, P:S], ident[:])
                    pe.transpose(g[:, P:2 * P], p[:, S:S + P], ident[:])
                    pe.transpose(g[:, 2 * P:3 * P], p[:, 0:P], ident[:]).then_inc(s_tn, 1)
                if name == "value":
                    l = set_block(st)
                    nb = batch_of(st, l)
                    b, r = st.arg % G4, st.arg % 2
                    if b == 0:
                        wait(pe, s_v[l], (nb if l == 0 else ahead(nb)).at(NT, NT))
                        if st.kind == "first":
                            pe.wait_ge(s_pool, POOL_PT)
                    wait(pe, s_ev, st.it.at(2 * H, G4 * (st.arg + 1) - H))
                    if r == 0:
                        wait(pe, s_at, at_before(st))
                    for t in range(NT):
                        for j in range(G4):
                            slot = 1 + 3 * ((G4 * st.arg + j) % TURNED)
                            first_col = VB * b + PAD * j - C * r
                            v = v_sb[l][:, t].rearrange("p b c -> p (b c)")[:, first_col:first_col + PAD]
                            lo, seen = (0, pt[:, slot + 1:slot + 3]) if t == 0 else \
                                (0, pt[:, 0:slot + 1:slot]) if l == 0 else (P, pt[:, slot])
                            last = pe.matmul(value_ps[PAD * j:PAD * j + PAD, lo:S], v, seen,
                                             start=(t == 0 and r == 0), stop=(t == 1 and r == 1))
                    last.then_inc(s_pv, 1)

            def before_block1():
                pe.wait_ge(s_lo, len(SPLIT))
                pe.wait_ge(s_t, 2 * TERN)
                pe.wait_ge(s_c, 16 * NC)
                pe.wait_ge(s_acc, NT * ACC_STEPS)
                pe.wait_ge(s_v[0], 2 * NT)

            run_passes(pe, do, before_block1, {})

        @block.vector
        def _(dve):
            def do(st):
                n, name, b = st.n, st.name, st.bank
                g = gen_ps[b] if b is not None else None
                if name == "setup" and st.arg == 0:
                    dve.memset(v_sb[0][:], 0.0).then_inc(s_set, 1)
                if name == "setup" and st.arg == 2:
                    dve.wait_ge(s_c, 16 * NC)
                    dve.reciprocal(half_t[:], half_t[:]).then_inc(s_set, 1)
                    dve.wait_ge(s_set, 2)
                    dve.tensor_scalar(half_t[:], half_t[:], 0.5, None, ALU.mult).then_inc(s_set, 1)
                    dve.tensor_scalar(bqk[0][:, 0:2], bqk[0][:, 0:2], float(C) ** -0.5, None, ALU.mult)\
                       .then_inc(s_set, 1)
                    dve.tensor_scalar(bqk[1][:, 0:2], bqk[1][:, 0:2], float(C) ** -0.5, None, ALU.mult)\
                       .then_inc(s_set, 1)
                if name == "setup" and st.arg == 1:
                    dve.wait_ge(s_pool, POOL_REL)
                    dve.tensor_copy(rel, rel_i).then_inc(s_set, 1)
                    dve.wait_ge(s_set, SET_REL)
                    for h in range(H):
                        dve.scalar_tensor_tensor(bias0[:, h], rel, slope_sb[:, h:h + 1], bias1[:], ALU.mult, ALU.add)\
                           .then_inc(s_set, 1)
                if name == "split":
                    i = st.arg
                    dve.wait_ge(s_hi, i + 1)
                    hi, lo = split_parts(i)
                    dve.scalar_tensor_tensor(lo, raw[i % 2], WSCALE, hi, ALU.mult, ALU.subtract).then_inc(s_lo, 1)
                if name == "tern":
                    i, step = st.arg // TERN_STEPS, st.arg % TERN_STEPS
                    t0 = TERN * i
                    w = (w1_raw, w2_raw)[i]
                    t = (t1_sb[:].rearrange("p k n -> p (k n)"), t2_sb[:].rearrange("p a d -> p (a d)"))[i]
                    if step == 0:
                        dve.wait_ge(s_w1, 32)
                        dve.tensor_reduce(t_max[:, i:i + 1], w, AX.X, ALU.max, apply_absolute_value=True).then_inc(s_t, 1)
                    if step == 1:
                        dve.wait_ge(s_tp, 2 * i + 1)
                        dve.tensor_scalar(t_delta[:, i, 0:1], t_amax[:, i:i + 1], 0.05, None, ALU.mult).then_inc(s_t, 1)
                        dve.tensor_scalar(t_delta[:, i, 1:2], t_amax[:, i:i + 1], -0.05, None, ALU.mult).then_inc(s_t, 1)
                        dve.wait_ge(s_t, t0 + 3)
                        dve.tensor_scalar(t, w, t_delta[:, i, 1:2], None, ALU.is_lt).then_inc(s_t, 1)
                    if step == 2:
                        dve.wait_ge(s_t, t0 + 4)
                        dve.scalar_tensor_tensor(t, w, t_delta[:, i, 0:1], t, ALU.is_gt, ALU.subtract).then_inc(s_t, 1)
                    if step == 3:
                        dve.wait_ge(s_t, t0 + 5)
                        dve.tensor_tensor_reduce(out=w, in0=w, in1=t, scale=1.0, scalar=0.0, op0=ALU.mult, op1=ALU.add,
                                                 accum_out=t_sum[:, i, 0:1]).then_inc(s_t, 1)
                    if step == 4:
                        dve.wait_ge(s_t, t0 + 6)
                        dve.tensor_tensor_reduce(out=w, in0=t, in1=t, scale=1.0, scalar=0.0, op0=ALU.mult, op1=ALU.add,
                                                 accum_out=t_sum[:, i, 1:2]).then_inc(s_t, 1)
                    if step == 5:
                        dve.wait_ge(s_tp, 2 * i + 2)
                        dve.tensor_scalar(t_tot[:, i, 1:2], t_tot[:, i, 1:2], 1.0, None, ALU.max).then_inc(s_t, 1)
                        dve.wait_ge(s_t, t0 + 8)
                        dve.reciprocal(t_tot[:, i, 1:2], t_tot[:, i, 1:2]).then_inc(s_t, 1)
                        dve.wait_ge(s_t, t0 + 9)
                        dve.tensor_tensor(alpha[:, i:i + 1], t_tot[:, i, 0:1], t_tot[:, i, 1:2], ALU.mult).then_inc(s_t, 1)
                if name in ("ln0a", "ln1a"):
                    l = int(name[2])
                    if l == 0:
                        wait(dve, s_x, n.at(16, 16))
                    else:
                        wait(dve, s_acc, n.at(NT * ACC_STEPS, NT * ACC_STEPS))
                    src = (x0, acc)[l]
                    for t in range(NT):
                        dve.bn_stats(stats[:, t], src[:, t]).then_inc(s_st[l], 1)
                    wait(dve, s_st[l], n.at(5, 2))
                    if st.kind == "steady":
                        settle(dve, s_dve)
                    for t in range(NT):
                        dve.bn_aggr(mv[l][:, t], stats[:, t]).then_inc(s_st[l], 1)
                    wait(dve, s_st[l], n.at(5, 4))
                    dve.tensor_scalar(var[l][:], mv[l][:, :, 1], EPS, None, ALU.add).then_inc(s_st[l], 1)
                if name in ("ln0b", "ln1b"):
                    l = int(name[2])
                    src = (x0, acc)[l]
                    wait(dve, s_rstd[l], n.at(1, 1))
                    wait(dve, s_xb[l], n.at(NT, NT))
                    for t in range(NT):
                        dve.tensor_scalar(src[:, t], src[:, t], mv[l][:, t, 0:1], rstd[l][:, t:t + 1],
                                          ALU.subtract, ALU.mult).then_inc(s_xn[l], 1)
                if name in ("tr0", "tr1"):
                    l = int(name[2])
                    wait(dve, s_xh[l], n.at(2, 2))
                    dve.tensor_tensor(xt_lo[:].rearrange("p k s -> p (k s)"), g[:, :],
                                      xt_hi[:].rearrange("p k s -> p (k s)"), ALU.subtract).then_inc(s_xl[l], 1)
                if name in ("r0", "r1"):
                    l = int(name[1])
                    wait(dve, s_ph[l], n.at(6, 6))
                    dve.tensor_tensor(rest[:], rest[:], parts[:, :, 0], ALU.subtract).then_inc(s_pr[l], 1)
                if name in ("l0", "l1"):
                    l = int(name[1])
                    wait(dve, s_pm[l], n.at(1, 1))
                    dve.tensor_tensor(parts[:, :, 2], rest[:], parts[:, :, 1], ALU.subtract).then_inc(s_pl[l], 1)
                if name in ("v0", "v1"):
                    l = int(name[1])
                    for t in ([st.arg] if l == 0 else range(NT)):
                        if l == 0:
                            wait(dve, s_th, n.at(NT, t + 1))
                        elif t == 0:
                            wait(dve, full[b], st.filled)
                        if t == 0:
                            if l == 0:
                                wait(dve, s_pv, n.at(8, -8) if n.reg is not None or n.off > 1 else 4 * n.off)
                            else:
                                wait(dve, s_pv, n.at(8, 4))
                        o = g[:, 0:D] if l == 0 else g[:, D * t:D * t + D]
                        four = dict(j=G4, c=C)
                        dve.tensor_tensor(v_sb[l][:, t, :, 0:P].rearrange("p b (j x) -> p b j x", x=PAD)[:, :, :, 0:C],
                                          o.rearrange("p (b j c) -> p b j c", **four),
                                          vb[l][:].rearrange("p (b j c) -> p b j c", **four), ALU.add).then_inc(s_v[l], 1)
                if name == "rt1":
                    def zone(ins):
                        ins.then_inc(s_rt, 1)
                    wait(dve, s_th, n.at(NT, NT))
                    zone(dve.tensor_scalar(r_in[:], r_tanh[:], 0.5, 0.5, ALU.mult, ALU.add))
                    wait(dve, s_rt, n.at(RT, 1))
                    zone(dve.tensor_scalar(r_zone[:], r_in[:], float(GOLD_LO), None, ALU.is_ge))
                    zone(dve.tensor_scalar(r_d[:], r_in[:], float(GOLD_C), None, ALU.subtract))
                    wait(dve, s_rt, n.at(RT, 3))
                    zone(dve.scalar_tensor_tensor(r_zone2[:], r_in[:], GOLD_HI, r_zone[:], ALU.is_le, ALU.mult))
                    wait(dve, s_re, n.at(2))
                    zone(dve.scalar_tensor_tensor(r_dist[:], r_d[:], -1.0, r_d[:], ALU.mult, ALU.max))
                if name == "rt2":
                    per_token = [P, NT, E]
                    pairs = [P, NT, E, E]

                    def route(k, ins):
                        ins.then_inc(s_rt, 1)

                    def after(k):
                        wait(dve, s_rt, n.at(RT, 5 + k))
                    if st.kind == "first":
                        dve.wait_ge(s_pool, POOL_BEFORE)
                    wait(dve, s_re, n.at(2, 2))
                    route(1, dve.tensor_tensor(r_gt[:], r_e2[:].unsqueeze(2).broadcast_to(pairs),
                                               r_e2[:].unsqueeze(3).broadcast_to(pairs), ALU.is_gt))
                    route(2, dve.tensor_tensor(r_eq[:], r_e2[:].unsqueeze(2).broadcast_to(pairs),
                                               r_e2[:].unsqueeze(3).broadcast_to(pairs), ALU.is_equal))
                    route(3, dve.tensor_tensor(r_w[:], r_e1[:], r_zone2[:], ALU.mult))
                    after(2)
                    route(4, dve.tensor_tensor(r_eq[:], r_eq[:], before[:].unsqueeze(1).broadcast_to(pairs), ALU.mult))
                    after(3)
                    route(5, dve.tensor_reduce(r_s[:, 0], r_w[:], AX.X, ALU.add))
                    after(4)
                    route(6, dve.tensor_tensor(r_gt[:], r_gt[:], r_eq[:], ALU.add))
                    after(5)
                    route(7, dve.tensor_scalar(r_s[:, 1], r_s[:, 0], 1e-8, None, ALU.is_lt))
                    after(6)
                    route(8, dve.tensor_reduce(r_rank[:].unsqueeze(3), r_gt[:], AX.X, ALU.add))
                    after(7)
                    route(9, dve.tensor_scalar(r_s[:, 2], r_s[:, 1], -1.0, 1.0, ALU.mult, ALU.add))
                    after(8)
                    route(10, dve.scalar_tensor_tensor(r_fb[:], r_rank[:], 2.0, r_e2[:], ALU.is_lt, ALU.mult))
                    after(10)
                    route(11, dve.tensor_reduce(r_s[:, 3], r_fb[:], AX.X, ALU.add))
                    route(12, dve.tensor_tensor(r_w[:], r_w[:], r_s[:, 2].broadcast_to(per_token), ALU.mult))
                    after(11)
                    route(13, dve.tensor_scalar(r_s[:, 3], r_s[:, 3], 1e-8, None, ALU.max))
                    after(13)
                    route(14, dve.reciprocal(r_s[:, 4], r_s[:, 3]))
                    after(14)
                    route(15, dve.tensor_tensor(r_fb[:], r_fb[:], r_s[:, 4].broadcast_to(per_token), ALU.mult))
                    after(15)
                    route(16, dve.tensor_tensor(r_fb[:], r_fb[:], r_s[:, 1].broadcast_to(per_token), ALU.mult))
                    after(16)
                    route(17, dve.tensor_tensor(r_w[:], r_w[:], r_fb[:], ALU.add))
                    after(17)
                    route(18, dve.tensor_reduce(r_s[:, 5], r_w[:], AX.X, ALU.add))
                    after(18)
                    route(19, dve.tensor_scalar(r_s[:, 5], r_s[:, 5], 1e-8, None, ALU.max))
                    after(19)
                    route(20, dve.reciprocal(r_s[:, 0], r_s[:, 5]))
                    after(20)
                    dve.scalar_tensor_tensor(w8[:], r_w[:], 1.0 / WSCALE, r_s[:, 0].broadcast_to(per_token),
                                             ALU.mult, ALU.mult).then_inc(s_w8, 1)
                if name == "gate":
                    wait(dve, s_tg, n.at(E, st.arg + 1))
                    dve.scalar_tensor_tensor(gated[:], tanh_sb[:], 1.0, g[:, :], ALU.add, ALU.mult).then_inc(s_ga, 1)
                if name == "up":
                    wait(dve, full[b], st.filled)
                    wait(dve, s_ga, n.at(E, st.arg + 1))
                    wait(dve, s_h0l, n.at(E, st.arg - 1))
                    dve.scalar_tensor_tensor(hid0[:, st.arg % 2].rearrange("p f s -> p (f s)"), gated[:],
                                             0.5 / (WSCALE * WSCALE), g[:, :], ALU.mult, ALU.mult).then_inc(s_h0, 1)
                if name == "down":
                    e = st.arg
                    wait(dve, full[b], st.filled)
                    if st.place == 0:
                        wait(dve, s_w8, n.at(1, 1))
                        wait(dve, s_xb[0], n.at(NT, NT))
                    wait(dve, s_acc, n.at(NT * ACC_STEPS, NT * st.place))
                    for t in range(NT):
                        dve.scalar_tensor_tensor(acc[:, t], g[:, D * t:D * t + D], w8[:, t, e:e + 1],
                                                 (xb[0] if st.place == 0 else acc)[:, t], ALU.mult, ALU.add)\
                           .then_inc(s_acc, 1)
                if name == "op0":
                    wait(dve, full[b], st.filled)
                    wait(dve, s_acc, n.at(NT * ACC_STEPS, NT * st.place))
                    for t in range(NT):
                        dve.tensor_tensor(acc[:, t], g[:, D * t:D * t + D], acc[:, t], ALU.add).then_inc(s_acc, 1)
                if name == "w2":
                    t = st.arg
                    wait(dve, full[b], st.filled)
                    if t == 0:
                        wait(dve, s_yw, ahead(n).at(16))
                    dve.scalar_tensor_tensor(y_sb[:, t], g[:, 0:D], alpha[:, 1:2], b2_sb[:], ALU.mult, ALU.add)\
                       .then_inc(s_y, 1)
                    wait(dve, s_y, ahead(n).at(NT, t + 1))
                    dve.tensor_reduce(ymax[:, bass.ds(n.at(NT, t), 1)], y_sb[:, t], AX.X, ALU.max,
                                      apply_absolute_value=True).then_inc(s_ym, 1)
                if name == "op1":
                    t = st.arg
                    wait(dve, full[b], st.filled)
                    if t == 0:
                        wait(dve, s_xb[1], n.at(NT, NT))
                        wait(dve, s_x2w, ahead(n).at(16))
                    if st.kind == "final":
                        dve.wait_ge(s_qo, B)
                    rest_of_sum = y_sb if st.kind == "final" else residual1(n)
                    dve.tensor_tensor(x2_sb[:, t], g[:, 0:D], rest_of_sum[:, t], ALU.add).then_inc(s_x2, 1)
                if name == "score":
                    s, l = st.arg, head_block(st)
                    k, g = s % PROBS, score_ps[s % 2]
                    wait(dve, s_sc, heads_before(st, 1))
                    if st.kind == "steady":
                        settle(dve, s_dve)
                    if st.kind == "first":
                        dve.wait_ge(s_set, SET_BIAS0)
                    bias = bias0[:, s % H] if l == 0 else bias1[:]
                    for lo, hi, blo, j in ((0, S, 0, 0), (S, S + P, P, 1)):
                        last = dve.tensor_tensor_reduce(out=probs[:, k, lo:hi], in0=g[:, lo:hi], in1=bias[:, blo:S],
                                                        scale=-1.0, scalar=BIG, op0=ALU.add, op1=ALU.min,
                                                        accum_out=nmax[:, k, j:j + 1])
                    last.then_inc(s_mx, 1)
                if name == "norm":
                    s, l = st.arg, head_block(st)
                    k = s % PROBS
                    wait(dve, s_ex, heads_before(st, 1))
                    dve.reciprocal(rsum[:, k], esum[:, k]).then_inc(s_rz, 1)
                    wait(dve, s_rz, heads_before(st, 1))
                    for lo, hi, j in ((0, S, 0), (S, S + P, 1)):
                        clamp = (CLAMP, ALU.mult, ALU.max) if l == 0 else (None, ALU.mult)
                        last = dve.tensor_scalar(probs[:, k, lo:hi], probs[:, k, lo:hi], rsum[:, k, j:j + 1], *clamp)
                    last.then_inc(s_nm, 1)

                if name == "qmax":
                    dve.wait_ge(s_ym, B * NT)
                    dve.tensor_reduce(yred[:, 0:1], ymax[:], AX.X, ALU.max).then_inc(s_q, 1)
                    dve.wait_ge(s_qp, 1)
                    dve.tensor_scalar(yred[:, 2:3], yred[:, 1:2], 1.0 / QMAX, 1e-8, ALU.mult, ALU.add).then_inc(s_q, 1)
                    dve.wait_ge(s_q, 2)
                    dve.reciprocal(yred[:, 3:4], yred[:, 2:3]).then_inc(s_q, 1)
                if name == "quant":
                    c = st.arg
                    y = y_all[:, NT * c:NT * c + NT, :] if c < B - 1 else y_sb
                    dve.wait_ge(s_qa, c + 1)
                    dve.tensor_scalar(y, y, ROUND + QMAX, ROUND - QMAX, ALU.min, ALU.max).then_inc(s_q, 1)
                    dve.wait_ge(s_q, 4 + c)
                    dve.tensor_scalar(y, y, ROUND, yred[:, 2:3], ALU.subtract, ALU.mult).then_inc(s_qs, 1)

            def before_block1():
                dve.wait_ge(s_v1z, 1)
                for counts in (s_v[1], s_y, s_x2):
                    dve.sem_inc(counts, NT)

            run_passes(dve, do, before_block1, LAG["vector"])


def kernel(L0_attn_qkv, L0_attn_in_proj, L0_attn_in_proj_bias, L0_attn_out_w, L0_attn_out_b, L0_attn_alibi_slopes,
           L0_ffn_Wg, L0_ffn_Wu, L0_ffn_Wd, L0_ffn_Wr, L0_ffn_temperature, L1_attn_Wq, L1_attn_bq, L1_attn_Wk,
           L1_attn_bk, L1_attn_Wv, L1_attn_bv, L1_attn_Wo, L1_attn_bo, L1_ffn_W1, L1_ffn_b1, L1_ffn_W2, L1_ffn_b2):
    import concourse.bacc as bacc
    from concourse.bass_utils import run_bass_kernel_spmd

    def by_channel(w):
        w = w.reshape(-1, H, C).transpose(0, 2, 1)
        return w.reshape(-1, P, 2).transpose(0, 2, 1).reshape(-1, H * C)

    def columns(q, k):
        return np.concatenate([by_channel(q.reshape(1, -1)), by_channel(k.reshape(1, -1))], 1).reshape(4, P).T

    proj, pb = np.asarray(L0_attn_in_proj), np.asarray(L0_attn_in_proj_bias)
    a = {k: np.asarray(v) for k, v in locals().items() if k.startswith("L")}
    heads = {k: a["L1_attn_W" + k].transpose(1, 0, 2).reshape(D, D) for k in "qkv"}
    arrays = {
        "x": a["L0_attn_qkv"],
        "wqk0": np.concatenate([by_channel(proj[0:D].T), by_channel(proj[D:2 * D].T)], 1),
        "bqk0": columns(pb[0:D], pb[D:2 * D]),
        "wv0": np.concatenate([proj[2 * D:].T, a["L0_ffn_Wr"]], 1),
        "vb0": pb[2 * D:],
        "wo0": a["L0_attn_out_w"].T,
        "ob0": a["L0_attn_out_b"],
        "slopes": a["L0_attn_alibi_slopes"],
        "wg": a["L0_ffn_Wg"],
        "wu": a["L0_ffn_Wu"],
        "wd": a["L0_ffn_Wd"],
        "temp": a["L0_ffn_temperature"],
        "wqk1": np.concatenate([by_channel(heads["q"]), by_channel(heads["k"])], 1),
        "bqk1": columns(a["L1_attn_bq"], a["L1_attn_bk"]),
        "wv1": heads["v"],
        "vb1": a["L1_attn_bv"].reshape(-1),
        "wo1": a["L1_attn_Wo"],
        "ob1": a["L1_attn_bo"],
        "w1t": a["L1_ffn_W1"].T,
        "b1c": a["L1_ffn_b1"].reshape(NH, P).T,
        "w2t": a["L1_ffn_W2"].T,
        "b2": a["L1_ffn_b2"],
    }
    arrays = {k: np.ascontiguousarray(v) for k, v in arrays.items()}
    nc = bacc.Bacc("TRN2", target_bir_lowering=False, num_devices=1)
    args = [nc.dram_tensor("in_" + k, v.shape, mybir.dt.from_np(v.dtype), kind="ExternalInput").ap() for k, v in arrays.items()]
    out = nc.dram_tensor("out_dram", (B, S, D), F32, kind="ExternalOutput").ap()
    two_blocks(nc, *args, out)
    r = run_bass_kernel_spmd(nc, [{"in_" + k: v for k, v in arrays.items()}], core_ids=[0])
    return r.results[0]["out_dram"]
```
